# Optimizing a Trainium2 kernel written in Bass

```python
import numpy as np
import jax
import jax.numpy as jnp

def _softmax(x, axis=-1):
    return jax.nn.softmax(x, axis=axis)

def _gelu(x):
    return jax.nn.gelu(x, approximate=True)

def _silu(x):
    return jax.nn.silu(x)

def _sigmoid(x):
    return jax.nn.sigmoid(x)

def _layernorm(x, axis=-1, eps=1e-05):
    m = jnp.mean(x, axis=axis, keepdims=True)
    v = jnp.var(x, axis=axis, keepdims=True)
    return (x - m) / jnp.sqrt(v + eps)

def _scatter_add(tgt, idx, src, axis=0):
    return tgt.at[idx].add(src)

def _segment_sum(src, seg, n):
    return jax.ops.segment_sum(src, seg, n)
kernel_name = 'mk_decoder_postln_d1_seqx_r8_bd7661'

def setup_inputs(seed: int=0):
    np.random.seed(seed)
    _w = jnp.asarray

    def _rec_inputs():
        import jax
        import jax.numpy as jnp
        _rk = jax.random.key(seed)
        x = 7.22e-05 + 1 * jax.random.normal(jax.random.fold_in(_rk, 1), (4, 256, 256), jnp.float32)
        _lenS = 256 - jax.random.randint(jax.random.fold_in(_rk, 7), (4,), 0, max(1, 256 // 4) + 1, jnp.int32)
        _lenS2 = 256 - jax.random.randint(jax.random.fold_in(_rk, 8), (4,), 0, max(1, 256 // 4) + 1, jnp.int32)
        _ctx_1024P = jax.random.normal(jax.random.fold_in(_rk, 11), (4, 16, 128), jnp.float32)
        _ctx_1024c = jax.random.dirichlet(jax.random.fold_in(_rk, 511), 0.3 * jnp.ones((16,), jnp.float32), (4, 256))
        _ctx_1024t = jnp.einsum('bsk,bkd->bsd', _ctx_1024c, _ctx_1024P)
        _ctx_1024t = _ctx_1024t * jax.lax.rsqrt(jnp.mean(jnp.square(_ctx_1024t)) + 1e-12) * 0.953939
        ctx_1024 = 2.81802e-05 + 1.00001 * (_ctx_1024t + 0.3 * jax.random.normal(jax.random.fold_in(_rk, 611), (4, 256, 128), jnp.float32))
        return (x, ctx_1024)
    x, ctx_1024 = _rec_inputs()

    def _L0_attn_setup():
        import math
        import jax, jax.numpy as jnp
        import numpy as np
        N_HEADS = 32
        N_KV_HEADS = 8
        ROPE_THETA = 10000.0
        LAYER_IDX = 12
        LAMBDA_INIT = 0.8 - 0.6 * math.exp(-0.3 * LAYER_IDX)

        def _rotate_half(x):
            x1, x2 = jnp.split(x, 2, axis=-1)
            return jnp.concatenate([-x2, x1], axis=-1)

        def _rope_tables(seq_len, head_dim, dtype):
            inv_freq = 1.0 / ROPE_THETA ** (jnp.arange(0, head_dim, 2, dtype=jnp.float32) / head_dim)
            freqs = jnp.arange(seq_len, dtype=jnp.float32)[:, None] * inv_freq[None, :]
            emb = jnp.concatenate([freqs, freqs], axis=-1)
            return (jnp.cos(emb).astype(dtype), jnp.sin(emb).astype(dtype))

        def _apply_rope(x, cos, sin):
            return x * cos[None, None] + _rotate_half(x) * sin[None, None]
        key = jax.random.key(seed)
        ks = jax.random.split(key, 9)
        B, S, H = (2, 128, 256)
        hd = H // N_HEADS
        return {'hidden_states': jax.random.normal(ks[0], (B, S, H), jnp.float32), 'wq': jax.random.normal(ks[1], (2 * H, H), jnp.float32) * 0.02, 'wk': jax.random.normal(ks[2], (2 * N_KV_HEADS * hd, H), jnp.float32) * 0.02, 'wv': jax.random.normal(ks[3], (N_KV_HEADS * hd, H), jnp.float32) * 0.02, 'wo': jax.random.normal(ks[4], (H, H), jnp.float32) * 0.02, 'lambda_q1': jax.random.normal(ks[5], (hd,), jnp.float32) * 0.1, 'lambda_k1': jax.random.normal(ks[6], (hd,), jnp.float32) * 0.1, 'lambda_q2': jax.random.normal(ks[7], (hd,), jnp.float32) * 0.1, 'lambda_k2': jax.random.normal(ks[8], (hd,), jnp.float32) * 0.1}
    _L0_attn_all = _L0_attn_setup()
    _L0_attn_in = {k: v for k, v in _L0_attn_all.items() if k in ('wq', 'wk', 'wv', 'wo', 'lambda_q1', 'lambda_k1', 'lambda_q2', 'lambda_k2')}
    del _L0_attn_all

    def _L0_xattn_setup():
        import jax, jax.numpy as jnp
        import numpy as np
        key = jax.random.key(seed)
        ks = jax.random.split(key, 6)
        B, L, N, C, D = (8, 64, 256, 128, 128)
        return {'teacher_logits': jax.random.normal(ks[0], (B, L, N), dtype=jnp.float32), 'teacher_features': jax.random.normal(ks[1], (B, N, C), dtype=jnp.float32), 'Wq': jax.random.normal(ks[2], (D, C), dtype=jnp.float32) * (1.0 / np.sqrt(C)), 'bq': jnp.zeros((D,), dtype=jnp.float32), 'Wk': jax.random.normal(ks[3], (D, C), dtype=jnp.float32) * (1.0 / np.sqrt(C)), 'bk': jnp.zeros((D,), dtype=jnp.float32)}
    _L0_xattn_all = _L0_xattn_setup()
    _L0_xattn_in = {k: v for k, v in _L0_xattn_all.items() if k in ('Wq', 'bq', 'Wk', 'bk')}
    del _L0_xattn_all

    def _L0_ffn_setup():
        import jax, jax.numpy as jnp
        import numpy as np
        B, S, D = (2, 256, 256)
        H, KV, HD = (16, 4, 128)
        E, F, TOPK = (8, 512, 2)
        THETA = 1000000.0
        EPS = 1e-05

        def rmsnorm(x, w):
            var = jnp.mean(jnp.square(x), axis=-1, keepdims=True)
            return x * jax.lax.rsqrt(var + EPS) * w

        def rope_cos_sin(seq_len):
            inv_freq = 1.0 / THETA ** (jnp.arange(0, HD, 2, dtype=jnp.float32) / HD)
            ang = jnp.arange(seq_len, dtype=jnp.float32)[:, None] * inv_freq[None, :]
            return (jnp.cos(ang)[None, :, None, :], jnp.sin(ang)[None, :, None, :])

        def apply_rope(x, cos, sin):
            x1, x2 = jnp.split(x, 2, axis=-1)
            return jnp.concatenate([x1 * cos - x2 * sin, x2 * cos + x1 * sin], axis=-1)

        def attention(x, wq, wk, wv, wo):
            b, s, _ = x.shape
            q = (x @ wq).reshape(b, s, H, HD)
            k = (x @ wk).reshape(b, s, KV, HD)
            v = (x @ wv).reshape(b, s, KV, HD)
            cos, sin = rope_cos_sin(s)
            q = apply_rope(q, cos, sin)
            k = apply_rope(k, cos, sin)
            rep = H // KV
            k = jnp.repeat(k, rep, axis=2)
            v = jnp.repeat(v, rep, axis=2)
            scores = jnp.einsum('bqhd,bkhd->bhqk', q, k) / np.sqrt(HD)
            causal = jnp.tril(jnp.ones((s, s), dtype=bool))
            scores = jnp.where(causal[None, None], scores, jnp.finfo(scores.dtype).min)
            probs = jax.nn.softmax(scores, axis=-1)
            out = jnp.einsum('bhqk,bkhd->bqhd', probs, v).reshape(b, s, H * HD)
            return out @ wo

        def moe(x, gate_w, w1, w3, w2):
            b, s, d = x.shape
            xt = x.reshape(b * s, d)
            logits = xt @ gate_w
            topv, topi = jax.lax.top_k(logits, TOPK)
            probs = jax.nn.softmax(topv, axis=-1)
            w = jnp.zeros_like(logits)
            for kk in range(TOPK):
                w = w + jax.nn.one_hot(topi[:, kk], E, dtype=logits.dtype) * probs[:, kk:kk + 1]
            out = jnp.zeros_like(xt)
            for e in range(E):
                h = jax.nn.silu(xt @ w1[e]) * (xt @ w3[e])
                out = out + w[:, e:e + 1] * (h @ w2[e])
            return out.reshape(b, s, d)
        key = jax.random.key(seed)
        ks = jax.random.split(key, 10)
        init = lambda k, shape: jax.random.normal(k, shape, jnp.float32) * 0.02
        return {'hidden_states': jax.random.normal(ks[0], (B, S, D), jnp.float32), 'norm1_w': jnp.ones((D,), jnp.float32), 'norm2_w': jnp.ones((D,), jnp.float32), 'wq': init(ks[1], (D, H * HD)), 'wk': init(ks[2], (D, KV * HD)), 'wv': init(ks[3], (D, KV * HD)), 'wo': init(ks[4], (H * HD, D)), 'gate_w': init(ks[5], (D, E)), 'w1': init(ks[6], (E, D, F)), 'w3': init(ks[7], (E, D, F)), 'w2': init(ks[8], (E, F, D))}
    _L0_ffn_all = _L0_ffn_setup()
    _L0_ffn_in = {k: v for k, v in _L0_ffn_all.items() if k in ('norm1_w', 'norm2_w', 'wq', 'wk', 'wv', 'wo', 'gate_w', 'w1', 'w3', 'w2')}
    del _L0_ffn_all
    return {'x': x, 'ctx_1024': ctx_1024, 'L0_attn_wq': _L0_attn_in['wq'], 'L0_attn_wk': _L0_attn_in['wk'], 'L0_attn_wv': _L0_attn_in['wv'], 'L0_attn_wo': _L0_attn_in['wo'], 'L0_attn_lambda_q1': _L0_attn_in['lambda_q1'], 'L0_attn_lambda_k1': _L0_attn_in['lambda_k1'], 'L0_attn_lambda_q2': _L0_attn_in['lambda_q2'], 'L0_attn_lambda_k2': _L0_attn_in['lambda_k2'], 'L0_xattn_Wq': _L0_xattn_in['Wq'], 'L0_xattn_bq': _L0_xattn_in['bq'], 'L0_xattn_Wk': _L0_xattn_in['Wk'], 'L0_xattn_bk': _L0_xattn_in['bk'], 'L0_ffn_norm1_w': _L0_ffn_in['norm1_w'], 'L0_ffn_norm2_w': _L0_ffn_in['norm2_w'], 'L0_ffn_wq': _L0_ffn_in['wq'], 'L0_ffn_wk': _L0_ffn_in['wk'], 'L0_ffn_wv': _L0_ffn_in['wv'], 'L0_ffn_wo': _L0_ffn_in['wo'], 'L0_ffn_gate_w': _L0_ffn_in['gate_w'], 'L0_ffn_w1': _L0_ffn_in['w1'], 'L0_ffn_w3': _L0_ffn_in['w3'], 'L0_ffn_w2': _L0_ffn_in['w2']}

def reference(x, ctx_1024, L0_attn_wq, L0_attn_wk, L0_attn_wv, L0_attn_wo, L0_attn_lambda_q1, L0_attn_lambda_k1, L0_attn_lambda_q2, L0_attn_lambda_k2, L0_xattn_Wq, L0_xattn_bq, L0_xattn_Wk, L0_xattn_bk, L0_ffn_norm1_w, L0_ffn_norm2_w, L0_ffn_wq, L0_ffn_wk, L0_ffn_wv, L0_ffn_wo, L0_ffn_gate_w, L0_ffn_w1, L0_ffn_w3, L0_ffn_w2):
    import jax
    import jax.numpy as jnp

    def _L0_attn_ref(hidden_states, wq, wk, wv, wo, lambda_q1, lambda_k1, lambda_q2, lambda_k2):
        import math
        import jax, jax.numpy as jnp
        import numpy as np
        N_HEADS = 32
        N_KV_HEADS = 8
        ROPE_THETA = 10000.0
        LAYER_IDX = 12
        LAMBDA_INIT = 0.8 - 0.6 * math.exp(-0.3 * LAYER_IDX)

        def _rotate_half(x):
            x1, x2 = jnp.split(x, 2, axis=-1)
            return jnp.concatenate([-x2, x1], axis=-1)

        def _rope_tables(seq_len, head_dim, dtype):
            inv_freq = 1.0 / ROPE_THETA ** (jnp.arange(0, head_dim, 2, dtype=jnp.float32) / head_dim)
            freqs = jnp.arange(seq_len, dtype=jnp.float32)[:, None] * inv_freq[None, :]
            emb = jnp.concatenate([freqs, freqs], axis=-1)
            return (jnp.cos(emb).astype(dtype), jnp.sin(emb).astype(dtype))

        def _apply_rope(x, cos, sin):
            return x * cos[None, None] + _rotate_half(x) * sin[None, None]
        B, S, H = hidden_states.shape
        hd = H // N_HEADS
        n_rep = N_HEADS // N_KV_HEADS
        qp = hidden_states @ wq.T
        kp = hidden_states @ wk.T
        v = hidden_states @ wv.T
        q1, q2 = jnp.split(qp, 2, axis=-1)
        k1, k2 = jnp.split(kp, 2, axis=-1)

        def to_heads(x):
            return x.reshape(B, S, -1, hd).transpose(0, 2, 1, 3)
        q1, q2 = (to_heads(q1), to_heads(q2))
        k1, k2 = (to_heads(k1), to_heads(k2))
        v = to_heads(v)
        cos, sin = _rope_tables(S, hd, hidden_states.dtype)
        q1, k1 = (_apply_rope(q1, cos, sin), _apply_rope(k1, cos, sin))
        q2, k2 = (_apply_rope(q2, cos, sin), _apply_rope(k2, cos, sin))
        k1 = jnp.repeat(k1, n_rep, axis=1)
        k2 = jnp.repeat(k2, n_rep, axis=1)
        v = jnp.repeat(v, n_rep, axis=1)
        scale = 1.0 / math.sqrt(hd)
        causal = jnp.where(jnp.tril(jnp.ones((S, S), dtype=bool)), 0.0, -1e+30).astype(jnp.float32)
        s1 = jnp.einsum('bhqd,bhkd->bhqk', q1, k1) * scale + causal
        s2 = jnp.einsum('bhqd,bhkd->bhqk', q2, k2) * scale + causal
        a1 = jax.nn.softmax(s1.astype(jnp.float32), axis=-1).astype(q1.dtype)
        a2 = jax.nn.softmax(s2.astype(jnp.float32), axis=-1).astype(q1.dtype)
        lam1 = jnp.exp(jnp.sum(lambda_q1 * lambda_k1))
        lam2 = jnp.exp(jnp.sum(lambda_q2 * lambda_k2))
        lam_full = lam1 - lam2 + LAMBDA_INIT
        aw = a1 - lam_full * a2
        attn = jnp.einsum('bhqk,bhkd->bhqd', aw, v) * (1.0 - LAMBDA_INIT)
        attn = attn.transpose(0, 2, 1, 3).reshape(B, S, H)
        return attn @ wo.T

    def _L0_xattn_ref(teacher_logits, teacher_features, Wq, bq, Wk, bk):
        import jax, jax.numpy as jnp
        import numpy as np
        query = jnp.einsum('bnc,dc->bnd', teacher_features, Wq) + bq
        key = jnp.einsum('bnc,dc->bnd', teacher_features, Wk) + bk
        energy = jnp.einsum('bnd,bmd->bnm', query, key)
        attention = jax.nn.softmax(energy, axis=-1)
        x_m = jnp.einsum('bln,bmn->blm', teacher_logits, attention)
        return x_m

    def _L0_ffn_ref(hidden_states, norm1_w, norm2_w, wq, wk, wv, wo, gate_w, w1, w3, w2):
        import jax, jax.numpy as jnp
        import numpy as np
        B, S, D = (2, 256, 256)
        H, KV, HD = (16, 4, 128)
        E, F, TOPK = (8, 512, 2)
        THETA = 1000000.0
        EPS = 1e-05

        def rmsnorm(x, w):
            var = jnp.mean(jnp.square(x), axis=-1, keepdims=True)
            return x * jax.lax.rsqrt(var + EPS) * w

        def rope_cos_sin(seq_len):
            inv_freq = 1.0 / THETA ** (jnp.arange(0, HD, 2, dtype=jnp.float32) / HD)
            ang = jnp.arange(seq_len, dtype=jnp.float32)[:, None] * inv_freq[None, :]
            return (jnp.cos(ang)[None, :, None, :], jnp.sin(ang)[None, :, None, :])

        def apply_rope(x, cos, sin):
            x1, x2 = jnp.split(x, 2, axis=-1)
            return jnp.concatenate([x1 * cos - x2 * sin, x2 * cos + x1 * sin], axis=-1)

        def attention(x, wq, wk, wv, wo):
            b, s, _ = x.shape
            q = (x @ wq).reshape(b, s, H, HD)
            k = (x @ wk).reshape(b, s, KV, HD)
            v = (x @ wv).reshape(b, s, KV, HD)
            cos, sin = rope_cos_sin(s)
            q = apply_rope(q, cos, sin)
            k = apply_rope(k, cos, sin)
            rep = H // KV
            k = jnp.repeat(k, rep, axis=2)
            v = jnp.repeat(v, rep, axis=2)
            scores = jnp.einsum('bqhd,bkhd->bhqk', q, k) / np.sqrt(HD)
            causal = jnp.tril(jnp.ones((s, s), dtype=bool))
            scores = jnp.where(causal[None, None], scores, jnp.finfo(scores.dtype).min)
            probs = jax.nn.softmax(scores, axis=-1)
            out = jnp.einsum('bhqk,bkhd->bqhd', probs, v).reshape(b, s, H * HD)
            return out @ wo

        def moe(x, gate_w, w1, w3, w2):
            b, s, d = x.shape
            xt = x.reshape(b * s, d)
            logits = xt @ gate_w
            topv, topi = jax.lax.top_k(logits, TOPK)
            probs = jax.nn.softmax(topv, axis=-1)
            w = jnp.zeros_like(logits)
            for kk in range(TOPK):
                w = w + jax.nn.one_hot(topi[:, kk], E, dtype=logits.dtype) * probs[:, kk:kk + 1]
            out = jnp.zeros_like(xt)
            for e in range(E):
                h = jax.nn.silu(xt @ w1[e]) * (xt @ w3[e])
                out = out + w[:, e:e + 1] * (h @ w2[e])
            return out.reshape(b, s, d)
        attn_out = attention(rmsnorm(hidden_states, norm1_w), wq, wk, wv, wo)
        h = hidden_states + attn_out
        out = h + moe(rmsnorm(h, norm2_w), gate_w, w1, w3, w2)
        return out
    x = _layernorm(x + _L0_attn_ref(x, L0_attn_wq, L0_attn_wk, L0_attn_wv, L0_attn_wo, L0_attn_lambda_q1, L0_attn_lambda_k1, L0_attn_lambda_q2, L0_attn_lambda_k2), axis=-1)
    x = _layernorm(x + _L0_xattn_ref(x, ctx_1024, L0_xattn_Wq, L0_xattn_bq, L0_xattn_Wk, L0_xattn_bk), axis=-1)
    x = _layernorm(x + _L0_ffn_ref(x, L0_ffn_norm1_w, L0_ffn_norm2_w, L0_ffn_wq, L0_ffn_wk, L0_ffn_wv, L0_ffn_wo, L0_ffn_gate_w, L0_ffn_w1, L0_ffn_w3, L0_ffn_w2), axis=-1)
    return x

_drawn_inputs = setup_inputs


def setup_inputs(seed=0):
    import zlib

    import numpy as np

    out = dict(_drawn_inputs(seed))
    spreads = {'L0_xattn_bq': (0.0, 0.1),
     'L0_xattn_bk': (0.0, 0.8),
     'L0_ffn_norm1_w': (1.0, 0.6),
     'L0_ffn_norm2_w': (1.0, 0.6)}
    factors = {'L0_attn_wq': 8.0,
     'L0_attn_wk': 8.0,
     'L0_attn_wv': 8.0,
     'L0_attn_wo': 8.0,
     'L0_attn_lambda_q1': 8.0,
     'L0_attn_lambda_k1': 8.0,
     'L0_attn_lambda_q2': 8.0,
     'L0_attn_lambda_k2': 8.0,
     'L0_ffn_wq': 8.0,
     'L0_ffn_wk': 8.0,
     'L0_ffn_gate_w': 6.465,
     'L0_ffn_w1': 5.765,
     'L0_ffn_w3': 5.682,
     'L0_ffn_w2': 5.691}
    for name, (base, spread) in spreads.items():
        noise = np.random.default_rng([zlib.crc32(name.encode()), seed]).standard_normal(out[name].shape)
        drawn = base * np.exp(spread * noise) if base else spread * noise
        out[name] = jnp.asarray(drawn.astype(out[name].dtype))
    for name, factor in factors.items():
        out[name] = (out[name] * factor).astype(out[name].dtype)
    return out
```

```python
from contextlib import ExitStack
import math

import numpy as np

import concourse.bass as bass
from concourse import mybir

P = 128
B, T, D = 4, 256, 256
TT, DT = T // P, D // P
H1, G1, HD1 = 32, 8, 8
REP1 = H1 // G1
SLOT = 64
C2 = 128
H3, G3, HD3 = 16, 4, 128
REP3 = H3 // G3
E, F = 8, 512
FT = F // P
NTOK = B * T
NT = NTOK // P
LAMBDA_INIT = 0.8 - 0.6 * math.exp(-0.3 * 12)
EPS = 1e-5
NEG = -1e30

ALU = mybir.AluOpType
ACT = mybir.ActivationFunctionType
AX = mybir.AxisListType
F32 = mybir.dt.float32
BF16 = mybir.dt.bfloat16
U32 = mybir.dt.uint32

S_USES, O_USES, G_USES = 68, 24, 38


class Ring:

    def __init__(self, filled, emptied, uses):
        self.filled, self.emptied, self.half = filled, emptied, uses // 2

    def wait_empty(self, eng, b, u):
        eng.wait_ge(self.emptied[u % 2], b * self.half + u // 2 + 1)

    def wait_filled(self, eng, b, u):
        eng.wait_ge(self.filled[u % 2], b * self.half + u // 2 + 1)

    def wait_emptied(self, eng, b, u):
        eng.wait_ge(self.emptied[u % 2], b * self.half + u // 2 + 2)


S_PROJ, S_KT, S_QT, S_MAX, S_QT2, S_EXP, S_FFN = 0, 2, 4, 8, 32, 36, 60
G_QK2, G_EN, G_OT, G_AT, G_WO, G_A2T, G_X1T, G_XM, G_N1T = 0, 1, 2, 10, 11, 12, 13, 14, 15
G_V3, G_P3, G_PV3, G_WO3, G_N2T = 16, 18, 28, 36, 37
O_PV, O_PT = 0, 8


def decoder_kernel(nc, x, xT, ctxT, w1qkv, w1o, lam, w2q, w2k, b2, nw, w3q, w3k, w3v, w3o, gate,
                   e1, e3, e2, rope1, rope3, out, dbg=None):
    ctx = ExitStack()
    with ctx:
        def sb(name, shape, dt=F32):
            return ctx.enter_context(nc.sbuf_tensor(name, shape, dt))

        def sem(name):
            return ctx.enter_context(nc.semaphore(name))

        psS = ctx.enter_context(nc.psum_tensor("psS", [P, 2, 1024], F32))
        psO = ctx.enter_context(nc.psum_tensor("psO", [P, 2, 512], F32))
        psG = ctx.enter_context(nc.psum_tensor("psG", [P, 2, 512], F32))

        ident = sb("ident", [P, P])
        identb = sb("identb", [P, P], BF16)
        maskb = sb("maskb", [P, P], BF16)
        maskTb = sb("maskTb", [P, P], BF16)
        neghalf = sb("neghalf", [P, TT])
        iota8 = sb("iota8", [P, E])
        wqkv1 = sb("wqkv1", [P, DT, 704])
        wo1 = sb("wo1", [P, DT, D])
        rope1s = sb("rope1s", [P, TT, 2, HD1])
        rope3s = sb("rope3s", [P, 2, T])
        lams = sb("lams", [P, 4, HD1])
        lamp = sb("lamp", [P, 2, HD1])
        lamd = sb("lamd", [P, 2])
        lame = sb("lame", [P, 2])
        fac = sb("fac", [P, 2, 2])
        wq2 = sb("wq2", [P, C2])
        wk2 = sb("wk2", [P, C2])
        b2s = sb("b2s", [P, 2])
        nws = sb("nws", [P, 2, DT])
        w3 = sb("w3", [P, DT, (H3 + 2 * G3) * HD3])
        wq3, wk3, wv3 = w3[:, :, 0:2048], w3[:, :, 2048:2560], w3[:, :, 2560:3072]
        wo3 = sb("wo3", [P, H3, D])
        gates = sb("gates", [P, DT, E])

        xTs = sb("xTs", [P, DT, T])
        xs = sb("xs", [P, TT, D])
        cTs = sb("cTs", [P, T])
        rt = sb("rt", [P, 2560])
        rt1 = rt[:, 0:1280].rearrange("p (t n) -> p t n", t=2)
        rt2 = rt[:, 1280:2560].rearrange("p (t n) -> p t n", t=2)
        hib = sb("hib", [P, 2, 640], BF16)
        midb = sb("midb", [P, 2, 640], BF16)
        lob = sb("lob", [P, 2, 640], BF16)
        qpack = sb("qpack", [P, TT, 2 * H1, SLOT], BF16)
        kpack = sb("kpack", [P, TT, 2 * G1, 2, SLOT], BF16)
        QT = sb("QT", [P, H1, T], BF16)
        KT = sb("KT", [P, 2 * G1, 2, T], BF16)
        Vx = sb("Vx", [P, TT, G1, 32])
        negm = sb("negm", [P, TT, 2 * H1])
        mres = sb("mres", [P, TT, 2 * H1])
        ptq = sb("ptq", [P, 6144])
        PT = ptq[:, :].rearrange("p (i c n) -> p i c n", i=2, c=3)
        OT = sb("OT", [P, 2, 512])
        rs1 = sb("rs1", [P, 2, 4, 4])
        on1 = sb("on1", [P, 2, 4, 4, HD1])
        att1 = sb("att1", [P, TT, D])
        tT = sb("tT", [P, DT, T])
        yb = sb("yb", [P, TT, D])
        x1 = sb("x1", [P, TT, D])
        x2 = sb("x2", [P, TT, D])
        xn = att1
        bst = sb("bst", [P, TT, 6])
        mv = sb("mv", [P, TT, 2])
        var = sb("var", [P, TT])
        rstd = sb("rstd", [P, TT])
        q2T = sb("q2T", [P, 2, T])
        att2 = sb("att2", [P, TT, T])
        junk = sb("junk", [P, 1])
        idle_v = sb("idle_v", [P, 1])
        junk2 = sb("junk2", [P, 1])
        mx2 = sb("mx2", [P, TT])
        sm2 = sb("sm2", [P, TT])
        V3 = OT
        ra = rt[:, 0:1024].rearrange("p (i a t) -> p i a t", i=2, a=2)
        rb = rt[:, 1024:2048].rearrange("p (i a t) -> p i a t", i=2, a=2)
        QK3 = ptq[:, 0:(G3 + H3) * T].rearrange("p (h t) -> p h t", t=T)
        mx3 = sb("mx3", [P, 2, 4])
        sm3 = sb("sm3", [P, 2, 4])
        rc3 = sb("rc3", [P, 2, 4])
        P3 = sb("P3", [P, 2, 2, 384])
        PT3 = sb("PT3", [P, 2, 384])
        O3 = QT[:, :, :].rearrange("p h t -> p (h t)").bitcast(F32).rearrange("p (h t) -> p h t", t=T)

        acc = sb("acc", [P, NT, D])
        n2T = sb("n2T", [P, DT, NTOK])
        lg = sb("lg", [P, NT, E])
        top = sb("top", [P, NT, 8])
        tix = sb("tix", [P, NT, 8], U32)
        tixf = sb("tixf", [P, NT, 8])
        pr = sb("pr", [P, 4, NT])
        wgt = sb("wgt", [P, NT, E])
        wgt2 = sb("wgt2", [P, NT, E])
        bstF = sb("bstF", [P, NT, 6])
        mvF = sb("mvF", [P, NT, 2])
        varF = sb("varF", [P, NT])
        nhF = sb("nhF", [P, NT])
        rstdF = sb("rstdF", [P, NT])

        e1s = [w3[:, i, 0:1024].rearrange("p (k f) -> p k f", k=DT) for i in range(2)]
        e3s = [w3[:, i, 1024:2048].rearrange("p (k f) -> p k f", k=DT) for i in range(2)]
        e2s = [w3[:, i, 2048:3072].rearrange("p (k f) -> p k f", k=FT) for i in range(2)]
        sil = rt[:, 0:1024].rearrange("p (c t) -> p c t", c=2)
        hT = QK3[:, 0:16, :].rearrange("p (f c) t -> p f (c t)", f=FT)

        ld_w1 = sem("ld_w1")
        ld_w1o = sem("ld_w1o")
        ld_w2 = sem("ld_w2")
        ld_w3v = sem("ld_w3v")
        ld_w3k = sem("ld_w3k")
        ld_w3q = sem("ld_w3q")
        ld_w3o = sem("ld_w3o")
        ld_gate = sem("ld_gate")
        ld_small = sem("ld_small")
        ld_xT = sem("ld_xT")
        ld_x = sem("ld_x")
        ld_c = sem("ld_c")
        ld_e = [sem(f"ld_e{i}") for i in range(2)]
        consts_made = sem("consts_made")
        S = Ring([sem(f"S_filled{i}") for i in range(2)], [sem(f"S_emptied{i}") for i in range(2)], S_USES)
        O = Ring([sem(f"O_filled{i}") for i in range(2)], [sem(f"O_emptied{i}") for i in range(2)], O_USES)
        G = Ring([sem(f"G_filled{i}") for i in range(2)], [sem(f"G_emptied{i}") for i in range(2)], G_USES)
        vec_step = sem("vec_step")
        pool_step = sem("pool_step")
        act_step = sem("act_step")
        roped1 = sem("roped1")
        summed1 = sem("summed1")
        high1 = sem("high1")
        rest1 = sem("rest1")
        mid1 = sem("mid1")
        low1 = sem("low1")
        packed1 = sem("packed1")
        maxed1 = sem("maxed1")
        attn1 = sem("attn1")
        var_ready = sem("var_ready")
        rstd_ready = sem("rstd_ready")
        x1_ready = sem("x1_ready")
        att2_max = sem("att2_max")
        att2_exp = sem("att2_exp")
        att2_ready = sem("att2_ready")
        xn_ready = sem("xn_ready")
        roped3 = sem("roped3")
        summed3 = sem("summed3")
        max3 = sem("max3")
        rec3 = sem("rec3")
        norm3 = sem("norm3")
        exp3 = sem("exp3")
        batch_done = sem("batch_done")
        lam_dots = sem("lam_dots")
        lam_exp = sem("lam_exp")
        lg_filled = sem("lg_filled")
        top_diff = sem("top_diff")
        top_exp = sem("top_exp")
        A_filled = [sem(f"A_filled{i}") for i in range(2)]
        A_read = [sem(f"A_read{i}") for i in range(2)]
        B_filled = [sem(f"B_filled{i}") for i in range(2)]
        h_ready = [sem(f"h_ready{i}") for i in range(2)]
        Y_filled = [sem(f"Y_filled{i}") for i in range(2)]
        Y_added = [sem(f"Y_added{i}") for i in range(2)]
        fin_var = sem("fin_var")
        fin_rstd = sem("fin_rstd")
        fin_ready = sem("fin_ready")
        stored = sem("stored")

        psT = psS[:, :, :].bitcast(BF16)
        block = ctx.enter_context(nc.Block())

        @block.sync
        def _(sp):
            sp.dma_start(wqkv1[:], w1qkv.rearrange("(k p) n -> p k n", p=P)).then_inc(ld_w1, 16)
            sp.dma_start(rope1s[:], rope1.rearrange("(t p) c d -> p t c d", p=P)).then_inc(ld_w1, 16)

            def load_batch(b):
                sp.wait_ge(S.emptied[0], b * S.half + 1)
                sp.wait_ge(S.emptied[1], b * S.half + 1)
                sp.dma_start(xTs[:], xT[bass.ds(b, 1), :, :].rearrange("o (k p) t -> p (o k) t", p=P)).then_inc(ld_xT, 16)
                sp.wait_ge(batch_done, b + 1)
                sp.dma_start(cTs[:], ctxT[bass.ds(b, 1), :, :].rearrange("o p t -> p (o t)")).then_inc(ld_c, 16)
                sp.dma_start(xs[:], x[bass.ds(b, 1), :, :].rearrange("o (k p) d -> p (o k) d", p=P)).then_inc(ld_x, 16)

            load_batch(0)
            sp.dma_start(wq2[:], w2q).then_inc(ld_w2, 16)
            sp.dma_start(wk2[:], w2k).then_inc(ld_w2, 16)
            sp.dma_start(b2s[:], b2).then_inc(ld_w2, 16)
            sp.dma_start(nws[:], nw).then_inc(ld_small, 16)
            sp.dma_start(lams[:], lam.partition_broadcast(P)).then_inc(ld_small, 16)
            sp.dma_start(wo1[:], w1o.rearrange("(k p) n -> p k n", p=P)).then_inc(ld_w1o, 16)
            sp.dma_start(rope3s[:], rope3).then_inc(ld_small, 16)
            sp.dma_start(wv3, w3v.rearrange("(k p) n -> p k n", p=P)).then_inc(ld_w3v, 16)
            sp.dma_start(wk3, w3k.rearrange("(k p) n -> p k n", p=P)).then_inc(ld_w3k, 16)
            sp.dma_start(wq3, w3q.rearrange("(k p) n -> p k n", p=P)).then_inc(ld_w3q, 16)
            sp.dma_start(wo3[:], w3o.rearrange("(k p) n -> p k n", p=P)).then_inc(ld_w3o, 16)
            sp.dma_start(gates[:], gate.rearrange("(k p) n -> p k n", p=P)).then_inc(ld_gate, 16)

            def load_expert(e, i):
                sp.dma_start(e1s[i], e1[bass.ds(e, 1), :, :].rearrange("o (k p) f -> p (o k) f", p=P)).then_inc(ld_e[i], 16)
                sp.dma_start(e3s[i], e3[bass.ds(e, 1), :, :].rearrange("o (k p) f -> p (o k) f", p=P)).then_inc(ld_e[i], 16)
                sp.dma_start(e2s[i], e2[bass.ds(e, 1), :, :].rearrange("o (k p) f -> p (o k) f", p=P)).then_inc(ld_e[i], 16)

            with sp.Fori(1, B) as b:
                load_batch(b)
            for u in (G_P3 + 8, G_P3 + 9):
                sp.wait_ge(G.emptied[u % 2], (B - 1) * G.half + u // 2 + 2)
            load_expert(0, 0)
            load_expert(1, 1)
            with sp.Fori(1, E // 2) as ep:
                for i in range(2):
                    sp.wait_ge(Y_filled[1], ep * NT + (i - 1) * NT // 2)
                    load_expert(ep * 2 + i, i)
            for t in range(NT):
                sp.wait_ge(fin_ready, t + 1)
                sp.dma_start(out.rearrange("b (t p) d -> p (b t) d", p=P)[:, t, :], acc[:, t, :]).then_inc(stored, 16)
            sp.wait_ge(stored, 16 * NT)

        @block.tensor
        def _(pe):
            mm = pe.matmul

            def project1(b):
                pe.wait_ge(ld_xT, b * 16 + 16)
                for t in range(TT):
                    S.wait_empty(pe, b, S_PROJ + t)
                    for lo, n in ((0, 512), (512, 192)):
                        for k in range(DT):
                            last = mm(psS[:, t, lo:lo + n], xTs[:, k, t * P:(t + 1) * P], wqkv1[:, k, lo:lo + n],
                                      start=(k == 0), stop=(k == DT - 1))
                    last.then_inc(S.filled[t], 1)

            def queries2(b):
                pe.wait_ge(ld_c, b * 16 + 16)
                G.wait_empty(pe, b, G_QK2)
                mm(psG[:, 0, 0:T], wq2[:], cTs[:], start=True, stop=True)
                mm(psG[:, 0, T:2 * T], wk2[:], cTs[:], start=True, stop=True).then_inc(G.filled[0], 1)

            def energy2(b):
                G.wait_emptied(pe, b, G_QK2)
                G.wait_empty(pe, b, G_EN)
                for n in range(TT):
                    last = mm(psG[:, 1, n * T:(n + 1) * T], q2T[:, 0, n * P:(n + 1) * P], q2T[:, 1, :], start=True, stop=True)
                last.then_inc(G.filled[1], 1)

            def turn(b, u, src, nblk):
                S.wait_empty(pe, b, u)
                for j in range(nblk):
                    last = pe.transpose(psT[:, u % 2, j * P:(j + 1) * P], src(j), identb[:])
                last.then_inc(S.filled[u % 2], 1)

            def turn_k(b):
                for t in range(TT):
                    pe.wait_ge(packed1, b * TT + t + 1)
                    turn(b, S_KT + t, lambda j: kpack[:, t, j, :, :].rearrange("p a c -> p (a c)"), 16)

            def turn_q(b, u0):
                for t in range(TT):
                    for s in range(2):
                        turn(b, u0 + 2 * t + s,
                             lambda j: qpack[:, t, 32 * s + 2 * j:32 * s + 2 * j + 2, :].rearrange("p a c -> p (a c)"), 16)

            def max_scores(b):
                for u in (S_MAX - 2, S_MAX - 1):
                    S.wait_emptied(pe, b, u)
                u = S_MAX
                for s in range(2):
                    for t, pairs in ((0, 4), (1, 2)):
                        keys = P * (t + 1)
                        for j0 in range(0, 16, pairs):
                            S.wait_empty(pe, b, u)
                            for j in range(j0, j0 + pairs):
                                w = 2 * keys
                                o = psS[:, u % 2, (j - j0) * w:(j - j0 + 1) * w].rearrange("p (a k) -> p a k", a=2)
                                g = (j * 2) // REP1
                                mm(o, QT[:, s * 16 + j, t * P:(t + 1) * P], KT[:, s * G1 + g, :, 0:keys],
                                   start=(j - j0) * w % 512 == 0, stop=True, skip_group_check=True)
                                last = mm(o[:, :, keys - P:keys], identb[:], maskb[:].unsqueeze(1).broadcast_to([P, 2, P]),
                                          start=False, stop=True, skip_group_check=True)
                            last.then_inc(S.filled[u % 2], 1)
                            u += 1

            def scoresT(b, g):
                u = S_EXP + 3 * g
                for s in range(2):
                    S.wait_empty(pe, b, u + s)
                    for a in range(2):
                        o = psS[:, (u + s) % 2, a * 512:(a + 1) * 512].rearrange("p (j q) -> p j q", q=T)
                        mm(o, KT[:, s * G1 + g, a, 0:P], QT[:, s * 16 + 2 * g:s * 16 + 2 * g + 2, :], start=True, stop=True)
                        last = mm(o[:, :, 0:P], identb[:], maskTb[:].unsqueeze(1).broadcast_to([P, 2, P]),
                                  start=False, stop=True, skip_group_check=True)
                    last.then_inc(S.filled[(u + s) % 2], 1)
                S.wait_empty(pe, b, u + 2)
                for s in range(2):
                    for a in range(2):
                        lo = s * 512 + a * T
                        mm(psS[:, (u + 2) % 2, lo:lo + T], KT[:, s * G1 + g, a, P:T],
                           QT[:, s * 16 + 2 * g:s * 16 + 2 * g + 2, P:T], start=True, stop=False)
                        last = mm(psS[:, (u + 2) % 2, lo:lo + T], identb[:], maskTb[:].unsqueeze(1).broadcast_to([P, 2, P]),
                                  start=False, stop=True)
                last.then_inc(S.filled[(u + 2) % 2], 1)

            def values1(b, g):
                o, i = psO[:, g % 2, :], g % 2
                O.wait_empty(pe, b, O_PV + g)
                for u in (S_EXP + 3 * g + 1, S_EXP + 3 * g + 2):
                    S.wait_emptied(pe, b, u)
                for j in range(4):
                    s, a = j // 2, j % 2
                    mm(o[32 * j:32 * j + 32, :], Vx[:, 0, g, :], PT[:, i, s, a * 512:(a + 1) * 512], start=True, stop=True)
                for j in range(4):
                    s, a = j // 2, j % 2
                    last = mm(o[32 * j:32 * j + 32, :].rearrange("p (j q) -> p j q", j=2)[:, :, P:T], Vx[:, 1, g, :],
                              PT[:, i, 2, s * 512 + a * T:s * 512 + (a + 1) * T].rearrange("p (j q) -> p j q", j=2),
                              start=False, stop=True, skip_group_check=True)
                last.then_inc(O.filled[i], 1)

            def turn_o(b, g):
                O.wait_emptied(pe, b, O_PV + g)
                G.wait_empty(pe, b, G_OT + g)
                for j in range(4):
                    last = pe.transpose(psG[:, g % 2, j * P:(j + 1) * P], OT[:, g % 2, j * P:(j + 1) * P], ident[:])
                last.then_inc(G.filled[g % 2], 1)

            def turn4(b, u, src):
                G.wait_empty(pe, b, u)
                for k in range(DT):
                    for t in range(TT):
                        last = pe.transpose(psG[:, u % 2, k * T + t * P:k * T + (t + 1) * P], src[:, t, k * P:(k + 1) * P], ident[:])
                last.then_inc(G.filled[u % 2], 1)

            def rows(b, u, lhs, rhs, n):
                G.wait_empty(pe, b, u)
                for t in range(TT):
                    for k in range(n):
                        last = mm(psG[:, u % 2, t * D:(t + 1) * D], lhs(k, t), rhs(k), start=(k == 0), stop=(k == n - 1))
                last.then_inc(G.filled[u % 2], 1)

            def project3(b):
                G.wait_emptied(pe, b, G_N1T)
                for t in range(TT):
                    u = G_V3 + t
                    G.wait_empty(pe, b, u)
                    for k in range(DT):
                        last = mm(psG[:, u % 2, :], tT[:, k, t * P:(t + 1) * P], wv3[:, k, :], start=(k == 0), stop=(k == DT - 1))
                    last.then_inc(G.filled[u % 2], 1)
                for c in range((G3 + H3) // 2):
                    u = G_P3 + c
                    G.wait_empty(pe, b, u)
                    for a in range(2):
                        h = 2 * c + a
                        w, n = (wk3, h) if h < G3 else (wq3, h - G3)
                        for k in range(DT):
                            last = mm(psG[:, u % 2, a * T:(a + 1) * T], w[:, k, n * P:(n + 1) * P], tT[:, k, :],
                                      start=(k == 0), stop=(k == DT - 1))
                    last.then_inc(G.filled[u % 2], 1)

            def scores3(b, c):
                u = S_FFN + c
                pe.wait_ge(summed3, b * 10 + 4 + c)
                S.wait_empty(pe, b, u)
                for a in range(2):
                    h = 2 * c + a
                    q, k = QK3[:, G3 + h, :], QK3[:, h // REP3, :]
                    o = psS[:, u % 2, a * 512:a * 512 + 384]
                    mm(o[:, 0:P], q[:, 0:P], k[:, 0:P], start=True, stop=False)
                    mm(o[:, 0:P], identb[:], maskb[:], start=False, stop=True)
                    mm(o[:, P:384], q[:, P:T], k[:, :], start=True, stop=True)
                    last = mm(o[:, T:384], identb[:], maskb[:], start=False, stop=True, skip_group_check=True)
                last.then_inc(S.filled[u % 2], 1)

            def turn_p(b, h):
                u, c, a = O_PT + h, h // 2, h % 2
                pe.wait_ge(norm3, b * 8 + c + 1)
                O.wait_empty(pe, b, u)
                src = P3[:, c % 2, a, :]
                for dst, lo in ((0, 0), (P, P), (T, T)):
                    last = pe.transpose(psO[:, u % 2, dst:dst + P], src[:, lo:lo + P], ident[:])
                last.then_inc(O.filled[u % 2], 1)

            def values3(b, c):
                u = G_PV3 + c
                G.wait_empty(pe, b, u)
                for a in range(2):
                    h = 2 * c + a
                    g = h // REP3
                    O.wait_emptied(pe, b, O_PT + h)
                    o = psG[:, u % 2, a * T:(a + 1) * T]
                    mm(o, V3[:, 0, g * P:(g + 1) * P], PT3[:, a, 0:T], start=True, stop=True)
                    last = mm(o[:, P:T], V3[:, 1, g * P:(g + 1) * P], PT3[:, a, T:384], start=False, stop=True,
                              skip_group_check=True)
                last.then_inc(G.filled[u % 2], 1)

            pe.wait_ge(consts_made, 1)
            pe.wait_ge(ld_w1, 32)
            pe.wait_ge(ld_w2, 48)
            pe.wait_ge(ld_w1o, 16)
            for s_ in (ld_w3v, ld_w3k, ld_w3q, ld_w3o):
                pe.wait_ge(s_, 16)
            with pe.Fori(0, B) as b:
                project1(b)
                queries2(b)
                energy2(b)
                turn_k(b)
                turn_q(b, S_QT)
                max_scores(b)
                pe.wait_ge(maxed1, b + 1)
                turn_q(b, S_QT2)
                for u in (S_QT2 + 2, S_QT2 + 3):
                    S.wait_emptied(pe, b, u)
                for g in range(G1):
                    scoresT(b, g)
                    if g >= 1:
                        values1(b, g - 1)
                    if g >= 2:
                        turn_o(b, g - 2)
                values1(b, G1 - 1)
                turn_o(b, G1 - 2)
                turn_o(b, G1 - 1)
                pe.wait_ge(attn1, b + 1)
                turn4(b, G_AT, att1)
                G.wait_emptied(pe, b, G_AT)
                rows(b, G_WO, lambda k, t: tT[:, k, t * P:(t + 1) * P], lambda k: wo1[:, k, :], DT)
                pe.wait_ge(att2_ready, b + 1)
                turn4(b, G_A2T, att2)
                pe.wait_ge(x1_ready, b + 1)
                turn4(b, G_X1T, x1)
                G.wait_emptied(pe, b, G_A2T)
                G.wait_emptied(pe, b, G_X1T)
                rows(b, G_XM, lambda k, t: tT[:, k, t * P:(t + 1) * P], lambda k: q2T[:, k, :], DT)
                pe.wait_ge(xn_ready, 2 * b + 1)
                turn4(b, G_N1T, xn)
                project3(b)
                for c in range(H3 // 2 + 1):
                    if c < H3 // 2:
                        scores3(b, c)
                    if c >= 1:
                        turn_p(b, 2 * c - 2)
                        turn_p(b, 2 * c - 1)
                        values3(b, c - 1)
                G.wait_emptied(pe, b, G_PV3 + 6)
                G.wait_emptied(pe, b, G_PV3 + 7)
                rows(b, G_WO3, lambda k, t: O3[:, k, t * P:(t + 1) * P], lambda k: wo3[:, k, :], H3)
                pe.wait_ge(xn_ready, 2 * b + 2)
                turn4(b, G_N2T, xn)

            for i in range(2):
                pe.wait_ge(G.emptied[i], B * G.half + 1)
                pe.wait_ge(S.emptied[i], B * S.half + 1)
                pe.wait_ge(O.emptied[i], B * O.half + 1)
            pe.wait_ge(ld_gate, 16)
            for t in range(NT):
                for k in range(DT):
                    last = mm(psG[:, 0, t * E:(t + 1) * E], n2T[:, k, t * P:(t + 1) * P], gates[:, k, :],
                              start=(k == 0), stop=(k == DT - 1))
            last.then_inc(lg_filled, 1)
            with pe.Fori(0, E // 2) as ep:
                for i in range(2):
                    pe.wait_ge(ld_e[i], ep * 48 + 48)
                    for f in range(FT):
                        for c in range(2):
                            pe.wait_ge(A_read[c], ep * 8 + 4 * i + f + 1)
                            pe.wait_ge(h_ready[c], ep * 8 + 4 * i + f + 1)
                            for k in range(DT):
                                last = mm(psS[:, c, 0:512], e1s[i][:, k, f * P:(f + 1) * P], n2T[:, k, c * 512:(c + 1) * 512],
                                          start=(k == 0), stop=(k == DT - 1))
                            last.then_inc(A_filled[c], 1)
                            for k in range(DT):
                                last = mm(psS[:, c, 512:1024], e3s[i][:, k, f * P:(f + 1) * P], n2T[:, k, c * 512:(c + 1) * 512],
                                          start=(k == 0), stop=(k == DT - 1))
                            last.then_inc(B_filled[c], 1)
                    for t in range(NT):
                        c = t // 4
                        pe.wait_ge(h_ready[c], ep * 8 + 4 * i + 5)
                        pe.wait_ge(Y_added[t % 2], ep * 8 + 4 * i + t // 2 + 1)
                        for f in range(FT):
                            last = mm(psO[:, t % 2, 0:D], hT[:, f, t * P:(t + 1) * P], e2s[i][:, f, :],
                                      start=(f == 0), stop=(f == FT - 1))
                        last.then_inc(Y_filled[t % 2], 1)

        @block.vector
        def _(dve):
            v = nc.vector
            PER = VEC_STEPS
            n = [0]
            base = [0]

            def link(ins):
                ins.then_inc(vec_step, 1)
                n[0] += 1
                dve.wait_ge(vec_step, base[0] + n[0])

            def rope1_products(b):
                for t in range(TT):
                    u = S_PROJ + t
                    S.wait_filled(dve, b, u)
                    qk = psS[:, t, 0:640].rearrange("p (h d) -> p h d", d=HD1)
                    c, s = rope1s[:, t, 0, :], rope1s[:, t, 1, :]
                    v.tensor_tensor(rt1[:, t, :].rearrange("p (h d) -> p h d", d=HD1), qk,
                                    c.unsqueeze(1).broadcast_to([P, 80, HD1]), ALU.mult)
                    r = rt2[:, t, :].rearrange("p (h d) -> p h d", d=HD1)
                    v.tensor_tensor(r[:, :, 0:4], qk[:, :, 4:8], s[:, 0:4].unsqueeze(1).broadcast_to([P, 80, 4]), ALU.mult)
                    v.tensor_tensor(r[:, :, 4:8], qk[:, :, 0:4], s[:, 4:8].unsqueeze(1).broadcast_to([P, 80, 4]),
                                    ALU.mult).then_inc(roped1, 1)
                    v.tensor_copy(Vx[:, t, :, 0:HD1], psS[:, t, 640:704].rearrange("p (g d) -> p g d", d=HD1)).then_inc(S.emptied[t], 1)

            def qk2_evacuate(b):
                G.wait_filled(dve, b, G_QK2)
                v.tensor_scalar(q2T[:, 0, :], psG[:, 0, 0:T], b2s[:, 0:1], None, ALU.add)
                v.tensor_scalar(q2T[:, 1, :], psG[:, 0, T:2 * T], b2s[:, 1:2], None, ALU.add).then_inc(G.emptied[0], 1)

            def energy_max(b):
                G.wait_filled(dve, b, G_EN)
                v.tensor_reduce(mx2[:], psG[:, 1, :].rearrange("p (n m) -> p n m", n=TT), AX.X, ALU.max, negate=True)\
                    .then_inc(att2_max, 1)

            def att2_normalise(b):
                dve.wait_ge(att2_exp, b + 1)
                link(v.reciprocal(sm2[:], sm2[:]))
                v.tensor_tensor(att2[:], att2[:], sm2[:].unsqueeze(2).broadcast_to([P, TT, T]), ALU.mult).then_inc(att2_ready, 1)

            def pack(b):
                for t in range(TT):
                    v.memset(qpack[:, t, :, 48:51], 0.0)
                    dve.wait_ge(high1, b * TT + t + 1)
                    for parts, src, done in (((0, 3), hib, None), ((3, 2), midb, mid1), ((5, 1), lob, low1)):
                        if done is not None:
                            dve.wait_ge(done, b * TT + t + 1)
                        lo, k = parts
                        v.tensor_copy(qpack[:, t, :, lo * 8:(lo + k) * 8].rearrange("p h (c d) -> p h c d", c=k),
                                      src[:, t, 0:512].rearrange("p (h d) -> p h d", d=HD1).unsqueeze(2).broadcast_to([P, 64, k, HD1]))
                    for a in range(2):
                        for slots, src in (((0, 3, 5), hib), ((1, 4), midb), ((2,), lob)):
                            for sl in slots:
                                last = v.tensor_copy(kpack[:, t, :, a, sl * 8:sl * 8 + 8],
                                                     src[:, t, 512:640].rearrange("p (h d) -> p h d", d=HD1))
                    last.then_inc(packed1, 1)

            def evac_k(b):
                for t in range(TT):
                    u = S_KT + t
                    S.wait_filled(dve, b, u)
                    src = psT[:, u % 2, :].rearrange("p (j q) -> p j q", q=P)
                    v.tensor_copy(KT[0:64, :, 0, t * P:(t + 1) * P], src[0:64])
                    v.tensor_copy(KT[64:128, :, 1, t * P:(t + 1) * P], src[64:128]).then_inc(S.emptied[u % 2], 1)

            def evac_q(b, u0):
                for t in range(TT):
                    for s in range(2):
                        u = u0 + 2 * t + s
                        S.wait_filled(dve, b, u)
                        v.tensor_copy(QT[:, 16 * s:16 * s + 16, t * P:(t + 1) * P],
                                      psT[:, u % 2, :].rearrange("p (j q) -> p j q", q=P)).then_inc(S.emptied[u % 2], 1)

            def maxima1(b):
                u = S_MAX
                for s in range(2):
                    for t, heads in ((0, 8), (1, 4)):
                        for h0 in range(0, H1, heads):
                            S.wait_filled(dve, b, u)
                            v.tensor_reduce(negm[:, t, s * H1 + h0:s * H1 + h0 + heads],
                                            psS[:, u % 2, :].rearrange("p (h k) -> p h k", h=heads),
                                            AX.X, ALU.max, negate=True).then_inc(S.emptied[u % 2], 1)
                            u += 1
                S.wait_emptied(dve, b, u - 1)
                q = [qpack[:, :, :, 48 + i] for i in range(3)]
                link(v.tensor_copy(q[0], negm[:]))
                link(v.tensor_tensor(mres[:], negm[:], q[0], ALU.subtract))
                link(v.tensor_copy(q[1], mres[:]))
                link(v.tensor_tensor(mres[:], mres[:], q[1], ALU.subtract))
                v.tensor_copy(q[2], mres[:]).then_inc(maxed1, 1)

            def evac_o(b, g):
                O.wait_filled(dve, b, O_PV + g)
                v.tensor_copy(OT[:, g % 2, :], psO[:, g % 2, :]).then_inc(O.emptied[g % 2], 1)

            def normalise1(b, g):
                G.wait_filled(dve, b, G_OT + g)
                o = psG[:, g % 2, :].rearrange("p (j a c) -> p j a c", j=4, a=4)
                i = g % 2
                link(v.reciprocal(rs1[:, i], o[:, :, :, HD1]))
                link(v.tensor_tensor(rs1[:, i], rs1[:, i], fac[:].rearrange("p s a -> p (s a)").unsqueeze(1).broadcast_to([P, 4, 4]),
                                     ALU.mult))
                ins = v.tensor_tensor(on1[:, i], o[:, :, :, 0:HD1], rs1[:, i].unsqueeze(3).broadcast_to([P, 4, 4, HD1]), ALU.mult)
                ins.then_inc(G.emptied[g % 2], 1)
                G.wait_emptied(dve, b, G_OT + g)
                s1 = on1[:, i].rearrange("p (j t) (s a) d -> p s j t (a d)", t=TT, s=2)
                for t in range(TT):
                    last = v.tensor_tensor(att1[:, t, g * 32:(g + 1) * 32].rearrange("p (j c) -> p j c", j=2),
                                           s1[:, 0, :, t, :], s1[:, 1, :, t, :], ALU.subtract)
                if g == G1 - 1:
                    last.then_inc(attn1, 1)

            def evac4(b, u, dst=tT):
                G.wait_filled(dve, b, u)
                v.tensor_copy(dst[:].rearrange("p k t -> p (k t)"), psG[:, u % 2, :]).then_inc(G.emptied[u % 2], 1)

            def evac4_scaled(b, u, w, dst):
                G.wait_filled(dve, b, u)
                for k in range(DT):
                    last = v.tensor_scalar(dst[:, k, :] if isinstance(dst, list) is False else dst[k],
                                           psG[:, u % 2, k * T:(k + 1) * T], nws[:, w, k:k + 1], None, ALU.mult)
                last.then_inc(G.emptied[u % 2], 1)

            def layer_norm(b, u, res, dst, nth, ready):
                G.wait_filled(dve, b, u)
                v.tensor_tensor(yb[:], psG[:, u % 2, :].rearrange("p (t d) -> p t d", t=TT), res[:], ALU.add)\
                    .then_inc(G.emptied[u % 2], 1)
                G.wait_emptied(dve, b, u)
                for t in range(TT):
                    ins = v.bn_stats(bst[:, t, :], yb[:, t, :])
                link(ins)
                v.memset(idle_v[:], 0.0)
                for t in range(TT):
                    ins = v.bn_aggr(mv[:, t, :], bst[:, t, :])
                link(ins)
                v.tensor_scalar(var[:], mv[:, :, 1], EPS, None, ALU.add).then_inc(var_ready, 1)
                dve.wait_ge(rstd_ready, b * 4 + nth + 1)
                for t in range(TT):
                    last = v.tensor_scalar(dst[:, t, :], yb[:, t, :], mv[:, t, 0:1], rstd[:, t:t + 1], ALU.subtract, ALU.mult)
                if ready is None:
                    link(last)
                else:
                    last.then_inc(ready, 1)

            def rms_norm(b, src, nth):
                for t in range(TT):
                    ins = v.tensor_tensor_reduce(xn[:, t, :], src[:, t, :], src[:, t, :], 1.0, 0.0, ALU.mult, ALU.add,
                                                 mv[:, t, 0:1])
                link(ins)
                v.tensor_scalar(var[:], mv[:, :, 0], 1.0 / D, EPS, ALU.mult, ALU.add).then_inc(var_ready, 1)
                dve.wait_ge(rstd_ready, b * 4 + nth + 1)
                for t in range(TT):
                    last = v.tensor_scalar(xn[:, t, :], src[:, t, :], rstd[:, t:t + 1], None, ALU.mult)
                last.then_inc(xn_ready, 1)

            def rope3_products(b, c):
                u = G_P3 + c
                i = c % 2
                G.wait_filled(dve, b, u)
                if c >= 2:
                    dve.wait_ge(summed3, b * 10 + c)
                q = psG[:, u % 2, :].rearrange("p (a t) -> p a t", a=2)
                cs, sn = rope3s[:, 0, :].unsqueeze(1), rope3s[:, 1, :].unsqueeze(1)
                v.tensor_tensor(ra[:, i], q, cs.broadcast_to([P, 2, T]), ALU.mult)
                v.tensor_tensor(rb[0:64, i], q[64:128], sn[64:128].broadcast_to([64, 2, T]), ALU.mult)
                v.tensor_tensor(rb[64:128, i], q[0:64], sn[0:64].broadcast_to([64, 2, T]), ALU.mult).then_inc(G.emptied[u % 2], 1)

            def maxima3(b, c):
                u, i = S_FFN + c, c % 2
                S.wait_filled(dve, b, u)
                o = psS[:, u % 2, :].rearrange("p (a k) -> p a k", a=2)
                v.tensor_reduce(mx3[:, i, 0:2], o[:, :, 0:P], AX.X, ALU.max, negate=True)
                link(v.tensor_reduce(mx3[:, i, 2:4], o[:, :, P:384], AX.X, ALU.max, negate=True))
                v.tensor_scalar(mx3[:, i, :], mx3[:, i, :], HD3 ** -0.5, None, ALU.mult).then_inc(max3, 1)

            def recip3(b, c):
                dve.wait_ge(exp3, b * 8 + c + 1)
                v.reciprocal(rc3[:, c % 2, :], sm3[:, c % 2, :]).then_inc(rec3, 1)

            for start in (*S.emptied, *O.emptied, *G.emptied, *A_read, *h_ready, *Y_added, summed3, batch_done):
                dve.sem_inc(start, 1)
            v.memset(KT[:], 0.0)
            v.memset(qpack[:], 0.0)
            v.memset(kpack[:], 0.0)
            v.memset(Vx[:], 0.0)
            dve.wait_ge(ld_small, 48)
            link(v.tensor_tensor(lamp[:], lams[:, 0:4:2, :], lams[:, 1:4:2, :], ALU.mult))
            v.memset(kpack[:, :, :, :, 48:51], 1.0)
            v.memset(Vx[:, :, :, HD1:HD1 + 1], 1.0)
            v.tensor_reduce(lamd[:], lamp[:], AX.X, ALU.add).then_inc(lam_dots, 1)
            dve.wait_ge(lam_exp, 1)
            link(v.tensor_tensor(lamd[:, 0:1], lame[:, 0:1], lame[:, 1:2], ALU.subtract))
            v.memset(fac[:, 0, :], 1.0 - LAMBDA_INIT)
            for a in range(2):
                ins = v.tensor_scalar(fac[:, 1, a:a + 1], lamd[:, 0:1], LAMBDA_INIT, 1.0 - LAMBDA_INIT, ALU.add, ALU.mult)
            link(ins)
            dve.wait_ge(ld_w1, 32)
            dve.wait_ge(ld_w2, 48)
            once = n[0]
            n[0] = 0
            with dve.Fori(0, B) as b:
                base[0] = b * PER + once
                rope1_products(b)
                qk2_evacuate(b)
                energy_max(b)
                pack(b)
                evac_k(b)
                evac_q(b, S_QT)
                att2_normalise(b)
                maxima1(b)
                evac_q(b, S_QT2)
                for g in range(G1):
                    evac_o(b, g)
                    if g >= 1:
                        normalise1(b, g - 1)
                normalise1(b, G1 - 1)
                evac4(b, G_AT)
                dve.wait_ge(ld_x, b * 16 + 16)
                layer_norm(b, G_WO, xs, x1, 0, x1_ready)
                evac4(b, G_A2T, q2T)
                evac4(b, G_X1T)
                layer_norm(b, G_XM, x1, x2, 1, None)
                rms_norm(b, x2, 2)
                evac4_scaled(b, G_N1T, 0, tT)
                for c in range(10):
                    rope3_products(b, c)
                for c in range(H3 // 2):
                    maxima3(b, c)
                    recip3(b, c)
                G.wait_filled(dve, b, G_WO3)
                ins = v.tensor_tensor(yb[:], psG[:, G_WO3 % 2, :].rearrange("p (t d) -> p t d", t=TT), x2[:], ALU.add)
                ins.then_inc(G.emptied[G_WO3 % 2], 1)
                G.wait_emptied(dve, b, G_WO3)
                v.tensor_tensor(acc[:, bass.ds(b * TT, TT), :], yb[:], x2[:], ALU.add)
                rms_norm(b, yb, 3)
                G.wait_filled(dve, b, G_N2T)
                for k in range(DT):
                    ins = v.tensor_scalar(n2T[:, k, bass.ds(b * T, T)], psG[:, G_N2T % 2, k * T:(k + 1) * T],
                                          nws[:, 1, k:k + 1], None, ALU.mult)
                ins.then_inc(G.emptied[G_N2T % 2], 1)
                v.tensor_copy(mres[:, 0, 0:8], negm[:, 0, 0:8]).then_inc(batch_done, 1)
            assert n[0] == PER, n[0]
            base[0] = B * PER + once
            n[0] = 0

            dve.wait_ge(lg_filled, 1)
            link(v.tensor_copy(lg[:].rearrange("p t e -> p (t e)"), psG[:, 0, 0:NT * E]))
            for t in range(NT):
                ins = v.max(top[:, t, :], lg[:, t, :])
            link(ins)
            v.tensor_tensor(pr[:, 0, :], top[:, :, 1], top[:, :, 0], ALU.subtract).then_inc(top_diff, 1)
            for t in range(NT):
                ins = v.max_index(tix[:, t, :], top[:, t, :], lg[:, t, :])
            link(ins)
            link(v.tensor_copy(tixf[:], tix[:]))
            dve.wait_ge(top_exp, 1)
            link(v.tensor_scalar(pr[:, 2, :], pr[:, 1, :], 1.0, None, ALU.add))
            link(v.reciprocal(pr[:, 2, :], pr[:, 2, :]))
            link(v.tensor_tensor(pr[:, 3, :], pr[:, 1, :], pr[:, 2, :], ALU.mult))
            it = iota8[:].unsqueeze(1).broadcast_to([P, NT, E])
            for j, w in ((0, wgt), (1, wgt2)):
                link(v.tensor_tensor(w[:], it, tixf[:, :, j].unsqueeze(2).broadcast_to([P, NT, E]), ALU.is_equal))
                link(v.tensor_tensor(w[:], w[:], pr[:, 2 + j, :].unsqueeze(2).broadcast_to([P, NT, E]), ALU.mult))
            link(v.tensor_tensor(wgt[:], wgt[:], wgt2[:], ALU.add))
            with dve.Fori(0, E // 2) as ep:
                for i in range(2):
                    for f in range(FT):
                        for c in range(2):
                            dve.wait_ge(A_read[c], ep * 8 + 4 * i + f + 2)
                            dve.wait_ge(B_filled[c], ep * 8 + 4 * i + f + 1)
                            v.tensor_tensor(hT[:, f, c * 512:(c + 1) * 512], sil[:, c, :], psS[:, c, 512:1024], ALU.mult)\
                                .then_inc(h_ready[c], 1)
                    for t in range(NT):
                        dve.wait_ge(Y_filled[t % 2], ep * 8 + 4 * i + t // 2 + 1)
                        v.scalar_tensor_tensor(out=acc[:, t, :], in0=psO[:, t % 2, 0:D],
                                               scalar=wgt[:, t, bass.ds(ep * 2 + i, 1)],
                                               in1=acc[:, t, :], op0=ALU.mult, op1=ALU.add).then_inc(Y_added[t % 2], 1)
            dve.wait_ge(Y_added[0], E * 4 + 1)
            dve.wait_ge(Y_added[1], E * 4 + 1)
            for t in range(NT):
                ins = v.bn_stats(bstF[:, t, :], acc[:, t, :])
            link(ins)
            for t in range(NT):
                ins = v.bn_aggr(mvF[:, t, :], bstF[:, t, :])
            link(ins)
            v.tensor_scalar(varF[:], mvF[:, :, 1], EPS, None, ALU.add).then_inc(fin_var, 1)
            dve.wait_ge(fin_rstd, 1)
            for t in range(NT):
                v.tensor_scalar(acc[:, t, :], acc[:, t, :], mvF[:, t, 0:1], rstdF[:, t:t + 1],
                                ALU.subtract, ALU.mult).then_inc(fin_ready, 1)

        @block.scalar
        def _(act):
            a_ = nc.scalar

            def high_parts(b):
                for t in range(TT):
                    act.wait_ge(summed1, b * TT + t + 1)
                    a_.copy(hib[:, t, :], rt1[:, t, :]).then_inc(high1, 1)
                    act.wait_ge(rest1, b * TT + t + 1)
                    a_.copy(midb[:, t, :], rt1[:, t, :]).then_inc(mid1, 1)

            def exp2(b):
                act.wait_ge(att2_max, b + 1)
                for n in range(TT):
                    ins = a_.activation(att2[:, n, :], psG[:, 1, n * T:(n + 1) * T], ACT.Exp, bias=mx2[:, n:n + 1],
                                        accum_out=sm2[:, n:n + 1])
                ins.then_inc(act_step, 1)
                act.wait_ge(act_step, b + 1)
                a_.copy(junk[:], ident[:, 0:1]).then_inc(G.emptied[1], 1)
                a_.copy(junk2[:], ident[:, 0:1]).then_inc(att2_exp, 1)

            def exp1(b):
                for g in range(G1):
                    if g >= 2:
                        O.wait_filled(act, b, O_PV + g - 2)
                    for c in range(3):
                        u = S_EXP + 3 * g + c
                        S.wait_filled(act, b, u)
                        a_.activation(PT[:, g % 2, c, :], psS[:, u % 2, :], ACT.Exp, scale=HD1 ** -0.5).then_inc(S.emptied[u % 2], 1)

            def evac_v3(b):
                for t in range(TT):
                    u = G_V3 + t
                    G.wait_filled(act, b, u)
                    a_.copy(V3[:, t, :], psG[:, u % 2, :]).then_inc(G.emptied[u % 2], 1)

            def exp3_(b, c):
                u, i = S_FFN + c, c % 2
                act.wait_ge(max3, b * 8 + c + 1)
                if c >= 2:
                    O.wait_filled(act, b, O_PT + 2 * c - 3)
                for a in range(2):
                    for t, (lo, hi) in enumerate(((0, P), (P, 384))):
                        ins = a_.activation(P3[:, i, a, lo:hi], psS[:, u % 2, a * 512 + lo:a * 512 + hi], ACT.Exp,
                                            bias=mx3[:, i, 2 * t + a:2 * t + a + 1], scale=HD3 ** -0.5,
                                            accum_out=sm3[:, i, 2 * t + a:2 * t + a + 1])
                ins.then_inc(exp3, 1)
                act.wait_ge(exp3, b * 8 + c + 1)
                a_.copy(junk[:], ident[:, 0:1]).then_inc(S.emptied[u % 2], 1)

            def evac_p(b, h):
                u = O_PT + h
                O.wait_filled(act, b, u)
                if h >= 2:
                    G.wait_filled(act, b, G_PV3 + h // 2 - 1)
                a_.copy(PT3[:, h % 2, :], psO[:, u % 2, 0:384]).then_inc(O.emptied[u % 2], 1)

            def evac_o3(b, c):
                u = G_PV3 + c
                G.wait_filled(act, b, u)
                a_.copy(O3[:, 2 * c:2 * c + 2, :], psG[:, u % 2, :].rearrange("p (a t) -> p a t", a=2)).then_inc(G.emptied[u % 2], 1)

            act.wait_ge(consts_made, 1)
            act.wait_ge(lam_dots, 1)
            a_.activation(lame[:], lamd[:], ACT.Exp).then_inc(lam_exp, 1)
            with act.Fori(0, B) as b:
                exp2(b)
                high_parts(b)
                exp1(b)
                evac_v3(b)
                for c in range(H3 // 2 + 1):
                    if c < H3 // 2:
                        exp3_(b, c)
                    if c >= 1:
                        evac_p(b, 2 * c - 2)
                        evac_p(b, 2 * c - 1)
                        evac_o3(b, c - 1)
            act.wait_ge(top_diff, 1)
            a_.activation(pr[:, 1, :], pr[:, 0, :], ACT.Exp).then_inc(top_exp, 1)
            with act.Fori(0, E // 2) as ep:
                for i in range(2):
                    for f in range(FT):
                        for c in range(2):
                            act.wait_ge(A_filled[c], ep * 8 + 4 * i + f + 1)
                            act.wait_ge(h_ready[c], ep * 8 + 4 * i + f + 1)
                            a_.activation(sil[:, c, :], psS[:, c, 0:512], ACT.Silu).then_inc(A_read[c], 1)

        @block.gpsimd
        def _(pool):
            p_ = nc.gpsimd
            p_.memset(ident[:], 0.0)
            p_.memset(maskb[:], 0.0)
            p_.memset(maskTb[:], 0.0)
            p_.memset(neghalf[:], -0.5)
            p_.memset(nhF[:], -0.5).then_inc(pool_step, 1)
            pool.wait_ge(pool_step, 1)
            p_.affine_select(out=ident[:], in_=ident[:], compare_op=ALU.not_equal, fill=1.0, base=0,
                             pattern=[[-1, P]], channel_multiplier=1).then_inc(pool_step, 1)
            p_.affine_select(out=maskb[:], in_=maskb[:], compare_op=ALU.is_ge, fill=NEG, base=0,
                             pattern=[[-1, P]], channel_multiplier=1)
            p_.affine_select(out=maskTb[:], in_=maskTb[:], compare_op=ALU.is_ge, fill=NEG, base=0,
                             pattern=[[1, P]], channel_multiplier=-1)
            p_.iota(iota8[:], [[1, E]], base=0, channel_multiplier=0, allow_small_or_imprecise_dtypes=True)
            pool.wait_ge(pool_step, 2)
            p_.tensor_copy(identb[:], ident[:]).then_inc(consts_made, 1)

            def root(b, nth):
                pool.wait_ge(var_ready, b * 4 + nth + 1)
                p_.tensor_tensor(rstd[:], var[:], neghalf[:], ALU.pow).then_inc(rstd_ready, 1)

            with pool.Fori(0, B) as b:
                for t in range(TT):
                    pool.wait_ge(roped1, b * TT + t + 1)
                    p_.tensor_tensor(rt1[:, t, :], rt1[:, t, :], rt2[:, t, :], ALU.add).then_inc(summed1, 1)
                    pool.wait_ge(high1, b * TT + t + 1)
                    p_.tensor_tensor(rt1[:, t, :], rt1[:, t, :], hib[:, t, :], ALU.subtract).then_inc(rest1, 1)
                    pool.wait_ge(mid1, b * TT + t + 1)
                    p_.tensor_tensor(lob[:, t, :], rt1[:, t, :], midb[:, t, :], ALU.subtract).then_inc(low1, 1)
                for nth in range(3):
                    root(b, nth)
                for c in range(10):
                    G.wait_emptied(pool, b, G_P3 + c)
                    p_.tensor_tensor(QK3[:, 2 * c:2 * c + 2, :], ra[:, c % 2], rb[:, c % 2], ALU.add).then_inc(summed3, 1)
                for c in range(H3 // 2):
                    i = c % 2
                    pool.wait_ge(rec3, b * 8 + c + 1)
                    p_.tensor_tensor(P3[:, i, :, 0:P], P3[:, i, :, 0:P], rc3[:, i, 0:2].unsqueeze(2).broadcast_to([P, 2, P]), ALU.mult)
                    p_.tensor_tensor(P3[:, i, :, P:384], P3[:, i, :, P:384], rc3[:, i, 2:4].unsqueeze(2).broadcast_to([P, 2, T]),
                                     ALU.mult).then_inc(norm3, 1)
                root(b, 3)
            pool.wait_ge(fin_var, 1)
            p_.tensor_tensor(rstdF[:], varF[:], nhF[:], ALU.pow).then_inc(fin_rstd, 1)


VEC_STEPS = 36


def kernel(**inputs):
    import numpy as _np
    import concourse.bacc as _bacc
    from concourse import mybir as _mybir
    from concourse.bass_utils import run_bass_kernel_spmd as _run

    i = {k: _np.asarray(v) for k, v in inputs.items()}
    f32 = _np.float32

    def angles(n, width, theta):
        inv = (1.0 / theta ** (_np.arange(0, width, 2, dtype=f32) / f32(width))).astype(f32)
        return _np.arange(n, dtype=f32)[:, None] * inv[None, :]

    a1 = angles(T, HD1, 10000.0)
    s1 = _np.sin(a1)
    rope1 = _np.stack([_np.tile(_np.cos(a1), (1, 2)), _np.concatenate([-s1, s1], 1)], 1).astype(f32)
    a3 = angles(T, HD3, 1000000.0).T
    s3 = _np.sin(a3)
    rope3 = _np.stack([_np.tile(_np.cos(a3), (2, 1)), _np.concatenate([s3, -s3], 0)], 1).astype(f32)

    feed = {
        "x": i["x"],
        "xT": i["x"].transpose(0, 2, 1),
        "ctxT": i["ctx_1024"].transpose(0, 2, 1),
        "w1qkv": _np.concatenate([i["L0_attn_wq"].T, i["L0_attn_wk"].T, i["L0_attn_wv"].T], 1),
        "w1o": i["L0_attn_wo"].T,
        "lam": _np.stack([i["L0_attn_lambda_q1"], i["L0_attn_lambda_k1"], i["L0_attn_lambda_q2"], i["L0_attn_lambda_k2"]]),
        "w2q": i["L0_xattn_Wq"].T,
        "w2k": i["L0_xattn_Wk"].T,
        "b2": _np.stack([i["L0_xattn_bq"], i["L0_xattn_bk"]], 1),
        "nw": _np.stack([i["L0_ffn_norm1_w"].reshape(DT, P).T, i["L0_ffn_norm2_w"].reshape(DT, P).T], 1),
        "w3q": i["L0_ffn_wq"], "w3k": i["L0_ffn_wk"], "w3v": i["L0_ffn_wv"], "w3o": i["L0_ffn_wo"],
        "gate": i["L0_ffn_gate_w"],
        "e1": i["L0_ffn_w1"], "e3": i["L0_ffn_w3"], "e2": i["L0_ffn_w2"],
        "rope1": rope1, "rope3": rope3,
    }
    nc = _bacc.Bacc("TRN2", target_bir_lowering=False, num_devices=1)
    arrays, args = {}, []
    for name, a in feed.items():
        a = _np.ascontiguousarray(a)
        arrays[f"in_{name}"] = a
        args.append(nc.dram_tensor(f"in_{name}", a.shape, _mybir.dt.from_np(a.dtype), kind="ExternalInput").ap())
    args.append(nc.dram_tensor("out_0", (B, T, D), _mybir.dt.float32, kind="ExternalOutput").ap())
    decoder_kernel(nc, *args)
    r = _run(nc, [arrays], core_ids=[0])
    return r.results[0]["out_0"]
```

```python
from contextlib import ExitStack
import math

import numpy as np

import concourse.bass as bass
from concourse import mybir

P = 128
B, T, D = 4, 256, 256
TT, DT = T // P, D // P
H1, G1, HD1 = 32, 8, 8
REP1 = H1 // G1
PTN = 5
SLOT = 64
C2 = 128
H3, G3, HD3 = 16, 4, 128
REP3 = H3 // G3
E, F = 8, 512
FT = F // P
NTOK = B * T
NT = NTOK // P
LAMBDA_INIT = 0.8 - 0.6 * math.exp(-0.3 * 12)
EPS = 1e-5
NEG = -1e30

ALU = mybir.AluOpType
ACT = mybir.ActivationFunctionType
AX = mybir.AxisListType
F32 = mybir.dt.float32
F32R = mybir.dt.float32r
BF16 = mybir.dt.bfloat16
U32 = mybir.dt.uint32



class Ring:

    def __init__(self, filled, emptied, uses):
        self.filled, self.emptied, self.half = filled, emptied, uses // 2

    def wait_empty(self, eng, b, u):
        eng.wait_ge(self.emptied[u % 2], b * self.half + u // 2 + 1)

    def wait_filled(self, eng, b, u):
        eng.wait_ge(self.filled[u % 2], b * self.half + u // 2 + 1)

    def wait_emptied(self, eng, b, u):
        eng.wait_ge(self.emptied[u % 2], b * self.half + u // 2 + 2)


S_PROJ, S_KT, S_QT, S_MAX, S_QT2, S_EXP, S_USES = 0, 2, 4, 8, 32, 36, 60
A_NAMES = ["q2", "k2", "energy"]
for _g in range(G1):
    A_NAMES += [("pv", _g)] + ([("turn_o", _g - 1)] if _g else [])
A_NAMES += [("turn_o", G1 - 1), "turn_att1", "wo1", "turn_att2", "turn_x1", "x_m"]
A_USE = {name: n for n, name in enumerate(A_NAMES)}
K_NAMES = ["turn_n1", ("v3", 0), ("v3", 1)] + [("p3", c) for c in range((G3 + H3) // 2)]
for _c in range(H3 // 2 + 2):
    K_NAMES += [("pv3", _c - 2)] if _c > 1 else []
    K_NAMES += [("s3", 2 * _c), ("s3", 2 * _c + 1)] if _c < H3 // 2 else []
    K_NAMES += [("turn_p", 2 * _c - 2), ("turn_p", 2 * _c - 1)] if 0 < _c <= H3 // 2 else []
K_NAMES += [("wo3", 0), ("wo3", 1), "turn_n2"]
K_USE = {name: n for n, name in enumerate(K_NAMES)}
assert len(A_NAMES) % 2 == 0 and len(K_NAMES) % 2 == 0

FRONT, HEAD, BACK = 0, 1, 2


def pass_order():
    order = [(FRONT, "ctx", 0), (BACK, "n1", 0), (FRONT, "max", 0), (BACK, "n1 scale", 0), (FRONT, "max", 1), (FRONT, "max", 2),
             (FRONT, "energy", 0), (FRONT, "exp2", 0)]
    projections = [("t1", 0), ("v3", 0), ("v3", 1)] + [("p3", c) for c in range((G3 + H3) // 2)]
    maxima = list(range(3, 24))
    while projections:
        order += [(BACK, *projections.pop(0))]
        order += [(FRONT, "max", maxima.pop(0)) for _ in range(min(2, len(maxima)))]
        if not maxima and (FRONT, "packmax", 0) not in order:
            order += [(FRONT, "packmax", 0)]
    order += [(FRONT, "qt2", 0), (FRONT, "qt2", 1)]
    for g in range(G1 + 1):
        order += [(FRONT, "sTa", g)] if g < G1 else []
        order += [(BACK, "pv3", g - 2)] if g > 1 else []
        order += [(BACK, "s3", g), (BACK, "e3", g), (FRONT, "sTb", g)] if g < G1 else []
        order += [(FRONT, "pv", g - 1)] if g else []
        order += [(FRONT, "ot", g - 2)] if g > 1 else []
        order += [(BACK, "pt3", g - 1)] if g else []
        order += [(FRONT, "att2", 0)] if g == 1 else []
    order += [(HEAD, "proj", 0), (BACK, "pv3", G1 - 1), (FRONT, "ot", G1 - 1), (BACK, "wo3", 0), (FRONT, "at", 0), (HEAD, "pack", 0), (BACK, "wo3", 1),
              (FRONT, "wo", 0), (HEAD, "kt", 0), (FRONT, "a2t", 0), (BACK, "wo3", 2), (HEAD, "pack", 1), (FRONT, "x1t", 0),
              (BACK, "wo3", 3), (FRONT, "xm", 0), (HEAD, "kt", 1), (BACK, "n2", 0), (HEAD, "qt", 0), (BACK, "t2", 0),
              (HEAD, "qt", 1)]
    return order


ORDER = pass_order()
MAX_STEPS = [(s, t, j0, pairs) for s in range(2) for t, pairs in ((0, 4), (1, 2)) for j0 in range(0, H1 // 2, pairs)]


def decoder_kernel(nc, x, xT, ctxT, w1qkv, w1o, lam, w2q, w2k, b2, nw, w3q, w3k, w3v, w3o, gate,
                   e1, e3, e2, rope1, rope3, out, dbg=None):
    ctx = ExitStack()
    with ctx:
        def sb(name, shape, dt=F32):
            return ctx.enter_context(nc.sbuf_tensor(name, shape, dt))

        def room(*groups):
            tensors = []
            for group in groups[:-1]:
                with ExitStack() as turn:
                    tensors += [turn.enter_context(nc.sbuf_tensor(name, shape, *(dt or (F32,)))) for name, shape, *dt in group]
            return tensors + [sb(*t) for t in groups[-1]]

        def sem(name):
            return ctx.enter_context(nc.semaphore(name))

        psS = ctx.enter_context(nc.psum_tensor("psS", [P, 2, 1024], F32))
        psA = ctx.enter_context(nc.psum_tensor("psA", [P, 2, 512], F32))
        psK = ctx.enter_context(nc.psum_tensor("psK", [P, 2, 512], F32))

        ident = sb("ident", [P, P])
        identb = sb("identb", [P, P], BF16)
        maskb = sb("maskb", [P, P], BF16)
        maskTb = sb("maskTb", [P, P], BF16)
        neghalf = sb("neghalf", [P, TT])
        neg1 = sb("neg1", [P, 4])
        iota8 = sb("iota8", [P, E])
        wqkv1 = sb("wqkv1", [P, DT, 704])
        wo1 = sb("wo1", [P, DT, D])
        rope1s = sb("rope1s", [P, TT, 2, HD1])
        rope3s = sb("rope3s", [P, 2, T])
        lams = sb("lams", [P, 4, HD1])
        lamp = sb("lamp", [P, 2, HD1])
        lamd = sb("lamd", [P, 2])
        lame = sb("lame", [P, 2])
        fac = sb("fac", [P, 2, 2])
        wq2 = sb("wq2", [P, C2])
        wk2 = sb("wk2", [P, C2])
        b2s = sb("b2s", [P, 2])
        nws = sb("nws", [P, 2, DT])
        ew, el, eh, w3, wo3, QK3 = room(
            [("ew", [P, 2, 3072])],
            [("el", [P, 2, 3072], F32R), ("eh", [P, 2, 3072], F32R)],
            [("w3", [P, DT, (H3 + 2 * G3) * HD3]), ("wo3", [P, H3, D]), ("QK3", [P, G3 + H3, T])])
        wq3, wk3, wv3 = w3[:, :, 0:2048], w3[:, :, 2048:2560], w3[:, :, 2560:3072]
        gates = sb("gates", [P, DT, E])

        xTs = sb("xTs", [P, DT, T])
        xs = sb("xs", [P, TT, D])
        cTs = sb("cTs", [P, T])
        rt1 = sb("rt1", [P, 640])
        rt2 = sb("rt2", [P, 640])
        hib = sb("hib", [P, 640], BF16)
        midb = sb("midb", [P, 640], BF16)
        lob = sb("lob", [P, 640], BF16)
        acc, n2T, n2h, n2l, hTh, hTl, QT, KT, PT, qpack = room(
            [("acc", [P, NT, D]), ("n2T", [P, DT, NTOK]), ("n2h", [P, DT, NTOK], F32R), ("n2l", [P, DT, NTOK], F32R),
             ("hTh", [P, FT, NTOK], F32R), ("hTl", [P, FT, NTOK], F32R)],
            [("QT", [P, H1, T], BF16), ("KT", [P, 2 * G1, 2, T], BF16), ("PT", [P, PTN, 1024]), ("qpack", [P, TT, 2 * H1, SLOT], BF16)])
        kpack = sb("kpack", [P, 2 * G1, 2, SLOT], BF16)
        Vx = sb("Vx", [P, TT, G1, 32])
        negm = sb("negm", [P, TT, 2 * H1])
        mres = sb("mres", [P, TT, 2 * H1])
        OT = sb("OT", [P, 2, 512])
        rs1 = sb("rs1", [P, 2, 4, 4])
        on1 = sb("on1", [P, 2, 4, 4, HD1])
        att1 = sb("att1", [P, TT, D])
        tT = sb("tT", [P, DT, T])
        x1 = sb("x1", [P, TT, D])
        x2 = sb("x2", [P, TT, D])
        bst = sb("bst", [P, TT, 6])
        mv = sb("mv", [P, TT, 2])
        var = sb("var", [P, TT])
        rstd = sb("rstd", [P, TT])
        q2T = sb("q2T", [P, 2, T])
        att2 = sb("att2", [P, TT, T])
        idle_v = sb("idle_v", [P, 1])
        mx2 = sb("mx2", [P, TT])
        sm2 = sb("sm2", [P, TT])
        x2b = sb("x2b", [P, TT, D])
        xnb = sb("xnb", [P, TT, D])
        nT = sb("nT", [P, DT, T])
        hb = nT
        sqb = sb("sqb", [P, TT])
        varb = sb("varb", [P, TT])
        rstdb = sb("rstdb", [P, TT])
        V3 = sb("V3", [P, TT, G3 * HD3])
        ra = sb("ra", [P, 2, 2, T])
        rb = sb("rb", [P, 2, 2, T])
        mx3 = sb("mx3", [P, 2, 4])
        sm3 = sb("sm3", [P, 2, 4])
        rc3 = sb("rc3", [P, 2, 4])
        P3 = sb("P3", [P, 2, 2, 384])
        PT3 = sb("PT3", [P, 2, 384])
        O3 = QK3[:, G3:G3 + H3, :]

        n2T_dram = nc.dram_tensor("n2T_dram", (B, P, DT, T), F32, kind="Internal").ap()
        acc_dram = nc.dram_tensor("acc_dram", (B, P, TT, D), F32, kind="Internal").ap()
        lg = sb("lg", [P, NT, E])
        top = sb("top", [P, NT, 8])
        tix = sb("tix", [P, NT, 8], U32)
        tixf = sb("tixf", [P, NT, 8])
        pr = sb("pr", [P, 4, NT])
        wgt = sb("wgt", [P, NT, E])
        wgt2 = sb("wgt2", [P, NT, E])
        bstF = sb("bstF", [P, NT, 6])
        mvF = sb("mvF", [P, NT, 2])
        varF = sb("varF", [P, NT])
        nhF = sb("nhF", [P, NT])
        rstdF = sb("rstdF", [P, NT])

        def matrices(w):
            return (w[:, 0:1024].rearrange("p (k f) -> p k f", k=DT), w[:, 1024:2048].rearrange("p (k f) -> p k f", k=DT),
                    w[:, 2048:3072].rearrange("p (k f) -> p k f", k=FT))

        ehs, els = [matrices(eh[:, i, :]) for i in range(2)], [matrices(el[:, i, :]) for i in range(2)]
        sil = ra[:, :, :, :].rearrange("p c a t -> p c (a t)")
        hid = rb[:, :, :, :].rearrange("p c a t -> p c (a t)")

        ld_w1 = sem("ld_w1")
        ld_w1o = sem("ld_w1o")
        ld_w2 = sem("ld_w2")
        ld_w3v = sem("ld_w3v")
        ld_w3k = sem("ld_w3k")
        ld_w3q = sem("ld_w3q")
        ld_w3o = sem("ld_w3o")
        ld_gate = sem("ld_gate")
        ld_small = sem("ld_small")
        ld_xT = sem("ld_xT")
        ld_x = sem("ld_x")
        ld_c = sem("ld_c")
        ld_e = [sem(f"ld_e{i}") for i in range(2)]
        consts_made = sem("consts_made")
        S = Ring([sem(f"S_filled{i}") for i in range(2)], [sem(f"S_emptied{i}") for i in range(2)], S_USES)
        A = Ring([sem(f"A_filled{i}") for i in range(2)], [sem(f"A_emptied{i}") for i in range(2)], len(A_NAMES))
        K = Ring([sem(f"K_filled{i}") for i in range(2)], [sem(f"K_emptied{i}") for i in range(2)], len(K_NAMES))
        vec_step = sem("vec_step")
        pool_step = sem("pool_step")
        roped1 = sem("roped1")
        summed1 = sem("summed1")
        high1 = sem("high1")
        rest1 = sem("rest1")
        mid1 = sem("mid1")
        low1 = sem("low1")
        packed1 = sem("packed1")
        maxed1 = sem("maxed1")
        attn1 = sem("attn1")
        var_ready = sem("var_ready")
        rstd_ready = sem("rstd_ready")
        x1_ready = sem("x1_ready")
        x2_ready = sem("x2_ready")
        x2_read = sem("x2_read")
        att2_max = sem("att2_max")
        att2_ready = sem("att2_ready")
        xn_ready = sem("xn_ready")
        varb_ready = sem("varb_ready")
        rstdb_ready = sem("rstdb_ready")
        acc_ready = sem("acc_ready")
        spilled = sem("spilled")
        ld_acc = sem("ld_acc")
        ld_n2T = sem("ld_n2T")
        swapped3 = sem("swapped3")
        sined3 = sem("sined3")
        summed3 = sem("summed3")
        max3 = sem("max3")
        rec3 = sem("rec3")
        norm3 = sem("norm3")
        lam_dots = sem("lam_dots")
        lam_exp = sem("lam_exp")
        lg_filled = sem("lg_filled")
        top_diff = sem("top_diff")
        top_exp = sem("top_exp")
        U_filled = [sem(f"U_filled{i}") for i in range(2)]
        U_read = [sem(f"U_read{i}") for i in range(2)]
        W_filled = [sem(f"W_filled{i}") for i in range(2)]
        hid_ready = [sem(f"hid_ready{i}") for i in range(2)]
        hid_high = [sem(f"hid_high{i}") for i in range(2)]
        h_ready = [sem(f"h_ready{i}") for i in range(2)]
        w_high = sem("w_high")
        w_split = sem("w_split")
        n2_high = sem("n2_high")
        n2_split = sem("n2_split")
        Y_filled = [sem(f"Y_filled{i}") for i in range(2)]
        Y_added = [sem(f"Y_added{i}") for i in range(2)]
        fin_var = sem("fin_var")
        fin_rstd = sem("fin_rstd")
        fin_ready = sem("fin_ready")
        stored = sem("stored")

        psT = psS[:, :, :].bitcast(BF16)
        block = ctx.enter_context(nc.Block())

        @block.sync
        def _(sp):
            sp.dma_start(wqkv1[:], w1qkv.rearrange("(k p) n -> p k n", p=P)).then_inc(ld_w1, 16)
            sp.dma_start(rope1s[:], rope1.rearrange("(t p) c d -> p t c d", p=P)).then_inc(ld_w1, 16)

            def load_xT(b):
                sp.dma_start(xTs[:], xT[bass.ds(b, 1), :, :].rearrange("o (k p) t -> p (o k) t", p=P)).then_inc(ld_xT, 16)

            def load_ctx(b):
                sp.dma_start(cTs[:], ctxT[bass.ds(b, 1), :, :].rearrange("o p t -> p (o t)")).then_inc(ld_c, 16)

            def load_x(b):
                sp.dma_start(xs[:], x[bass.ds(b, 1), :, :].rearrange("o (k p) d -> p (o k) d", p=P)).then_inc(ld_x, 16)

            def load_next(b):
                for t in range(TT):
                    S.wait_emptied(sp, b - 1, S_PROJ + t)
                load_xT(b)
                A.wait_emptied(sp, b - 1, A_USE["k2"])
                load_ctx(b)
                A.wait_emptied(sp, b - 1, A_USE["wo1"])
                load_x(b)

            def spill(b):
                sp.wait_ge(acc_ready, b + 1)
                sp.dma_start(acc_dram[bass.ds(b, 1), :, :, :].rearrange("o p t d -> p (o t) d"), x2b[:]).then_inc(spilled, 16)
                K.wait_emptied(sp, b, K_USE["turn_n2"])
                sp.dma_start(n2T_dram[bass.ds(b, 1), :, :, :].rearrange("o p k t -> p (o k) t"), nT[:]).then_inc(spilled, 16)

            load_xT(0)
            load_ctx(0)
            sp.dma_start(wq2[:], w2q).then_inc(ld_w2, 16)
            sp.dma_start(wk2[:], w2k).then_inc(ld_w2, 16)
            sp.dma_start(b2s[:], b2).then_inc(ld_w2, 16)
            sp.dma_start(nws[:], nw).then_inc(ld_small, 16)
            sp.dma_start(lams[:], lam.partition_broadcast(P)).then_inc(ld_small, 16)
            load_x(0)
            sp.dma_start(wo1[:], w1o.rearrange("(k p) n -> p k n", p=P)).then_inc(ld_w1o, 16)
            sp.dma_start(rope3s[:], rope3).then_inc(ld_w3v, 16)
            sp.dma_start(wv3, w3v.rearrange("(k p) n -> p k n", p=P)).then_inc(ld_w3v, 16)
            sp.dma_start(wk3, w3k.rearrange("(k p) n -> p k n", p=P)).then_inc(ld_w3k, 16)
            sp.dma_start(wq3, w3q.rearrange("(k p) n -> p k n", p=P)).then_inc(ld_w3q, 16)
            sp.dma_start(wo3[:], w3o.rearrange("(k p) n -> p k n", p=P)).then_inc(ld_w3o, 16)
            sp.dma_start(gates[:], gate.rearrange("(k p) n -> p k n", p=P)).then_inc(ld_gate, 16)
            load_next(1)
            with sp.Fori(0, B - 2) as b:
                load_next(b + 2)
                spill(b)
            spill(B - 2)

            def load_expert(e, i):
                for w, lo, k in ((e1, 0, DT), (e3, 1024, DT), (e2, 2048, FT)):
                    sp.dma_start(ew[:, i, lo:lo + 1024].rearrange("p (k f) -> p k f", k=k),
                                 w[bass.ds(e, 1), :, :].rearrange("o (k p) f -> p (o k) f", p=P)).then_inc(ld_e[i], 16)

            A.wait_emptied(sp, B - 1, A_USE["x_m"])
            sp.wait_ge(spilled, 1 + 32 * (B - 1))
            for b in range(B - 1):
                sp.dma_start(n2T[:, :, b * T:(b + 1) * T], n2T_dram[b, :, :, :]).then_inc(ld_n2T, 16)
                sp.dma_start(acc[:, b * TT:(b + 1) * TT, :], acc_dram[b, :, :, :]).then_inc(ld_acc, 16)
            for c in (8, 9):
                K.wait_emptied(sp, B - 1, K_USE["p3", c])
            load_expert(0, 0)
            load_expert(1, 1)
            with sp.Fori(1, E // 2) as ep:
                for i in range(2):
                    sp.wait_ge(Y_filled[1], ep * NT + (i - 1) * NT // 2)
                    load_expert(ep * 2 + i, i)
            for t in range(NT):
                sp.wait_ge(fin_ready, t + 1)
                sp.dma_start(out.rearrange("b (t p) d -> p (b t) d", p=P)[:, t, :], acc[:, t, :]).then_inc(stored, 16)
            sp.wait_ge(stored, 16 * NT)

        @block.tensor
        def _(pe):
            mm = pe.matmul

            def project1(b):
                pe.wait_ge(ld_xT, b * 16 + 16)
                for t in range(TT):
                    S.wait_empty(pe, b, S_PROJ + t)
                    for lo, n in ((0, 512), (512, 192)):
                        for k in range(DT):
                            last = mm(psS[:, t, lo:lo + n], xTs[:, k, t * P:(t + 1) * P], wqkv1[:, k, lo:lo + n],
                                      start=(k == 0), stop=(k == DT - 1))
                    last.then_inc(S.filled[t], 1)

            def queries2(b):
                pe.wait_ge(ld_c, b * 16 + 16)
                for name, w in (("q2", wq2), ("k2", wk2)):
                    u = A_USE[name]
                    A.wait_empty(pe, b, u)
                    mm(psA[:, u % 2, 0:T], w[:], cTs[:], start=True, stop=True).then_inc(A.filled[u % 2], 1)

            def energy2(b):
                u = A_USE["energy"]
                A.wait_emptied(pe, b, A_USE["q2"])
                A.wait_emptied(pe, b, A_USE["k2"])
                for n in range(TT):
                    last = mm(psA[:, u % 2, n * T:(n + 1) * T], q2T[:, 0, n * P:(n + 1) * P], q2T[:, 1, :], start=True, stop=True)
                last.then_inc(A.filled[u % 2], 1)

            def turn(b, u, src):
                S.wait_empty(pe, b, u)
                for j in range(16):
                    last = pe.transpose(psT[:, u % 2, j * P:(j + 1) * P], src(j), identb[:])
                last.then_inc(S.filled[u % 2], 1)

            def turn_k(b, t):
                pe.wait_ge(packed1, b * TT + t + 1)
                turn(b, S_KT + t, lambda j: kpack[:, j, :, :].rearrange("p a c -> p (a c)"))

            def turn_q(b, u0, t):
                for s in range(2):
                    turn(b, u0 + 2 * t + s, lambda j: qpack[:, t, 32 * s + 2 * j:32 * s + 2 * j + 2, :].rearrange("p a c -> p (a c)"))

            def max_scores(b, n):
                if n == 0:
                    for u in (S_MAX - 2, S_MAX - 1):
                        S.wait_emptied(pe, b, u)
                u = S_MAX + n
                s, t, j0, pairs = MAX_STEPS[n]
                keys = P * (t + 1)
                S.wait_empty(pe, b, u)
                for j in range(j0, j0 + pairs):
                    w = 2 * keys
                    o = psS[:, u % 2, (j - j0) * w:(j - j0 + 1) * w].rearrange("p (a k) -> p a k", a=2)
                    g = (j * 2) // REP1
                    mm(o, QT[:, s * 16 + j, t * P:(t + 1) * P], KT[:, s * G1 + g, :, 0:keys],
                       start=(j - j0) * w % 512 == 0, stop=True, skip_group_check=True)
                    last = mm(o[:, :, keys - P:keys], identb[:], maskb[:].unsqueeze(1).broadcast_to([P, 2, P]),
                              start=False, stop=True, skip_group_check=True)
                last.then_inc(S.filled[u % 2], 1)

            mask2 = maskTb[:].unsqueeze(1).broadcast_to([P, 2, P])

            def scoresT(b, g):
                if g == 0:
                    for u in (S_QT2 + 2, S_QT2 + 3):
                        S.wait_emptied(pe, b, u)
                u = S_EXP + 3 * g
                for s in range(2):
                    S.wait_empty(pe, b, u + s)
                    for a in range(2):
                        o = psS[:, (u + s) % 2, a * 512:(a + 1) * 512].rearrange("p (j q) -> p j q", q=T)
                        mm(o, KT[:, s * G1 + g, a, 0:P], QT[:, s * 16 + 2 * g:s * 16 + 2 * g + 2, :], start=True, stop=True)
                        last = mm(o[:, :, 0:P], identb[:], mask2, start=False, stop=True, skip_group_check=True)
                    last.then_inc(S.filled[(u + s) % 2], 1)

            def scoresT_second(b, g):
                u = S_EXP + 3 * g + 2
                S.wait_empty(pe, b, u)
                for s in range(2):
                    for a in range(2):
                        o = psS[:, u % 2, s * 512 + a * T:s * 512 + (a + 1) * T]
                        mm(o, KT[:, s * G1 + g, a, P:T], QT[:, s * 16 + 2 * g:s * 16 + 2 * g + 2, P:T], start=True, stop=False)
                        last = mm(o, identb[:], mask2, start=False, stop=True)
                last.then_inc(S.filled[u % 2], 1)

            def values1(b, g):
                u = A_USE["pv", g]
                o = psA[:, u % 2, :]
                A.wait_empty(pe, b, u)
                for c in (1, 2):
                    S.wait_emptied(pe, b, S_EXP + 3 * g + c)
                for j in range(4):
                    s, a = j // 2, j % 2
                    mm(o[32 * j:32 * j + 32, :], Vx[:, 0, g, :], PT[:, (3 * g + s) % PTN, a * 512:(a + 1) * 512], start=True, stop=True)
                for j in range(4):
                    s, a = j // 2, j % 2
                    last = mm(o[32 * j:32 * j + 32, :].rearrange("p (j q) -> p j q", j=2)[:, :, P:T], Vx[:, 1, g, :],
                              PT[:, (3 * g + 2) % PTN, s * 512 + a * T:s * 512 + (a + 1) * T].rearrange("p (j q) -> p j q", j=2),
                              start=False, stop=True, skip_group_check=True)
                last.then_inc(A.filled[u % 2], 1)

            def turn_o(b, g):
                u = A_USE["turn_o", g]
                A.wait_emptied(pe, b, A_USE["pv", g])
                A.wait_empty(pe, b, u)
                for j in range(4):
                    last = pe.transpose(psA[:, u % 2, j * P:(j + 1) * P], OT[:, g % 2, j * P:(j + 1) * P], ident[:])
                last.then_inc(A.filled[u % 2], 1)

            def turn4(ring, ps, b, u, src):
                ring.wait_empty(pe, b, u)
                for k in range(DT):
                    for t in range(TT):
                        last = pe.transpose(ps[:, u % 2, k * T + t * P:k * T + (t + 1) * P], src[:, t, k * P:(k + 1) * P], ident[:])
                last.then_inc(ring.filled[u % 2], 1)

            def rows(b, u, rhs):
                A.wait_empty(pe, b, u)
                for t in range(TT):
                    for k in range(DT):
                        last = mm(psA[:, u % 2, t * D:(t + 1) * D], tT[:, k, t * P:(t + 1) * P], rhs[:, k, :],
                                  start=(k == 0), stop=(k == DT - 1))
                last.then_inc(A.filled[u % 2], 1)

            def front(b, step, n):
                if step == "proj":
                    project1(b)
                elif step == "ctx":
                    queries2(b)
                elif step == "energy":
                    energy2(b)
                elif step == "kt":
                    turn_k(b, n)
                elif step == "qt":
                    turn_q(b, S_QT, n)
                elif step == "max":
                    max_scores(b, n)
                elif step == "qt2":
                    pe.wait_ge(maxed1, b + 1)
                    turn_q(b, S_QT2, n)
                elif step == "sTa":
                    scoresT(b, n)
                elif step == "sTb":
                    scoresT_second(b, n)
                elif step == "pv":
                    values1(b, n)
                elif step == "ot":
                    turn_o(b, n)
                elif step == "at":
                    pe.wait_ge(attn1, b + 1)
                    turn4(A, psA, b, A_USE["turn_att1"], att1)
                elif step == "wo":
                    A.wait_emptied(pe, b, A_USE["turn_att1"])
                    rows(b, A_USE["wo1"], wo1)
                elif step == "a2t":
                    pe.wait_ge(att2_ready, b + 1)
                    turn4(A, psA, b, A_USE["turn_att2"], att2)
                elif step == "x1t":
                    pe.wait_ge(x1_ready, b + 1)
                    turn4(A, psA, b, A_USE["turn_x1"], x1)
                elif step == "xm":
                    A.wait_emptied(pe, b, A_USE["turn_att2"])
                    A.wait_emptied(pe, b, A_USE["turn_x1"])
                    rows(b, A_USE["x_m"], q2T)

            def values3_project(b, t):
                u = K_USE["v3", t]
                K.wait_emptied(pe, b, K_USE["turn_n1"])
                K.wait_empty(pe, b, u)
                for k in range(DT):
                    last = mm(psK[:, u % 2, :], nT[:, k, t * P:(t + 1) * P], wv3[:, k, :], start=(k == 0), stop=(k == DT - 1))
                last.then_inc(K.filled[u % 2], 1)

            def heads3_project(b, c):
                u = K_USE["p3", c]
                K.wait_empty(pe, b, u)
                for a in range(2):
                    h = 2 * c + a
                    w, n = (wk3, h) if h < G3 else (wq3, h - G3)
                    for k in range(DT):
                        last = mm(psK[:, u % 2, a * T:(a + 1) * T], w[:, k, n * P:(n + 1) * P], nT[:, k, :],
                                  start=(k == 0), stop=(k == DT - 1))
                last.then_inc(K.filled[u % 2], 1)

            def scores3(b, c):
                pe.wait_ge(summed3, b * 10 + 4 + c)
                for a in range(2):
                    h = 2 * c + a
                    u = K_USE["s3", h]
                    K.wait_empty(pe, b, u)
                    q, k = QK3[:, G3 + h, :], QK3[:, h // REP3, :]
                    o = psK[:, u % 2, 0:384]
                    mm(o[:, 0:P], q[:, 0:P], k[:, 0:P], start=True, stop=False)
                    mm(o[:, 0:P], identb[:], maskb[:], start=False, stop=True)
                    mm(o[:, P:384], q[:, P:T], k[:, :], start=True, stop=True)
                    mm(o[:, T:384], identb[:], maskb[:], start=False, stop=True, skip_group_check=True).then_inc(K.filled[u % 2], 1)

            def turn_p(b, c):
                pe.wait_ge(norm3, b * 8 + c + 1)
                for a in range(2):
                    u = K_USE["turn_p", 2 * c + a]
                    K.wait_empty(pe, b, u)
                    src = P3[:, c % 2, a, :]
                    for lo in (0, P, T):
                        last = pe.transpose(psK[:, u % 2, lo:lo + P], src[:, lo:lo + P], ident[:])
                    last.then_inc(K.filled[u % 2], 1)

            def values3(b, c):
                u = K_USE["pv3", c]
                for a in range(2):
                    K.wait_emptied(pe, b, K_USE["turn_p", 2 * c + a])
                K.wait_empty(pe, b, u)
                for a in range(2):
                    g = (2 * c + a) // REP3
                    o = psK[:, u % 2, a * T:(a + 1) * T]
                    mm(o, V3[:, 0, g * P:(g + 1) * P], PT3[:, a, 0:T], start=True, stop=True)
                    last = mm(o[:, P:T], V3[:, 1, g * P:(g + 1) * P], PT3[:, a, T:384], start=False, stop=True,
                              skip_group_check=True)
                last.then_inc(K.filled[u % 2], 1)

            def out3(b, n):
                t, half = n // 2, n % 2
                if n == 0:
                    for c in (H3 // 2 - 2, H3 // 2 - 1):
                        K.wait_emptied(pe, b, K_USE["pv3", c])
                u = K_USE["wo3", t]
                if half == 0:
                    K.wait_empty(pe, b, u)
                for h in range(half * H3 // 2, (half + 1) * H3 // 2):
                    last = mm(psK[:, u % 2, 0:D], O3[:, h, t * P:(t + 1) * P], wo3[:, h, :],
                              start=(h == 0), stop=(h == H3 - 1))
                if half:
                    last.then_inc(K.filled[u % 2], 1)

            def back(b, step, n):
                if step == "t1":
                    pe.wait_ge(xn_ready, 2 * b + 1)
                    turn4(K, psK, b, K_USE["turn_n1"], xnb)
                elif step == "v3":
                    values3_project(b, n)
                elif step == "p3":
                    heads3_project(b, n)
                elif step == "s3":
                    scores3(b, n)
                elif step == "pt3":
                    turn_p(b, n)
                elif step == "pv3":
                    values3(b, n)
                elif step == "wo3":
                    out3(b, n)
                elif step == "t2":
                    pe.wait_ge(xn_ready, 2 * b + 2)
                    turn4(K, psK, b, K_USE["turn_n2"], xnb)

            def one_pass(b, order):
                for which, step, n in order:
                    if which == BACK:
                        back(b, step, n)
                    else:
                        front(b + 1 + which, step, n)

            pe.wait_ge(consts_made, 1)
            pe.wait_ge(ld_w1, 32)
            pe.wait_ge(ld_w2, 48)
            for which, step, n in [(0, *x[1:]) for x in ORDER if x[0] == HEAD] + [x for x in ORDER if x[0] != BACK]:
                if step == "wo":
                    pe.wait_ge(ld_w1o, 16)
                front(which, step, n)
            for weights, count in ((ld_w3v, 32), (ld_w3k, 16), (ld_w3q, 16), (ld_w3o, 16)):
                pe.wait_ge(weights, count)
            with pe.Fori(0, B - 2) as b:
                one_pass(b, ORDER)
            one_pass(B - 2, [x for x in ORDER if x[0] != HEAD])
            one_pass(B - 1, [x for x in ORDER if x[0] == BACK])

            pe.wait_ge(ld_n2T, 16 * (B - 1))
            pe.wait_ge(ld_gate, 16)
            for u in (len(K_NAMES) - 2, len(K_NAMES) - 1):
                K.wait_emptied(pe, B - 1, u)
            for t in range(NT):
                for k in range(DT):
                    last = mm(psK[:, 0, t * E:(t + 1) * E], n2T[:, k, t * P:(t + 1) * P], gates[:, k, :],
                              start=(k == 0), stop=(k == DT - 1))
            last.then_inc(lg_filled, 1)

            def product3(o, pairs):
                for n, (lh, ll, rh, rl) in enumerate(pairs):
                    mm(o, lh, rl, start=(n == 0), stop=False)
                    mm(o, ll, rh, start=False, stop=False)
                    last = mm(o, lh, rh, start=False, stop=(n == len(pairs) - 1))
                return last

            pe.wait_ge(n2_split, 2)
            with pe.Fori(0, E // 2) as ep:
                for i in range(2):
                    pe.wait_ge(w_split, ep * 2 + i + 1)
                    for f in range(FT):
                        for c in range(2):
                            pe.wait_ge(U_read[c], ep * 8 + 4 * i + f + 1)
                            pe.wait_ge(hid_ready[c], ep * 8 + 4 * i + f + 1)
                            for w, half, filled in ((0, slice(0, 512), U_filled), (1, slice(512, 1024), W_filled)):
                                product3(psS[:, c, half],
                                         [(ehs[i][w][:, k, f * P:(f + 1) * P], els[i][w][:, k, f * P:(f + 1) * P],
                                           n2h[:, k, c * 512:(c + 1) * 512], n2l[:, k, c * 512:(c + 1) * 512]) for k in range(DT)])\
                                    .then_inc(filled[c], 1)
                    for t in range(NT):
                        c = t // 4
                        pe.wait_ge(h_ready[c], ep * 8 + 4 * i + 5)
                        pe.wait_ge(Y_added[t % 2], ep * 8 + 4 * i + t // 2 + 1)
                        product3(psA[:, t % 2, 0:D],
                                 [(hTh[:, f, t * P:(t + 1) * P], hTl[:, f, t * P:(t + 1) * P],
                                   ehs[i][2][:, f, :], els[i][2][:, f, :]) for f in range(FT)]).then_inc(Y_filled[t % 2], 1)

        @block.vector
        def _(dve):
            v = nc.vector
            n_ = [0]
            base = [0]

            def link(ins):
                ins.then_inc(vec_step, 1)
                n_[0] += 1
                dve.wait_ge(vec_step, base[0] + n_[0])

            def rope1_products(b, t):
                if t:
                    dve.wait_ge(low1, b * TT + t)
                S.wait_filled(dve, b, S_PROJ + t)
                qk = psS[:, t, 0:640].rearrange("p (h d) -> p h d", d=HD1)
                c, s = rope1s[:, t, 0, :], rope1s[:, t, 1, :]
                v.tensor_tensor(rt1[:].rearrange("p (h d) -> p h d", d=HD1), qk, c.unsqueeze(1).broadcast_to([P, 80, HD1]), ALU.mult)
                r = rt2[:].rearrange("p (h d) -> p h d", d=HD1)
                v.tensor_tensor(r[:, :, 0:4], qk[:, :, 4:8], s[:, 0:4].unsqueeze(1).broadcast_to([P, 80, 4]), ALU.mult)
                v.tensor_tensor(r[:, :, 4:8], qk[:, :, 0:4], s[:, 4:8].unsqueeze(1).broadcast_to([P, 80, 4]),
                                ALU.mult).then_inc(roped1, 1)
                v.tensor_copy(Vx[:, t, :, 0:HD1], psS[:, t, 640:704].rearrange("p (g d) -> p g d", d=HD1)).then_inc(S.emptied[t], 1)

            def pack(b, t):
                v.memset(qpack[:, t, :, 48:51], 0.0)
                if t:
                    S.wait_filled(dve, b, S_KT)
                for parts, src, done in (((0, 3), hib, high1), ((3, 2), midb, mid1), ((5, 1), lob, low1)):
                    dve.wait_ge(done, b * TT + t + 1)
                    lo, k = parts
                    v.tensor_copy(qpack[:, t, :, lo * 8:(lo + k) * 8].rearrange("p h (c d) -> p h c d", c=k),
                                  src[:, 0:512].rearrange("p (h d) -> p h d", d=HD1).unsqueeze(2).broadcast_to([P, 64, k, HD1]))
                for a in range(2):
                    for slots, src in (((0, 3, 5), hib), ((1, 4), midb), ((2,), lob)):
                        for sl in slots:
                            last = v.tensor_copy(kpack[:, :, a, sl * 8:sl * 8 + 8],
                                                 src[:, 512:640].rearrange("p (h d) -> p h d", d=HD1))
                last.then_inc(packed1, 1)

            def evac_k(b, t):
                u = S_KT + t
                S.wait_filled(dve, b, u)
                src = psT[:, u % 2, :].rearrange("p (j q) -> p j q", q=P)
                v.tensor_copy(KT[0:64, :, 0, t * P:(t + 1) * P], src[0:64])
                v.tensor_copy(KT[64:128, :, 1, t * P:(t + 1) * P], src[64:128]).then_inc(S.emptied[u % 2], 1)

            def evac_q(b, u0, t):
                u = u0 + 2 * t
                S.wait_filled(dve, b, u)
                v.tensor_copy(QT[:, 0:16, t * P:(t + 1) * P],
                              psT[:, u % 2, :].rearrange("p (j q) -> p j q", q=P)).then_inc(S.emptied[u % 2], 1)

            def maxima1(b, n):
                u = S_MAX + n
                s, t, j0, pairs = MAX_STEPS[n]
                S.wait_filled(dve, b, u)
                v.tensor_reduce(negm[:, t, s * H1 + 2 * j0:s * H1 + 2 * (j0 + pairs)],
                                psS[:, u % 2, :].rearrange("p (h k) -> p h k", h=2 * pairs),
                                AX.X, ALU.max, negate=True).then_inc(S.emptied[u % 2], 1)

            def pack_maxima(b):
                S.wait_emptied(dve, b, S_MAX + 23)
                q = [qpack[:, :, :, 48 + i] for i in range(3)]
                link(v.tensor_copy(q[0], negm[:]))
                link(v.tensor_tensor(mres[:], negm[:], q[0], ALU.subtract))
                link(v.tensor_copy(q[1], mres[:]))
                link(v.tensor_tensor(mres[:], mres[:], q[1], ALU.subtract))
                v.tensor_copy(q[2], mres[:]).then_inc(maxed1, 1)

            def qk2_evacuate(b):
                for i, name in enumerate(("q2", "k2")):
                    u = A_USE[name]
                    A.wait_filled(dve, b, u)
                    v.tensor_scalar(q2T[:, i, :], psA[:, u % 2, 0:T], b2s[:, i:i + 1], None, ALU.add).then_inc(A.emptied[u % 2], 1)

            def energy_max(b):
                u = A_USE["energy"]
                A.wait_filled(dve, b, u)
                v.tensor_reduce(mx2[:], psA[:, u % 2, :].rearrange("p (n m) -> p n m", n=TT), AX.X, ALU.max, negate=True)\
                    .then_inc(att2_max, 1)

            def att2_normalise(b):
                A.wait_emptied(dve, b, A_USE["energy"])
                link(v.reciprocal(sm2[:], sm2[:]))
                v.tensor_tensor(att2[:], att2[:], sm2[:].unsqueeze(2).broadcast_to([P, TT, T]), ALU.mult).then_inc(att2_ready, 1)

            def normalise1(b, g):
                u = A_USE["turn_o", g]
                A.wait_filled(dve, b, u)
                o = psA[:, u % 2, :].rearrange("p (j a c) -> p j a c", j=4, a=4)
                i = g % 2
                link(v.reciprocal(rs1[:, i], o[:, :, :, HD1]))
                link(v.tensor_tensor(rs1[:, i], rs1[:, i], fac[:].rearrange("p s a -> p (s a)").unsqueeze(1).broadcast_to([P, 4, 4]),
                                     ALU.mult))
                v.tensor_tensor(on1[:, i], o[:, :, :, 0:HD1], rs1[:, i].unsqueeze(3).broadcast_to([P, 4, 4, HD1]),
                                ALU.mult).then_inc(A.emptied[u % 2], 1)
                A.wait_emptied(dve, b, u)
                s1 = on1[:, i].rearrange("p (j t) (s a) d -> p s j t (a d)", t=TT, s=2)
                for t in range(TT):
                    last = v.tensor_tensor(att1[:, t, g * 32:(g + 1) * 32].rearrange("p (j c) -> p j c", j=2),
                                           s1[:, 0, :, t, :], s1[:, 1, :, t, :], ALU.subtract)
                if g == G1 - 1:
                    last.then_inc(attn1, 1)

            def evac4(b, name, dst):
                u = A_USE[name]
                A.wait_filled(dve, b, u)
                v.tensor_copy(dst[:].rearrange("p k t -> p (k t)"), psA[:, u % 2, :]).then_inc(A.emptied[u % 2], 1)

            def layer_norm(b, name, res, dst, nth):
                u = A_USE[name]
                A.wait_filled(dve, b, u)
                v.tensor_tensor(dst[:], psA[:, u % 2, :].rearrange("p (t d) -> p t d", t=TT), res[:], ALU.add)\
                    .then_inc(A.emptied[u % 2], 1)
                A.wait_emptied(dve, b, u)
                for t in range(TT):
                    ins = v.bn_stats(bst[:, t, :], dst[:, t, :])
                link(ins)
                v.memset(idle_v[:], 0.0)
                for t in range(TT):
                    ins = v.bn_aggr(mv[:, t, :], bst[:, t, :])
                link(ins)
                v.tensor_scalar(var[:], mv[:, :, 1], EPS, None, ALU.add).then_inc(var_ready, 1)
                dve.wait_ge(rstd_ready, b * 2 + nth + 1)
                for t in range(TT):
                    last = v.tensor_scalar(dst[:, t, :], dst[:, t, :], mv[:, t, 0:1], rstd[:, t:t + 1], ALU.subtract, ALU.mult)
                last.then_inc((x1_ready, x2_ready)[nth], 1)

            def front(b, step, n):
                if step == "proj":
                    rope1_products(b, 0)
                elif step == "ctx":
                    qk2_evacuate(b)
                elif step == "energy":
                    energy_max(b)
                elif step == "pack":
                    pack(b, n)
                    if n == 0:
                        rope1_products(b, 1)
                elif step == "kt":
                    evac_k(b, n)
                elif step == "qt":
                    evac_q(b, S_QT, n)
                elif step == "max":
                    maxima1(b, n)
                elif step == "packmax":
                    pack_maxima(b)
                elif step == "att2":
                    att2_normalise(b)
                elif step == "qt2":
                    evac_q(b, S_QT2, n)
                elif step == "ot":
                    normalise1(b, n)
                elif step == "at":
                    evac4(b, "turn_att1", tT)
                elif step == "wo":
                    dve.wait_ge(ld_x, b * 16 + 16)
                    layer_norm(b, "wo1", xs, x1, 0)
                elif step == "a2t":
                    evac4(b, "turn_att2", q2T)
                elif step == "x1t":
                    evac4(b, "turn_x1", tT)
                elif step == "xm":
                    dve.wait_ge(x2_read, b + 1)
                    layer_norm(b, "x_m", x1, x2, 1)

            def rms_norm(b, src, nth):
                for t in range(TT):
                    ins = v.tensor_tensor_reduce(xnb[:, t, :], src[:, t, :], src[:, t, :], 1.0, 0.0, ALU.mult, ALU.add,
                                                 sqb[:, t:t + 1])
                link(ins)
                v.tensor_scalar(varb[:], sqb[:], 1.0 / D, EPS, ALU.mult, ALU.add).then_inc(varb_ready, 1)

            def rms_scale(b, src, nth):
                dve.wait_ge(rstdb_ready, b * 2 + nth + 1)
                for t in range(TT):
                    last = v.tensor_scalar(xnb[:, t, :], src[:, t, :], rstdb[:, t:t + 1], None, ALU.mult)
                last.then_inc(xn_ready, 1)

            def turned_scaled(b, name, w, dst):
                u = K_USE[name]
                K.wait_filled(dve, b, u)
                for k in range(DT):
                    last = v.tensor_scalar(dst[:, k, :], psK[:, u % 2, k * T:(k + 1) * T], nws[:, w, k:k + 1], None, ALU.mult)
                last.then_inc(K.emptied[u % 2], 1)

            def rope3_products(b, c):
                u, i = K_USE["p3", c], c % 2
                K.wait_filled(dve, b, u)
                if c >= 2:
                    dve.wait_ge(summed3, b * 10 + c)
                dve.wait_ge(swapped3, b * 10 + c + 1)
                v.tensor_tensor(ra[:, i], psK[:, u % 2, :].rearrange("p (a t) -> p a t", a=2),
                                rope3s[:, 0, :].unsqueeze(1).broadcast_to([P, 2, T]), ALU.mult).then_inc(K.emptied[u % 2], 1)

            def maxima3(b, c):
                for a in range(2):
                    K.wait_filled(dve, b, K_USE["s3", 2 * c + a])
                v.tensor_reduce(mx3[:, c % 2, 0:2], psK[:, :, 0:P], AX.X, ALU.max, negate=True)
                v.tensor_reduce(mx3[:, c % 2, 2:4], psK[:, :, P:384], AX.X, ALU.max, negate=True).then_inc(max3, 1)

            def back(b, step, n, final=None):
                if step == "n1":
                    dve.wait_ge(x2_ready, b + 1)
                    dve.wait_ge(spilled, b * 32 + 1)
                    v.tensor_copy(x2b[:], x2[:]).then_inc(x2_read, 1)
                    dve.wait_ge(x2_read, b + 2)
                    rms_norm(b, x2b, 0)
                elif step == "n1 scale":
                    rms_scale(b, x2b, 0)
                elif step == "t1":
                    turned_scaled(b, "turn_n1", 0, nT)
                elif step == "p3":
                    rope3_products(b, n)
                elif step == "s3":
                    maxima3(b, n)
                elif step == "wo3" and n % 2:
                    u = K_USE["wo3", n // 2]
                    K.wait_filled(dve, b, u)
                    v.tensor_tensor(hb[:, n // 2, :], psK[:, u % 2, 0:D], x2b[:, n // 2, :], ALU.add).then_inc(K.emptied[u % 2], 1)
                elif step == "n2":
                    for t in range(TT):
                        K.wait_emptied(dve, b, K_USE["wo3", t])
                    rms_norm(b, hb, 1)
                    v.tensor_tensor(x2b[:] if final is None else acc[:, final * TT:(final + 1) * TT, :], hb[:], x2b[:], ALU.add)\
                        .then_inc(acc_ready, 1)
                    rms_scale(b, hb, 1)
                elif step == "t2":
                    turned_scaled(b, "turn_n2", 1, nT if final is None else n2T[:, :, final * T:(final + 1) * T])

            def one_pass(b, order):
                for which, step, n in order:
                    if which == BACK:
                        back(b, step, n)
                    else:
                        front(b + 1 + which, step, n)

            for start in (*S.emptied, *A.emptied, *K.emptied, *U_read, *hid_ready, *h_ready, *Y_added, summed3, x2_read, spilled):
                dve.sem_inc(start, 1)
            v.memset(KT[:], 0.0)
            v.memset(qpack[:], 0.0)
            v.memset(kpack[:], 0.0)
            v.memset(Vx[:], 0.0)
            dve.wait_ge(ld_small, 32)
            link(v.tensor_tensor(lamp[:], lams[:, 0:4:2, :], lams[:, 1:4:2, :], ALU.mult))
            v.memset(kpack[:, :, :, 48:51], 1.0)
            v.memset(Vx[:, :, :, HD1:HD1 + 1], 1.0)
            v.tensor_reduce(lamd[:], lamp[:], AX.X, ALU.add).then_inc(lam_dots, 1)
            dve.wait_ge(lam_exp, 1)
            link(v.tensor_tensor(lamd[:, 0:1], lame[:, 0:1], lame[:, 1:2], ALU.subtract))
            v.memset(fac[:, 0, :], 1.0 - LAMBDA_INIT)
            for a in range(2):
                ins = v.tensor_scalar(fac[:, 1, a:a + 1], lamd[:, 0:1], LAMBDA_INIT, 1.0 - LAMBDA_INIT, ALU.add, ALU.mult)
            link(ins)
            dve.wait_ge(ld_w1, 32)
            dve.wait_ge(ld_w2, 48)
            for which, step, n in [(0, *x[1:]) for x in ORDER if x[0] == HEAD] + [x for x in ORDER if x[0] != BACK]:
                front(which, step, n)
            first = n_[0]
            dve.wait_ge(ld_w3v, 32)
            for whole in (True, False):
                n_[0] = 0
                if whole:
                    with dve.Fori(0, B - 2) as b:
                        base[0] = b * VEC_STEPS + first
                        one_pass(b, ORDER)
                else:
                    base[0] = (B - 2) * VEC_STEPS + first
                    one_pass(B - 2, [x for x in ORDER if x[0] != HEAD])
                assert n_[0] == VEC_STEPS, n_[0]
            base[0] = (B - 1) * VEC_STEPS + first
            n_[0] = 0
            for which, step, n in ORDER:
                if which == BACK:
                    back(B - 1, step, n, final=B - 1)

            for n in range(2):
                dve.wait_ge(n2_high, n + 1)
                cols = (slice(0, NTOK - T), slice(NTOK - T, NTOK))[n]
                v.tensor_tensor(n2l[:, :, cols], n2T[:, :, cols], n2h[:, :, cols].bitcast(F32), ALU.subtract).then_inc(n2_split, 1)
            dve.wait_ge(lg_filled, 1)
            link(v.tensor_copy(lg[:].rearrange("p t e -> p (t e)"), psK[:, 0, 0:NT * E]))
            for t in range(NT):
                ins = v.max(top[:, t, :], lg[:, t, :])
            link(ins)
            v.tensor_tensor(pr[:, 0, :], top[:, :, 1], top[:, :, 0], ALU.subtract).then_inc(top_diff, 1)
            for t in range(NT):
                ins = v.max_index(tix[:, t, :], top[:, t, :], lg[:, t, :])
            link(ins)
            link(v.tensor_copy(tixf[:], tix[:]))
            dve.wait_ge(top_exp, 1)
            link(v.tensor_scalar(pr[:, 2, :], pr[:, 1, :], 1.0, None, ALU.add))
            link(v.reciprocal(pr[:, 2, :], pr[:, 2, :]))
            link(v.tensor_tensor(pr[:, 3, :], pr[:, 1, :], pr[:, 2, :], ALU.mult))
            it = iota8[:].unsqueeze(1).broadcast_to([P, NT, E])
            for j, w in ((0, wgt), (1, wgt2)):
                link(v.tensor_tensor(w[:], it, tixf[:, :, j].unsqueeze(2).broadcast_to([P, NT, E]), ALU.is_equal))
                link(v.tensor_tensor(w[:], w[:], pr[:, 2 + j, :].unsqueeze(2).broadcast_to([P, NT, E]), ALU.mult))
            link(v.tensor_tensor(wgt[:], wgt[:], wgt2[:], ALU.add))
            dve.wait_ge(ld_acc, 16 * (B - 1))

            def low_part(ep, i, f, c):
                dve.wait_ge(hid_high[c], ep * 8 + 4 * i + f + 1)
                o = hTh[:, f, c * 512:(c + 1) * 512]
                v.tensor_tensor(hTl[:, f, c * 512:(c + 1) * 512], hid[:, c, :], o.bitcast(F32), ALU.subtract).then_inc(h_ready[c], 1)

            with dve.Fori(0, E // 2) as ep:
                for i in range(2):
                    for n in range(2 * FT):
                        f, c = n // 2, n % 2
                        dve.wait_ge(U_read[c], ep * 8 + 4 * i + f + 2)
                        dve.wait_ge(W_filled[c], ep * 8 + 4 * i + f + 1)
                        dve.wait_ge(h_ready[c], ep * 8 + 4 * i + f + 1)
                        v.tensor_tensor(hid[:, c, :], sil[:, c, :], psS[:, c, 512:1024], ALU.mult).then_inc(hid_ready[c], 1)
                        if n:
                            low_part(ep, i, (n - 1) // 2, (n - 1) % 2)
                    low_part(ep, i, FT - 1, 1)
                    for t in range(NT):
                        dve.wait_ge(Y_filled[t % 2], ep * 8 + 4 * i + t // 2 + 1)
                        v.scalar_tensor_tensor(out=acc[:, t, :], in0=psA[:, t % 2, 0:D],
                                               scalar=wgt[:, t, bass.ds(ep * 2 + i, 1)],
                                               in1=acc[:, t, :], op0=ALU.mult, op1=ALU.add).then_inc(Y_added[t % 2], 1)
            dve.wait_ge(Y_added[0], E * 4 + 1)
            dve.wait_ge(Y_added[1], E * 4 + 1)
            for t in range(NT):
                ins = v.bn_stats(bstF[:, t, :], acc[:, t, :])
            link(ins)
            for t in range(NT):
                ins = v.bn_aggr(mvF[:, t, :], bstF[:, t, :])
            link(ins)
            v.tensor_scalar(varF[:], mvF[:, :, 1], EPS, None, ALU.add).then_inc(fin_var, 1)
            dve.wait_ge(fin_rstd, 1)
            for t in range(NT):
                v.tensor_scalar(acc[:, t, :], acc[:, t, :], mvF[:, t, 0:1], rstdF[:, t:t + 1],
                                ALU.subtract, ALU.mult).then_inc(fin_ready, 1)

        @block.scalar
        def _(act):
            a_ = nc.scalar

            def exp2(b):
                u = A_USE["energy"]
                act.wait_ge(att2_max, b + 1)
                for n in range(TT):
                    ins = a_.activation(att2[:, n, :], psA[:, u % 2, n * T:(n + 1) * T], ACT.Exp, bias=mx2[:, n:n + 1],
                                        accum_out=sm2[:, n:n + 1])
                ins.then_inc(A.emptied[u % 2], 1)

            def high_parts(b, t):
                act.wait_ge(summed1, b * TT + t + 1)
                if t:
                    act.wait_ge(packed1, b * TT + t)
                a_.copy(hib[:], rt1[:]).then_inc(high1, 1)
                act.wait_ge(rest1, b * TT + t + 1)
                a_.copy(midb[:], rt1[:]).then_inc(mid1, 1)

            def exp1(b, g, uses):
                for c in uses:
                    u = S_EXP + 3 * g + c
                    before = (3 * g + c - PTN) // 3
                    if before >= 0:
                        A.wait_filled(act, b, A_USE["pv", before])
                    S.wait_filled(act, b, u)
                    a_.activation(PT[:, (3 * g + c) % PTN, :], psS[:, u % 2, :], ACT.Exp, scale=HD1 ** -0.5).then_inc(S.emptied[u % 2], 1)

            def evac_q(b, u0, t):
                u = u0 + 2 * t + 1
                S.wait_filled(act, b, u)
                a_.copy(QT[:, 16:32, t * P:(t + 1) * P], psT[:, u % 2, :].rearrange("p (j q) -> p j q", q=P)).then_inc(S.emptied[u % 2], 1)

            def evac_o(b, g):
                u = A_USE["pv", g]
                A.wait_filled(act, b, u)
                if g >= 2:
                    A.wait_filled(act, b, A_USE["turn_o", g - 2])
                a_.copy(OT[:, g % 2, :], psA[:, u % 2, :]).then_inc(A.emptied[u % 2], 1)

            def front(b, step, n):
                if step == "exp2":
                    exp2(b)
                elif step == "pack":
                    high_parts(b, n)
                elif step == "sTa":
                    exp1(b, n, (0, 1))
                elif step == "sTb":
                    exp1(b, n, (2,))
                elif step == "qt":
                    evac_q(b, S_QT, n)
                elif step == "qt2":
                    evac_q(b, S_QT2, n)
                elif step == "pv":
                    evac_o(b, n)

            def evac_v3(b, t):
                u = K_USE["v3", t]
                K.wait_filled(act, b, u)
                a_.copy(V3[:, t, :], psK[:, u % 2, :]).then_inc(K.emptied[u % 2], 1)

            def swap3(b, c):
                u, i = K_USE["p3", c], c % 2
                K.wait_filled(act, b, u)
                if c >= 2:
                    act.wait_ge(summed3, b * 10 + c)
                q = psK[:, u % 2, :].rearrange("p (a t) -> p a t", a=2)
                a_.copy(rb[0:64, i], q[64:128])
                a_.copy(rb[64:128, i], q[0:64]).then_inc(swapped3, 1)

            def exp3(b, c):
                i = c % 2
                act.wait_ge(max3, b * 8 + c + 1)
                if c >= 2:
                    K.wait_filled(act, b, K_USE["turn_p", 2 * c - 3])
                for a in range(2):
                    u = K_USE["s3", 2 * c + a]
                    for t, (lo, hi) in enumerate(((0, P), (P, 384))):
                        ins = a_.activation(P3[:, i, a, lo:hi], psK[:, u % 2, lo:hi], ACT.Exp,
                                            bias=mx3[:, i, 2 * t + u % 2:2 * t + u % 2 + 1],
                                            accum_out=sm3[:, i, 2 * t + a:2 * t + a + 1])
                    ins.then_inc(K.emptied[u % 2], 1)

            def evac_p(b, h):
                u = K_USE["turn_p", h]
                K.wait_filled(act, b, u)
                if h >= 2:
                    K.wait_filled(act, b, K_USE["pv3", h // 2 - 1])
                a_.copy(PT3[:, h % 2, :], psK[:, u % 2, 0:384]).then_inc(K.emptied[u % 2], 1)

            def evac_o3(b, c):
                u = K_USE["pv3", c]
                K.wait_filled(act, b, u)
                a_.copy(O3[:, 2 * c:2 * c + 2, :], psK[:, u % 2, :].rearrange("p (a t) -> p a t", a=2)).then_inc(K.emptied[u % 2], 1)

            def back(b, step, n):
                if step == "v3":
                    evac_v3(b, n)
                elif step == "p3":
                    swap3(b, n)
                elif step == "e3":
                    exp3(b, n)
                elif step == "pt3":
                    evac_p(b, 2 * n)
                    evac_p(b, 2 * n + 1)
                elif step == "pv3":
                    evac_o3(b, n)

            def one_pass(b, order):
                for which, step, n in order:
                    if which == BACK:
                        back(b, step, n)
                    else:
                        front(b + 1 + which, step, n)

            act.wait_ge(consts_made, 1)
            act.wait_ge(lam_dots, 1)
            a_.activation(lame[:], lamd[:], ACT.Exp).then_inc(lam_exp, 1)
            for which, step, n in [(0, *x[1:]) for x in ORDER if x[0] == HEAD] + [x for x in ORDER if x[0] != BACK]:
                front(which, step, n)
            with act.Fori(0, B - 2) as b:
                one_pass(b, ORDER)
            one_pass(B - 2, [x for x in ORDER if x[0] != HEAD])
            one_pass(B - 1, [x for x in ORDER if x[0] == BACK])

            def high_weights(ep, i):
                act.wait_ge(ld_e[i], ep * 48 + 48)
                a_.copy(eh[:, i, :], ew[:, i, :]).then_inc(w_high, 1)

            K.wait_filled(act, B - 1, K_USE["wo3", TT - 1])
            high_weights(0, 0)
            act.wait_ge(ld_n2T, 16 * (B - 1))
            a_.copy(n2h[:, :, 0:NTOK - T], n2T[:, :, 0:NTOK - T]).then_inc(n2_high, 1)
            K.wait_emptied(act, B - 1, K_USE["turn_n2"])
            a_.copy(n2h[:, :, NTOK - T:NTOK], n2T[:, :, NTOK - T:NTOK]).then_inc(n2_high, 1)
            act.wait_ge(top_diff, 1)
            a_.activation(pr[:, 1, :], pr[:, 0, :], ACT.Exp).then_inc(top_exp, 1)

            def high_part(ep, i, f, c):
                act.wait_ge(hid_ready[c], ep * 8 + 4 * i + f + 2)
                a_.copy(hTh[:, f, c * 512:(c + 1) * 512], hid[:, c, :]).then_inc(hid_high[c], 1)

            def expert(ep, i, more):
                for n in range(2 * FT):
                    f, c = n // 2, n % 2
                    act.wait_ge(U_filled[c], ep * 8 + 4 * i + f + 1)
                    act.wait_ge(hid_ready[c], ep * 8 + 4 * i + f + 1)
                    a_.activation(sil[:, c, :], psS[:, c, 0:512], ACT.Silu).then_inc(U_read[c], 1)
                    if n:
                        high_part(ep, i, (n - 1) // 2, (n - 1) % 2)
                high_part(ep, i, FT - 1, 1)
                if more:
                    high_weights(ep + i, 1 - i)

            with act.Fori(0, E // 2 - 1) as ep:
                for i in range(2):
                    expert(ep, i, True)
            for i in range(2):
                expert(E // 2 - 1, i, i == 0)

        @block.gpsimd
        def _(pool):
            p_ = nc.gpsimd
            p_.memset(ident[:], 0.0)
            p_.memset(maskb[:], 0.0)
            p_.memset(maskTb[:], 0.0)
            p_.memset(neghalf[:], -0.5)
            p_.memset(neg1[:], -1.0)
            p_.memset(nhF[:], -0.5).then_inc(pool_step, 1)
            pool.wait_ge(pool_step, 1)
            p_.affine_select(out=ident[:], in_=ident[:], compare_op=ALU.not_equal, fill=1.0, base=0,
                             pattern=[[-1, P]], channel_multiplier=1).then_inc(pool_step, 1)
            p_.affine_select(out=maskb[:], in_=maskb[:], compare_op=ALU.is_ge, fill=NEG, base=0,
                             pattern=[[-1, P]], channel_multiplier=1)
            p_.affine_select(out=maskTb[:], in_=maskTb[:], compare_op=ALU.is_ge, fill=NEG, base=0,
                             pattern=[[1, P]], channel_multiplier=-1)
            p_.iota(iota8[:], [[1, E]], base=0, channel_multiplier=0, allow_small_or_imprecise_dtypes=True)
            pool.wait_ge(pool_step, 2)
            p_.tensor_copy(identb[:], ident[:]).then_inc(consts_made, 1)

            def split1(b, t):
                pool.wait_ge(roped1, b * TT + t + 1)
                p_.tensor_tensor(rt1[:], rt1[:], rt2[:], ALU.add).then_inc(summed1, 1)
                pool.wait_ge(high1, b * TT + t + 1)
                p_.tensor_tensor(rt1[:], rt1[:], hib[:], ALU.subtract).then_inc(rest1, 1)
                pool.wait_ge(mid1, b * TT + t + 1)
                p_.tensor_tensor(lob[:], rt1[:], midb[:], ALU.subtract).then_inc(low1, 1)

            def front(b, step, n):
                if step == "pack":
                    split1(b, n)
                elif step in ("wo", "xm"):
                    pool.wait_ge(var_ready, b * 2 + (step == "xm") + 1)
                    p_.tensor_tensor(rstd[:], var[:], neghalf[:], ALU.pow).then_inc(rstd_ready, 1)

            def back(b, step, n):
                if step in ("n1", "n2"):
                    pool.wait_ge(varb_ready, b * 2 + (step == "n2") + 1)
                    p_.tensor_tensor(rstdb[:], varb[:], neghalf[:], ALU.pow).then_inc(rstdb_ready, 1)
                elif step == "p3":
                    i = n % 2
                    pool.wait_ge(swapped3, b * 10 + n + 1)
                    p_.tensor_tensor(rb[:, i], rb[:, i], rope3s[:, 1, :].unsqueeze(1).broadcast_to([P, 2, T]), ALU.mult)\
                        .then_inc(sined3, 1)
                    K.wait_emptied(pool, b, K_USE["p3", n])
                    pool.wait_ge(sined3, b * 10 + n + 1)
                    p_.tensor_tensor(QK3[:, 2 * n:2 * n + 2, :], ra[:, i], rb[:, i], ALU.add).then_inc(summed3, 1)
                elif step == "e3":
                    i = n % 2
                    for a in range(2):
                        K.wait_emptied(pool, b, K_USE["s3", 2 * n + a])
                    p_.tensor_tensor(rc3[:, i, :], sm3[:, i, :], neg1[:], ALU.pow).then_inc(rec3, 1)
                    pool.wait_ge(rec3, b * 8 + n + 1)
                    p_.tensor_tensor(P3[:, i, :, 0:P], P3[:, i, :, 0:P], rc3[:, i, 0:2].unsqueeze(2).broadcast_to([P, 2, P]), ALU.mult)
                    p_.tensor_tensor(P3[:, i, :, P:384], P3[:, i, :, P:384], rc3[:, i, 2:4].unsqueeze(2).broadcast_to([P, 2, T]),
                                     ALU.mult).then_inc(norm3, 1)

            def one_pass(b, order):
                for which, step, n in order:
                    if which == BACK:
                        back(b, step, n)
                    else:
                        front(b + 1 + which, step, n)

            for which, step, n in [(0, *x[1:]) for x in ORDER if x[0] == HEAD] + [x for x in ORDER if x[0] != BACK]:
                front(which, step, n)
            with pool.Fori(0, B - 2) as b:
                one_pass(b, ORDER)
            one_pass(B - 2, [x for x in ORDER if x[0] != HEAD])
            one_pass(B - 1, [x for x in ORDER if x[0] == BACK])
            def low_weights(e, i):
                pool.wait_ge(w_high, e + 1)
                p_.tensor_tensor(el[:, i, :], ew[:, i, :], eh[:, i, :].bitcast(F32), ALU.subtract).then_inc(w_split, 1)

            with pool.Fori(0, E // 2) as ep:
                for i in range(2):
                    low_weights(ep * 2 + i, i)
            pool.wait_ge(fin_var, 1)
            p_.tensor_tensor(rstdF[:], varF[:], nhF[:], ALU.pow).then_inc(fin_rstd, 1)


VEC_STEPS = 27


def kernel(**inputs):
    import numpy as _np
    import concourse.bacc as _bacc
    from concourse import mybir as _mybir
    from concourse.bass_utils import run_bass_kernel_spmd as _run

    i = {k: _np.asarray(v) for k, v in inputs.items()}
    f32 = _np.float32

    def angles(n, width, theta):
        inv = (1.0 / theta ** (_np.arange(0, width, 2, dtype=f32) / f32(width))).astype(f32)
        return _np.arange(n, dtype=f32)[:, None] * inv[None, :]

    a1 = angles(T, HD1, 10000.0)
    s1 = _np.sin(a1)
    rope1 = _np.stack([_np.tile(_np.cos(a1), (1, 2)), _np.concatenate([-s1, s1], 1)], 1).astype(f32)
    a3 = angles(T, HD3, 1000000.0).T
    s3 = _np.sin(a3)
    rope3 = (_np.stack([_np.tile(_np.cos(a3), (2, 1)), _np.concatenate([-s3, s3], 0)], 1) * HD3 ** -0.25).astype(f32)

    feed = {
        "x": i["x"],
        "xT": i["x"].transpose(0, 2, 1),
        "ctxT": i["ctx_1024"].transpose(0, 2, 1),
        "w1qkv": _np.concatenate([i["L0_attn_wq"].T, i["L0_attn_wk"].T, i["L0_attn_wv"].T], 1),
        "w1o": i["L0_attn_wo"].T,
        "lam": _np.stack([i["L0_attn_lambda_q1"], i["L0_attn_lambda_k1"], i["L0_attn_lambda_q2"], i["L0_attn_lambda_k2"]]),
        "w2q": i["L0_xattn_Wq"].T,
        "w2k": i["L0_xattn_Wk"].T,
        "b2": _np.stack([i["L0_xattn_bq"], i["L0_xattn_bk"]], 1),
        "nw": _np.stack([i["L0_ffn_norm1_w"].reshape(DT, P).T, i["L0_ffn_norm2_w"].reshape(DT, P).T], 1),
        "w3q": i["L0_ffn_wq"], "w3k": i["L0_ffn_wk"], "w3v": i["L0_ffn_wv"], "w3o": i["L0_ffn_wo"],
        "gate": i["L0_ffn_gate_w"],
        "e1": i["L0_ffn_w1"], "e3": i["L0_ffn_w3"], "e2": i["L0_ffn_w2"],
        "rope1": rope1, "rope3": rope3,
    }
    nc = _bacc.Bacc("TRN2", target_bir_lowering=False, num_devices=1)
    arrays, args = {}, []
    for name, a in feed.items():
        a = _np.ascontiguousarray(a)
        arrays[f"in_{name}"] = a
        args.append(nc.dram_tensor(f"in_{name}", a.shape, _mybir.dt.from_np(a.dtype), kind="ExternalInput").ap())
    args.append(nc.dram_tensor("out_0", (B, T, D), _mybir.dt.float32, kind="ExternalOutput").ap())
    decoder_kernel(nc, *args)
    r = _run(nc, [arrays], core_ids=[0])
    return r.results[0]["out_0"]
```

```python
from contextlib import ExitStack
import math

import numpy as np

import concourse.bass as bass
from concourse import mybir

P = 128
B, T, D = 4, 256, 256
TT, DT = T // P, D // P
H1, G1, HD1 = 32, 8, 8
REP1 = H1 // G1
PTN = 6
SLOT = 64
C2 = 128
H3, G3, HD3 = 16, 4, 128
REP3 = H3 // G3
E, F = 8, 512
FT = F // P
NTOK = B * T
NT = NTOK // P
VEC_STEPS = 27
LAMBDA_INIT = 0.8 - 0.6 * math.exp(-0.3 * 12)
EPS = 1e-5
NEG = -1e30

ALU = mybir.AluOpType
ACT = mybir.ActivationFunctionType
AX = mybir.AxisListType
F32 = mybir.dt.float32
F32R = mybir.dt.float32r
BF16 = mybir.dt.bfloat16
U32 = mybir.dt.uint32


class Ring:

    def __init__(self, filled, emptied, uses):
        self.filled, self.emptied, self.half = filled, emptied, uses // 2

    def wait_empty(self, eng, b, u):
        eng.wait_ge(self.emptied[u % 2], b * self.half + u // 2 + 1)

    def wait_filled(self, eng, b, u):
        eng.wait_ge(self.filled[u % 2], b * self.half + u // 2 + 1)

    def wait_emptied(self, eng, b, u):
        eng.wait_ge(self.emptied[u % 2], b * self.half + u // 2 + 2)


S_PROJ, S_KT, S_QT, S_MAX, S_QT2, S_EXP, S_USES = 0, 2, 4, 8, 32, 36, 60
A_NAMES = ["q2", "k2", "energy"]
for _g in range(G1):
    A_NAMES += [("pv", _g)] + ([("turn_o", _g - 1)] if _g else [])
A_NAMES += [("turn_o", G1 - 1), "turn_att1", "wo1", "turn_att2", "turn_x1", "x_m"]
A_USE = {name: n for n, name in enumerate(A_NAMES)}
assert len(A_NAMES) % 2 == 0

FRONT, HEAD, BACK = 0, 1, 2


def pass_order():
    order = [(FRONT, "ctx", 0), (BACK, "n1", 0), (FRONT, "max", 0), (BACK, "n1 scale", 0), (FRONT, "max", 1), (FRONT, "max", 2),
             (FRONT, "energy", 0), (FRONT, "exp2", 0)]
    projections = [("t1", 0), ("v3", 0), ("v3", 1)] + [("p3", c) for c in range((G3 + H3) // 2)]
    maxima = list(range(3, 24))
    while projections:
        order += [(BACK, *projections.pop(0))]
        order += [(FRONT, "max", maxima.pop(0)) for _ in range(min(2, len(maxima)))]
        if not maxima and (FRONT, "packmax", 0) not in order:
            order += [(FRONT, "packmax", 0)]
    order += [(FRONT, "qt2", 0), (FRONT, "qt2", 1)]
    for g in range(G1 + 1):
        scores = [(BACK, "s3", g), (BACK, "e3", g)] if g < G1 else []
        transposed = [(FRONT, "sTa", g)] if g < G1 else []
        values = [(FRONT, "pv", g - 1)] if g else []
        values += [(FRONT, "ot", g - 2)] if g > 1 else []
        values3 = [(BACK, "pv3", g - 2)] if g > 1 else []
        if g == 0:
            order += scores[:1] + transposed + scores[1:] + [(FRONT, "sTb", g)]
        elif g < G1:
            order += transposed + values3 + scores + [(FRONT, "sTb", g)] + values
        else:
            order += values + values3
        order += [(BACK, "pt3", g - 1)] if g else []
        order += [(FRONT, "att2", 0)] if g == 1 else []
    order += [(HEAD, "proj", 0), (BACK, "pv3", G1 - 1), (FRONT, "ot", G1 - 1), (HEAD, "split", 0), (HEAD, "rope", 1),
              (BACK, "wo3", 0), (FRONT, "at", 0), (HEAD, "split", 1), (HEAD, "pack", 0), (BACK, "wo3", 1), (FRONT, "wo", 0),
              (HEAD, "kt", 0), (FRONT, "a2t", 0), (BACK, "wo3", 2), (HEAD, "pack", 1), (FRONT, "x1t", 0), (BACK, "wo3", 3),
              (HEAD, "kt", 1), (FRONT, "xm", 0), (HEAD, "qt", 0), (BACK, "n2", 0), (HEAD, "qt", 1), (BACK, "t2", 0)]
    return order


def headless_order():
    moved = [(BACK, "wo3", 2), (BACK, "wo3", 3), (BACK, "n2", 0), (BACK, "t2", 0)]
    return [x for x in pass_order() if x[0] != HEAD and x not in moved] + moved


def last_order():
    order = [(BACK, step, n) for step, n in (("n1", 0), ("n1 scale", 0), ("t1", 0), ("v3", 0), ("v3", 1), ("p3", 0), ("p3", 1),
                                             ("p3", 2))]
    for c in range(H3 // 2 + 2):
        order += [(BACK, "p3", c + 3)] if c + 3 < (G3 + H3) // 2 else []
        order += [(BACK, "s3", c)] if c < H3 // 2 else []
        order += [(BACK, "e3", c - 1)] if 0 < c <= H3 // 2 else []
        order += [(BACK, "pt3", c - 2), (BACK, "pv3", c - 2)] if c > 1 else []
        order += [(BACK, "early", 0)] if c == 3 else []
    return order + [(BACK, "wo3", n) for n in range(2 * TT)] + [(BACK, "n2", 0), (BACK, "t2", 0)]


def k_uses(order, scores):
    names = []
    for which, step, n in order:
        if which == BACK:
            names += {"t1": ["turn_n1"], "v3": [("v3", n)], "p3": [("p3", n)], "s3": [("s3", 2 * n), ("s3", 2 * n + 1)] * scores,
                      "pt3": [("turn_p", 2 * n), ("turn_p", 2 * n + 1)], "pv3": [("pv3", n)],
                      "wo3": [("wo3", n // 2)] * (n % 2 == 0), "t2": ["turn_n2"]}.get(step, [])
    return {name: u for u, name in enumerate(names)}


def is_last(b):
    return isinstance(b, int) and b == B - 1


def k_use(b):
    return K_LAST if is_last(b) else K_USE


ORDER = pass_order()
LAST_ORDER = last_order()
K_USE, K_LAST = k_uses(ORDER, True), k_uses(LAST_ORDER, False)
assert len(K_USE) % 2 == 0
MAX_STEPS = [(s, t, j0, pairs) for s in range(2) for t, pairs in ((0, 4), (1, 2)) for j0 in range(0, H1 // 2, pairs)]


def decoder_kernel(nc, x, xT, ctxT, w1qkv, w1o, lam, w2q, w2k, b2, nw, w3q, w3k, w3v, w3o, gate,
                   e1, e3, e2, rope1, rope3, out):
    ctx = ExitStack()
    with ctx:
        def sb(name, shape, dt=F32):
            return ctx.enter_context(nc.sbuf_tensor(name, shape, dt))

        def room(*groups):
            tensors = []
            for group in groups[:-1]:
                with ExitStack() as turn:
                    tensors += [turn.enter_context(nc.sbuf_tensor(name, shape, *(dt or (F32,)))) for name, shape, *dt in group]
            return tensors + [sb(*t) for t in groups[-1]]

        def sem(name):
            return ctx.enter_context(nc.semaphore(name))

        psS = ctx.enter_context(nc.psum_tensor("psS", [P, 2, 1024], F32))
        psA = ctx.enter_context(nc.psum_tensor("psA", [P, 2, 512], F32))
        psK = ctx.enter_context(nc.psum_tensor("psK", [P, 2, 512], F32))

        ident = sb("ident", [P, P])
        identb = sb("identb", [P, P], BF16)
        maskb = sb("maskb", [P, P], BF16)
        maskTb = sb("maskTb", [P, P], BF16)
        neghalf = sb("neghalf", [P, TT])
        neg1 = sb("neg1", [P, 4])
        iota8 = sb("iota8", [P, E])
        wqkv1 = sb("wqkv1", [P, DT, 704])
        wo1 = sb("wo1", [P, DT, D])
        rope1s = sb("rope1s", [P, TT, 2, HD1])
        rope3s = sb("rope3s", [P, 2, T])
        lams = sb("lams", [P, 4, HD1])
        lamp = sb("lamp", [P, 2, HD1])
        lamd = sb("lamd", [P, 2])
        lame = sb("lame", [P, 2])
        fac = sb("fac", [P, 2, 2])
        wq2 = sb("wq2", [P, C2])
        wk2 = sb("wk2", [P, C2])
        b2s = sb("b2s", [P, 2])
        nws = sb("nws", [P, 2, DT])
        ew, el, eh, w3, wo3, QK3 = room(
            [("ew", [P, 2, 3072])],
            [("el", [P, 2, 3072], F32R), ("eh", [P, 2, 3072], F32R)],
            [("w3", [P, DT, (H3 + 2 * G3) * HD3]), ("wo3", [P, H3, D]), ("QK3", [P, G3 + H3, T])])
        wq3, wk3, wv3 = w3[:, :, 0:2048], w3[:, :, 2048:2560], w3[:, :, 2560:3072]
        gates = sb("gates", [P, DT, E])

        xTs = sb("xTs", [P, DT, T])
        xs = sb("xs", [P, TT, D])
        cTs = sb("cTs", [P, T])
        acc, n2T, n2h, n2l, hTh, hTl, QT, KT, PT, qpack = room(
            [("acc", [P, NT, D]), ("n2T", [P, DT, NTOK]), ("n2h", [P, DT, NTOK], F32R), ("n2l", [P, DT, NTOK], F32R),
             ("hTh", [P, FT, NTOK], F32R), ("hTl", [P, FT, NTOK], F32R)],
            [("QT", [P, H1, T], BF16), ("KT", [P, 2 * G1, 2, T], BF16), ("PT", [P, PTN, 1024]), ("qpack", [P, TT, 2 * H1, SLOT], BF16)])
        PTf = PT[:, :, :].rearrange("p n c -> p (n c)")
        rt1, rt2 = [PTf[:, i * TT * 640:(i + 1) * TT * 640].rearrange("p (t c) -> p t c", t=TT) for i in range(2)]
        hib, midb, lob = [PTf[:, 2 * TT * 640 + i * TT * 320:2 * TT * 640 + (i + 1) * TT * 320].bitcast(BF16)
                          .rearrange("p (t c) -> p t c", t=TT) for i in range(3)]
        kpack = sb("kpack", [P, 2 * G1, 2, SLOT], BF16)
        Vx = sb("Vx", [P, TT, G1, 32])
        negm = sb("negm", [P, TT, 2 * H1])
        mres = sb("mres", [P, TT, 2 * H1])
        OT = sb("OT", [P, 2, 512])
        rs1 = sb("rs1", [P, 2, 4, 4])
        on1 = sb("on1", [P, 2, 4, 4, HD1])
        att1 = sb("att1", [P, TT, D])
        tT = sb("tT", [P, DT, T])
        x1 = sb("x1", [P, TT, D])
        x2 = sb("x2", [P, TT, D])
        bst = sb("bst", [P, TT, 6])
        mv = sb("mv", [P, TT, 2])
        var = sb("var", [P, TT])
        rstd = sb("rstd", [P, TT])
        q2T = sb("q2T", [P, 2, T])
        att2 = sb("att2", [P, TT, T])
        idle_v = sb("idle_v", [P, 1])
        mx2 = sb("mx2", [P, TT])
        sm2 = sb("sm2", [P, TT])
        x2b = sb("x2b", [P, TT, D])
        xnb = sb("xnb", [P, TT, D])
        nT = sb("nT", [P, DT, T])
        hb = nT
        sqb = sb("sqb", [P, TT])
        varb = sb("varb", [P, TT])
        rstdb = sb("rstdb", [P, TT])
        V3 = sb("V3", [P, TT, G3 * HD3])
        ra = sb("ra", [P, 2, 2, T])
        rb = sb("rb", [P, 2, 2, T])
        mx3 = sb("mx3", [P, 2, 4])
        sm3 = sb("sm3", [P, 2, 4])
        rc3 = sb("rc3", [P, 2, 4])
        P3 = sb("P3", [P, 2, 2, 384])
        PT3 = sb("PT3", [P, 2, 384])
        O3 = QK3[:, G3:G3 + H3, :]

        n2T_dram = nc.dram_tensor("n2T_dram", (B, P, DT, T), F32, kind="Internal").ap()
        acc_dram = nc.dram_tensor("acc_dram", (B, P, TT, D), F32, kind="Internal").ap()
        lg = sb("lg", [P, NT, E])
        top = sb("top", [P, NT, 8])
        tix = sb("tix", [P, NT, 8], U32)
        tixf = sb("tixf", [P, NT, 8])
        pr = sb("pr", [P, 4, NT])
        wgt = sb("wgt", [P, NT, E])
        wgt2 = sb("wgt2", [P, NT, E])
        bstF = sb("bstF", [P, NT, 6])
        mvF = sb("mvF", [P, NT, 2])
        varF = sb("varF", [P, NT])
        nhF = sb("nhF", [P, NT])
        rstdF = sb("rstdF", [P, NT])

        def matrices(w):
            return (w[:, 0:1024].rearrange("p (k f) -> p k f", k=DT), w[:, 1024:2048].rearrange("p (k f) -> p k f", k=DT),
                    w[:, 2048:3072].rearrange("p (k f) -> p k f", k=FT))

        ehs, els = [matrices(eh[:, i, :]) for i in range(2)], [matrices(el[:, i, :]) for i in range(2)]
        sil = ra[:, :, :, :].rearrange("p c a t -> p c (a t)")
        hid = rb[:, :, :, :].rearrange("p c a t -> p c (a t)")

        ld_w1 = sem("ld_w1")
        ld_rope1 = sem("ld_rope1")
        ld_w1o = sem("ld_w1o")
        ld_w2 = sem("ld_w2")
        ld_w3v = sem("ld_w3v")
        ld_w3k = sem("ld_w3k")
        ld_w3q = sem("ld_w3q")
        ld_w3o = sem("ld_w3o")
        ld_gate = sem("ld_gate")
        ld_small = sem("ld_small")
        ld_xT = sem("ld_xT")
        ld_x = sem("ld_x")
        ld_c = sem("ld_c")
        ld_e = [sem(f"ld_e{i}") for i in range(2)]
        consts_made = sem("consts_made")
        S = Ring([sem(f"S_filled{i}") for i in range(2)], [sem(f"S_emptied{i}") for i in range(2)], S_USES)
        A = Ring([sem(f"A_filled{i}") for i in range(2)], [sem(f"A_emptied{i}") for i in range(2)], len(A_NAMES))
        K = Ring([sem(f"K_filled{i}") for i in range(2)], [sem(f"K_emptied{i}") for i in range(2)], len(K_USE))
        vec_step = sem("vec_step")
        pool_step = sem("pool_step")
        roped1 = sem("roped1")
        summed1 = sem("summed1")
        high1 = sem("high1")
        rest1 = sem("rest1")
        mid1 = sem("mid1")
        low1 = sem("low1")
        packed1 = sem("packed1")
        maxed1 = sem("maxed1")
        attn1 = sem("attn1")
        var_ready = sem("var_ready")
        rstd_ready = sem("rstd_ready")
        x1_ready = sem("x1_ready")
        x2_ready = sem("x2_ready")
        x2_read = sem("x2_read")
        att2_max = sem("att2_max")
        att2_ready = sem("att2_ready")
        xn_ready = sem("xn_ready")
        varb_ready = sem("varb_ready")
        rstdb_ready = sem("rstdb_ready")
        acc_ready = sem("acc_ready")
        spilled = sem("spilled")
        ld_acc = sem("ld_acc")
        ld_n2T = sem("ld_n2T")
        swapped3 = sem("swapped3")
        sined3 = sem("sined3")
        summed3 = sem("summed3")
        max3 = sem("max3")
        rec3 = sem("rec3")
        norm3 = sem("norm3")
        zeros_made = sem("zeros_made")
        lam_dots = sem("lam_dots")
        lam_exp = sem("lam_exp")
        lg_filled = sem("lg_filled")
        lg_read = sem("lg_read")
        top_diff = sem("top_diff")
        top_exp = sem("top_exp")
        U_filled = [sem(f"U_filled{i}") for i in range(2)]
        U_read = [sem(f"U_read{i}") for i in range(2)]
        W_filled = [sem(f"W_filled{i}") for i in range(2)]
        hid_ready = [sem(f"hid_ready{i}") for i in range(2)]
        hid_high = [sem(f"hid_high{i}") for i in range(2)]
        h_ready = [sem(f"h_ready{i}") for i in range(2)]
        w_high = sem("w_high")
        w_split = sem("w_split")
        n2_high = sem("n2_high")
        n2_split = sem("n2_split")
        Y_filled = [sem(f"Y_filled{i}") for i in range(2)]
        Y_added = [sem(f"Y_added{i}") for i in range(2)]
        fin_var = sem("fin_var")
        fin_rstd = sem("fin_rstd")
        fin_ready = sem("fin_ready")
        stored = sem("stored")

        psT = psS[:, :, :].bitcast(BF16)
        block = ctx.enter_context(nc.Block())

        @block.sync
        def _(sp):
            sp.dma_start(wqkv1[:, 0, :], w1qkv[0:P, :]).then_inc(ld_w1, 16)

            def load_xT(b):
                sp.dma_start(xTs[:], xT[bass.ds(b, 1), :, :].rearrange("o (k p) t -> p (o k) t", p=P)).then_inc(ld_xT, 16)

            def load_ctx(b):
                sp.dma_start(cTs[:], ctxT[bass.ds(b, 1), :, :].rearrange("o p t -> p (o t)")).then_inc(ld_c, 16)

            def load_x(b):
                sp.dma_start(xs[:], x[bass.ds(b, 1), :, :].rearrange("o (k p) d -> p (o k) d", p=P)).then_inc(ld_x, 16)

            def load_next(b):
                for t in range(TT):
                    S.wait_emptied(sp, b - 1, S_PROJ + t)
                load_xT(b)
                A.wait_emptied(sp, b - 1, A_USE["k2"])
                load_ctx(b)
                A.wait_emptied(sp, b - 1, A_USE["wo1"])
                load_x(b)

            def spill(b):
                sp.wait_ge(acc_ready, b + 1)
                sp.dma_start(acc_dram[bass.ds(b, 1), :, :, :].rearrange("o p t d -> p (o t) d"), x2b[:]).then_inc(spilled, 16)
                K.wait_emptied(sp, b, k_use(b)["turn_n2"])
                sp.dma_start(n2T_dram[bass.ds(b, 1), :, :, :].rearrange("o p k t -> p (o k) t"), nT[:]).then_inc(spilled, 16)

            load_xT(0)
            sp.dma_start(rope1s[:], rope1.rearrange("(t p) c d -> p t c d", p=P)).then_inc(ld_rope1, 16)
            load_ctx(0)
            sp.dma_start(wq2[:], w2q).then_inc(ld_w2, 16)
            sp.dma_start(wk2[:], w2k).then_inc(ld_w2, 16)
            sp.dma_start(b2s[:], b2).then_inc(ld_w2, 16)
            sp.dma_start(nws[:], nw).then_inc(ld_small, 16)
            sp.dma_start(lams[:], lam.partition_broadcast(P)).then_inc(ld_small, 16)
            load_x(0)
            sp.dma_start(wo1[:], w1o.rearrange("(k p) n -> p k n", p=P)).then_inc(ld_w1o, 16)
            sp.dma_start(rope3s[:], rope3).then_inc(ld_w3v, 16)
            sp.dma_start(wv3, w3v.rearrange("(k p) n -> p k n", p=P)).then_inc(ld_w3v, 16)
            sp.dma_start(wk3, w3k.rearrange("(k p) n -> p k n", p=P)).then_inc(ld_w3k, 16)
            sp.dma_start(wq3, w3q.rearrange("(k p) n -> p k n", p=P)).then_inc(ld_w3q, 16)
            sp.dma_start(wo3[:], w3o.rearrange("(k p) n -> p k n", p=P)).then_inc(ld_w3o, 16)
            sp.dma_start(gates[:], gate.rearrange("(k p) n -> p k n", p=P)).then_inc(ld_gate, 16)
            load_next(1)
            with sp.Fori(0, B - 2) as b:
                load_next(b + 2)
                spill(b)
            spill(B - 2)

            def load_expert(e, i):
                for w, lo, k in ((e1, 0, DT), (e3, 1024, DT), (e2, 2048, FT)):
                    sp.dma_start(ew[:, i, lo:lo + 1024].rearrange("p (k f) -> p k f", k=k),
                                 w[bass.ds(e, 1), :, :].rearrange("o (k p) f -> p (o k) f", p=P)).then_inc(ld_e[i], 16)

            A.wait_emptied(sp, B - 1, A_USE["x_m"])
            sp.wait_ge(spilled, 1 + 32 * (B - 1))
            for b in range(B - 1):
                sp.dma_start(n2T[:, :, b * T:(b + 1) * T], n2T_dram[b, :, :, :]).then_inc(ld_n2T, 16)
                sp.dma_start(acc[:, b * TT:(b + 1) * TT, :], acc_dram[b, :, :, :]).then_inc(ld_acc, 16)
            for c in (8, 9):
                K.wait_emptied(sp, B - 1, k_use(B - 1)["p3", c])
            load_expert(0, 0)
            load_expert(1, 1)
            with sp.Fori(1, E // 2) as ep:
                for i in range(2):
                    sp.wait_ge(Y_filled[1], ep * NT + (i - 1) * NT // 2)
                    load_expert(ep * 2 + i, i)
            for t in range(NT):
                sp.wait_ge(fin_ready, t + 1)
                sp.dma_start(out.rearrange("b (t p) d -> p (b t) d", p=P)[:, t, :], acc[:, t, :]).then_inc(stored, 16)
            sp.wait_ge(stored, 16 * NT)

        @block.tensor
        def _(pe):
            mm = pe.matmul

            def project1(b):
                pe.wait_ge(ld_xT, b * 16 + 16)
                for t in range(TT):
                    S.wait_empty(pe, b, S_PROJ + t)
                    for lo, n in ((0, 512), (512, 192)):
                        for k in range(DT):
                            last = mm(psS[:, t, lo:lo + n], xTs[:, k, t * P:(t + 1) * P], wqkv1[:, k, lo:lo + n],
                                      start=(k == 0), stop=(k == DT - 1))
                    last.then_inc(S.filled[t], 1)

            def queries2(b):
                pe.wait_ge(ld_c, b * 16 + 16)
                for name, w in (("q2", wq2), ("k2", wk2)):
                    u = A_USE[name]
                    A.wait_empty(pe, b, u)
                    mm(psA[:, u % 2, 0:T], w[:], cTs[:], start=True, stop=True).then_inc(A.filled[u % 2], 1)

            def energy2(b):
                u = A_USE["energy"]
                A.wait_emptied(pe, b, A_USE["q2"])
                A.wait_emptied(pe, b, A_USE["k2"])
                for n in range(TT):
                    last = mm(psA[:, u % 2, n * T:(n + 1) * T], q2T[:, 0, n * P:(n + 1) * P], q2T[:, 1, :], start=True, stop=True)
                last.then_inc(A.filled[u % 2], 1)

            def turn(b, u, src):
                S.wait_empty(pe, b, u)
                for j in range(16):
                    last = pe.transpose(psT[:, u % 2, j * P:(j + 1) * P], src(j), identb[:])
                last.then_inc(S.filled[u % 2], 1)

            def turn_k(b, t):
                pe.wait_ge(packed1, b * TT + t + 1)
                turn(b, S_KT + t, lambda j: kpack[:, j, :, :].rearrange("p a c -> p (a c)"))

            def turn_q(b, u0, t):
                for s in range(2):
                    turn(b, u0 + 2 * t + s, lambda j: qpack[:, t, 32 * s + 2 * j:32 * s + 2 * j + 2, :].rearrange("p a c -> p (a c)"))

            def max_scores(b, n):
                if n == 0:
                    for u in (S_MAX - 2, S_MAX - 1):
                        S.wait_emptied(pe, b, u)
                u = S_MAX + n
                s, t, j0, pairs = MAX_STEPS[n]
                keys = P * (t + 1)
                S.wait_empty(pe, b, u)
                for j in range(j0, j0 + pairs):
                    w = 2 * keys
                    o = psS[:, u % 2, (j - j0) * w:(j - j0 + 1) * w].rearrange("p (a k) -> p a k", a=2)
                    g = (j * 2) // REP1
                    mm(o, QT[:, s * 16 + j, t * P:(t + 1) * P], KT[:, s * G1 + g, :, 0:keys],
                       start=(j - j0) * w % 512 == 0, stop=True, skip_group_check=True)
                    last = mm(o[:, :, keys - P:keys], identb[:], maskb[:].unsqueeze(1).broadcast_to([P, 2, P]),
                              start=False, stop=True, skip_group_check=True)
                last.then_inc(S.filled[u % 2], 1)

            mask2 = maskTb[:].unsqueeze(1).broadcast_to([P, 2, P])

            def scoresT(b, g):
                if g == 0:
                    for u in (S_QT2 + 2, S_QT2 + 3):
                        S.wait_emptied(pe, b, u)
                u = S_EXP + 3 * g
                for s in range(2):
                    S.wait_empty(pe, b, u + s)
                    for a in range(2):
                        o = psS[:, (u + s) % 2, a * 512:(a + 1) * 512].rearrange("p (j q) -> p j q", q=T)
                        mm(o, KT[:, s * G1 + g, a, 0:P], QT[:, s * 16 + 2 * g:s * 16 + 2 * g + 2, :], start=True, stop=True)
                        last = mm(o[:, :, 0:P], identb[:], mask2, start=False, stop=True, skip_group_check=True)
                    last.then_inc(S.filled[(u + s) % 2], 1)

            def scoresT_second(b, g):
                u = S_EXP + 3 * g + 2
                S.wait_empty(pe, b, u)
                for s in range(2):
                    for a in range(2):
                        o = psS[:, u % 2, s * 512 + a * T:s * 512 + (a + 1) * T]
                        mm(o, KT[:, s * G1 + g, a, P:T], QT[:, s * 16 + 2 * g:s * 16 + 2 * g + 2, P:T], start=True, stop=False)
                        last = mm(o, identb[:], mask2, start=False, stop=True)
                last.then_inc(S.filled[u % 2], 1)

            def values1(b, g):
                u = A_USE["pv", g]
                o = psA[:, u % 2, :]
                A.wait_empty(pe, b, u)
                for c in (1, 2):
                    S.wait_emptied(pe, b, S_EXP + 3 * g + c)
                for j in range(4):
                    s, a = j // 2, j % 2
                    mm(o[32 * j:32 * j + 32, :], Vx[:, 0, g, :], PT[:, (3 * g + s) % PTN, a * 512:(a + 1) * 512], start=True, stop=True)
                for j in range(4):
                    s, a = j // 2, j % 2
                    last = mm(o[32 * j:32 * j + 32, :].rearrange("p (j q) -> p j q", j=2)[:, :, P:T], Vx[:, 1, g, :],
                              PT[:, (3 * g + 2) % PTN, s * 512 + a * T:s * 512 + (a + 1) * T].rearrange("p (j q) -> p j q", j=2),
                              start=False, stop=True, skip_group_check=True)
                last.then_inc(A.filled[u % 2], 1)

            def turn_o(b, g):
                u = A_USE["turn_o", g]
                A.wait_emptied(pe, b, A_USE["pv", g])
                A.wait_empty(pe, b, u)
                for j in range(4):
                    last = pe.transpose(psA[:, u % 2, j * P:(j + 1) * P], OT[:, g % 2, j * P:(j + 1) * P], ident[:])
                last.then_inc(A.filled[u % 2], 1)

            def turn4(ring, ps, b, u, src):
                ring.wait_empty(pe, b, u)
                for k in range(DT):
                    for t in range(TT):
                        last = pe.transpose(ps[:, u % 2, k * T + t * P:k * T + (t + 1) * P], src[:, t, k * P:(k + 1) * P], ident[:])
                last.then_inc(ring.filled[u % 2], 1)

            def rows(b, u, rhs):
                A.wait_empty(pe, b, u)
                for t in range(TT):
                    for k in range(DT):
                        last = mm(psA[:, u % 2, t * D:(t + 1) * D], tT[:, k, t * P:(t + 1) * P], rhs[:, k, :],
                                  start=(k == 0), stop=(k == DT - 1))
                last.then_inc(A.filled[u % 2], 1)

            def front(b, step, n):
                if step == "proj":
                    project1(b)
                elif step == "ctx":
                    queries2(b)
                elif step == "energy":
                    energy2(b)
                elif step == "kt":
                    turn_k(b, n)
                elif step == "qt":
                    turn_q(b, S_QT, n)
                elif step == "max":
                    max_scores(b, n)
                elif step == "qt2":
                    pe.wait_ge(maxed1, b + 1)
                    turn_q(b, S_QT2, n)
                elif step == "sTa":
                    scoresT(b, n)
                elif step == "sTb":
                    scoresT_second(b, n)
                elif step == "pv":
                    values1(b, n)
                elif step == "ot":
                    turn_o(b, n)
                elif step == "at":
                    pe.wait_ge(attn1, b + 1)
                    turn4(A, psA, b, A_USE["turn_att1"], att1)
                elif step == "wo":
                    A.wait_emptied(pe, b, A_USE["turn_att1"])
                    rows(b, A_USE["wo1"], wo1)
                elif step == "a2t":
                    pe.wait_ge(att2_ready, b + 1)
                    turn4(A, psA, b, A_USE["turn_att2"], att2)
                elif step == "x1t":
                    pe.wait_ge(x1_ready, b + 1)
                    turn4(A, psA, b, A_USE["turn_x1"], x1)
                elif step == "xm":
                    A.wait_emptied(pe, b, A_USE["turn_att2"])
                    A.wait_emptied(pe, b, A_USE["turn_x1"])
                    rows(b, A_USE["x_m"], q2T)

            def values3_project(b, t):
                u = k_use(b)["v3", t]
                K.wait_emptied(pe, b, k_use(b)["turn_n1"])
                K.wait_empty(pe, b, u)
                for k in range(DT):
                    last = mm(psK[:, u % 2, :], nT[:, k, t * P:(t + 1) * P], wv3[:, k, :], start=(k == 0), stop=(k == DT - 1))
                last.then_inc(K.filled[u % 2], 1)

            def heads3_project(b, c):
                u = k_use(b)["p3", c]
                K.wait_empty(pe, b, u)
                for a in range(2):
                    h = 2 * c + a
                    w, n = (wk3, h) if h < G3 else (wq3, h - G3)
                    for k in range(DT):
                        last = mm(psK[:, u % 2, a * T:(a + 1) * T], w[:, k, n * P:(n + 1) * P], nT[:, k, :],
                                  start=(k == 0), stop=(k == DT - 1))
                last.then_inc(K.filled[u % 2], 1)

            def scores3(b, c):
                pe.wait_ge(summed3, b * 10 + 4 + c)
                if is_last(b):
                    S.wait_empty(pe, B, c)
                for a in range(2):
                    h = 2 * c + a
                    if is_last(b):
                        o = psS[:, c % 2, a * 512:a * 512 + 384]
                    else:
                        u = k_use(b)["s3", h]
                        K.wait_empty(pe, b, u)
                        o = psK[:, u % 2, 0:384]
                    q, k = QK3[:, G3 + h, :], QK3[:, h // REP3, :]
                    mm(o[:, 0:P], q[:, 0:P], k[:, 0:P], start=True, stop=False)
                    mm(o[:, 0:P], identb[:], maskb[:], start=False, stop=True)
                    mm(o[:, P:384], q[:, P:T], k[:, :], start=True, stop=True)
                    last = mm(o[:, T:384], identb[:], maskb[:], start=False, stop=True, skip_group_check=True)
                    if not is_last(b):
                        last.then_inc(K.filled[u % 2], 1)
                if is_last(b):
                    last.then_inc(S.filled[c % 2], 1)

            def turn_p(b, c):
                pe.wait_ge(norm3, b * 8 + c + 1)
                for a in range(2):
                    u = k_use(b)["turn_p", 2 * c + a]
                    K.wait_empty(pe, b, u)
                    src = P3[:, c % 2, a, :]
                    for lo in (0, P, T):
                        last = pe.transpose(psK[:, u % 2, lo:lo + P], src[:, lo:lo + P], ident[:])
                    last.then_inc(K.filled[u % 2], 1)

            def values3(b, c):
                u = k_use(b)["pv3", c]
                for a in range(2):
                    K.wait_emptied(pe, b, k_use(b)["turn_p", 2 * c + a])
                K.wait_empty(pe, b, u)
                for a in range(2):
                    g = (2 * c + a) // REP3
                    o = psK[:, u % 2, a * T:(a + 1) * T]
                    mm(o, V3[:, 0, g * P:(g + 1) * P], PT3[:, a, 0:T], start=True, stop=True)
                    last = mm(o[:, P:T], V3[:, 1, g * P:(g + 1) * P], PT3[:, a, T:384], start=False, stop=True,
                              skip_group_check=True)
                last.then_inc(K.filled[u % 2], 1)

            def out3(b, n):
                t, half = n // 2, n % 2
                if n == 0:
                    for c in (H3 // 2 - 2, H3 // 2 - 1):
                        K.wait_emptied(pe, b, k_use(b)["pv3", c])
                u = k_use(b)["wo3", t]
                if half == 0:
                    K.wait_empty(pe, b, u)
                for h in range(half * H3 // 2, (half + 1) * H3 // 2):
                    last = mm(psK[:, u % 2, 0:D], O3[:, h, t * P:(t + 1) * P], wo3[:, h, :],
                              start=(h == 0), stop=(h == H3 - 1))
                if half:
                    last.then_inc(K.filled[u % 2], 1)

            def back(b, step, n):
                if step == "t1":
                    pe.wait_ge(xn_ready, 2 * b + 1)
                    turn4(K, psK, b, k_use(b)["turn_n1"], xnb)
                elif step == "v3":
                    values3_project(b, n)
                elif step == "p3":
                    heads3_project(b, n)
                elif step == "s3":
                    scores3(b, n)
                elif step == "pt3":
                    turn_p(b, n)
                elif step == "pv3":
                    values3(b, n)
                elif step == "wo3":
                    out3(b, n)
                elif step == "early":
                    pe.wait_ge(ld_n2T, 16 * (B - 1))
                    pe.wait_ge(ld_gate, 16)
                    logits(0, NT - TT)
                elif step == "t2":
                    pe.wait_ge(xn_ready, 2 * b + 2)
                    turn4(K, psK, b, k_use(b)["turn_n2"], xnb)

            def logits(t0, t1):
                for t in range(t0, t1):
                    for k in range(DT):
                        last = mm(psA[:, t0 % 4 // 2, t * E:(t + 1) * E], n2T[:, k, t * P:(t + 1) * P], gates[:, k, :],
                                  start=(k == 0), stop=(k == DT - 1))
                last.then_inc(lg_filled, 1)

            def one_pass(b, order):
                for which, step, n in order:
                    if which == BACK:
                        back(b, step, n)
                    else:
                        front(b + 1 + which, step, n)

            pe.wait_ge(consts_made, 1)
            pe.wait_ge(ld_w1, 32)
            for which, step, n in [(0, *x[1:]) for x in ORDER if x[0] == HEAD] + [x for x in ORDER if x[0] != BACK]:
                if step == "ctx":
                    pe.wait_ge(ld_w2, 48)
                elif step == "wo":
                    pe.wait_ge(ld_w1o, 16)
                front(which, step, n)
            for weights, count in ((ld_w3v, 32), (ld_w3k, 16), (ld_w3q, 16), (ld_w3o, 16)):
                pe.wait_ge(weights, count)
            with pe.Fori(0, B - 2) as b:
                one_pass(b, ORDER)
            one_pass(B - 2, headless_order())
            one_pass(B - 1, LAST_ORDER)

            for name in (("wo3", TT - 1), "turn_n2"):
                K.wait_emptied(pe, B - 1, k_use(B - 1)[name])
            logits(NT - TT, NT)

            def product3(o, pairs):
                for n, (lh, ll, rh, rl) in enumerate(pairs):
                    mm(o, lh, rl, start=(n == 0), stop=False)
                    mm(o, ll, rh, start=False, stop=False)
                    last = mm(o, lh, rh, start=False, stop=(n == len(pairs) - 1))
                return last

            pe.wait_ge(n2_split, 2)
            pe.wait_ge(lg_read, 2)
            with pe.Fori(0, E // 2) as ep:
                for i in range(2):
                    pe.wait_ge(w_split, ep * 2 + i + 1)
                    for f in range(FT):
                        for c in range(2):
                            pe.wait_ge(U_read[c], ep * 8 + 4 * i + f + 1)
                            pe.wait_ge(hid_ready[c], ep * 8 + 4 * i + f + 1)
                            for w, half, filled in ((0, slice(0, 512), U_filled), (1, slice(512, 1024), W_filled)):
                                product3(psS[:, c, half],
                                         [(ehs[i][w][:, k, f * P:(f + 1) * P], els[i][w][:, k, f * P:(f + 1) * P],
                                           n2h[:, k, c * 512:(c + 1) * 512], n2l[:, k, c * 512:(c + 1) * 512]) for k in range(DT)])\
                                    .then_inc(filled[c], 1)
                    for t in range(NT):
                        c = t // 4
                        pe.wait_ge(h_ready[c], ep * 8 + 4 * i + 5)
                        pe.wait_ge(Y_added[t % 2], ep * 8 + 4 * i + t // 2 + 1)
                        product3(psA[:, t % 2, 0:D],
                                 [(hTh[:, f, t * P:(t + 1) * P], hTl[:, f, t * P:(t + 1) * P],
                                   ehs[i][2][:, f, :], els[i][2][:, f, :]) for f in range(FT)]).then_inc(Y_filled[t % 2], 1)

        @block.vector
        def _(dve):
            v = nc.vector
            n_ = [0]
            base = [0]

            def link(ins):
                ins.then_inc(vec_step, 1)
                n_[0] += 1
                dve.wait_ge(vec_step, base[0] + n_[0])

            def rope1_products(b, t):
                S.wait_filled(dve, b, S_PROJ + t)
                qk = psS[:, t, 0:640].rearrange("p (h d) -> p h d", d=HD1)
                c, s = rope1s[:, t, 0, :], rope1s[:, t, 1, :]
                v.tensor_tensor(rt1[:, t, :].rearrange("p (h d) -> p h d", d=HD1), qk, c.unsqueeze(1).broadcast_to([P, 80, HD1]), ALU.mult)
                r = rt2[:, t, :].rearrange("p (h d) -> p h d", d=HD1)
                v.tensor_tensor(r[:, :, 0:4], qk[:, :, 4:8], s[:, 0:4].unsqueeze(1).broadcast_to([P, 80, 4]), ALU.mult)
                v.tensor_tensor(r[:, :, 4:8], qk[:, :, 0:4], s[:, 4:8].unsqueeze(1).broadcast_to([P, 80, 4]),
                                ALU.mult).then_inc(roped1, 1)
                v.tensor_copy(Vx[:, t, :, 0:HD1], psS[:, t, 640:704].rearrange("p (g d) -> p g d", d=HD1)).then_inc(S.emptied[t], 1)

            def pack(b, t):
                v.memset(qpack[:, t, :, 48:51], 0.0)
                if t:
                    S.wait_filled(dve, b, S_KT)
                for parts, src, done in (((0, 3), hib, high1), ((3, 2), midb, mid1), ((5, 1), lob, low1)):
                    dve.wait_ge(done, b * TT + t + 1)
                    lo, k = parts
                    v.tensor_copy(qpack[:, t, :, lo * 8:(lo + k) * 8].rearrange("p h (c d) -> p h c d", c=k),
                                  src[:, t, 0:512].rearrange("p (h d) -> p h d", d=HD1).unsqueeze(2).broadcast_to([P, 64, k, HD1]))
                for a in range(2):
                    for slots, src in (((0, 3, 5), hib), ((1, 4), midb), ((2,), lob)):
                        for sl in slots:
                            last = v.tensor_copy(kpack[:, :, a, sl * 8:sl * 8 + 8],
                                                 src[:, t, 512:640].rearrange("p (h d) -> p h d", d=HD1))
                last.then_inc(packed1, 1)

            def evac_k(b, t):
                u = S_KT + t
                S.wait_filled(dve, b, u)
                src = psT[:, u % 2, :].rearrange("p (j q) -> p j q", q=P)
                v.tensor_copy(KT[0:64, :, 0, t * P:(t + 1) * P], src[0:64])
                v.tensor_copy(KT[64:128, :, 1, t * P:(t + 1) * P], src[64:128]).then_inc(S.emptied[u % 2], 1)

            def evac_q(b, u0, t):
                s = 1 if u0 == S_QT else 0
                u = u0 + 2 * t + s
                S.wait_filled(dve, b, u)
                v.tensor_copy(QT[:, 16 * s:16 * s + 16, t * P:(t + 1) * P],
                              psT[:, u % 2, :].rearrange("p (j q) -> p j q", q=P)).then_inc(S.emptied[u % 2], 1)

            def maxima1(b, n):
                u = S_MAX + n
                s, t, j0, pairs = MAX_STEPS[n]
                S.wait_filled(dve, b, u)
                v.tensor_reduce(negm[:, t, s * H1 + 2 * j0:s * H1 + 2 * (j0 + pairs)],
                                psS[:, u % 2, :].rearrange("p (h k) -> p h k", h=2 * pairs),
                                AX.X, ALU.max, negate=True).then_inc(S.emptied[u % 2], 1)

            def pack_maxima(b):
                S.wait_emptied(dve, b, S_MAX + 23)
                q = [qpack[:, :, :, 48 + i] for i in range(3)]
                link(v.tensor_copy(q[0], negm[:]))
                link(v.tensor_tensor(mres[:], negm[:], q[0], ALU.subtract))
                link(v.tensor_copy(q[1], mres[:]))
                link(v.tensor_tensor(mres[:], mres[:], q[1], ALU.subtract))
                v.tensor_copy(q[2], mres[:]).then_inc(maxed1, 1)

            def qk2_evacuate(b):
                for i, name in enumerate(("q2", "k2")):
                    u = A_USE[name]
                    A.wait_filled(dve, b, u)
                    v.tensor_scalar(q2T[:, i, :], psA[:, u % 2, 0:T], b2s[:, i:i + 1], None, ALU.add).then_inc(A.emptied[u % 2], 1)

            def energy_max(b):
                u = A_USE["energy"]
                A.wait_filled(dve, b, u)
                v.tensor_reduce(mx2[:], psA[:, u % 2, :].rearrange("p (n m) -> p n m", n=TT), AX.X, ALU.max, negate=True)\
                    .then_inc(att2_max, 1)

            def att2_normalise(b):
                A.wait_emptied(dve, b, A_USE["energy"])
                link(v.reciprocal(sm2[:], sm2[:]))
                v.tensor_tensor(att2[:], att2[:], sm2[:].unsqueeze(2).broadcast_to([P, TT, T]), ALU.mult).then_inc(att2_ready, 1)

            def evac_o(b, g):
                u = A_USE["pv", g]
                A.wait_filled(dve, b, u)
                if g >= 2:
                    A.wait_filled(dve, b, A_USE["turn_o", g - 2])
                v.tensor_copy(OT[:, g % 2, :], psA[:, u % 2, :]).then_inc(A.emptied[u % 2], 1)

            def normalise1(b, g):
                u = A_USE["turn_o", g]
                A.wait_filled(dve, b, u)
                o = psA[:, u % 2, :].rearrange("p (j a c) -> p j a c", j=4, a=4)
                i = g % 2
                link(v.reciprocal(rs1[:, i], o[:, :, :, HD1]))
                link(v.tensor_tensor(rs1[:, i], rs1[:, i], fac[:].rearrange("p s a -> p (s a)").unsqueeze(1).broadcast_to([P, 4, 4]),
                                     ALU.mult))
                v.tensor_tensor(on1[:, i], o[:, :, :, 0:HD1], rs1[:, i].unsqueeze(3).broadcast_to([P, 4, 4, HD1]),
                                ALU.mult).then_inc(A.emptied[u % 2], 1)
                A.wait_emptied(dve, b, u)
                s1 = on1[:, i].rearrange("p (j t) (s a) d -> p s j t (a d)", t=TT, s=2)
                for t in range(TT):
                    last = v.tensor_tensor(att1[:, t, g * 32:(g + 1) * 32].rearrange("p (j c) -> p j c", j=2),
                                           s1[:, 0, :, t, :], s1[:, 1, :, t, :], ALU.subtract)
                if g == G1 - 1:
                    last.then_inc(attn1, 1)

            def layer_norm(b, name, res, dst, nth):
                u = A_USE[name]
                A.wait_filled(dve, b, u)
                v.tensor_tensor(dst[:], psA[:, u % 2, :].rearrange("p (t d) -> p t d", t=TT), res[:], ALU.add)\
                    .then_inc(A.emptied[u % 2], 1)
                A.wait_emptied(dve, b, u)
                for t in range(TT):
                    ins = v.bn_stats(bst[:, t, :], dst[:, t, :])
                link(ins)
                v.memset(idle_v[:], 0.0)
                for t in range(TT):
                    ins = v.bn_aggr(mv[:, t, :], bst[:, t, :])
                link(ins)
                v.tensor_scalar(var[:], mv[:, :, 1], EPS, None, ALU.add).then_inc(var_ready, 1)
                dve.wait_ge(rstd_ready, b * 2 + nth + 1)
                for t in range(TT):
                    last = v.tensor_scalar(dst[:, t, :], dst[:, t, :], mv[:, t, 0:1], rstd[:, t:t + 1], ALU.subtract, ALU.mult)
                last.then_inc((x1_ready, x2_ready)[nth], 1)

            def front(b, step, n):
                if step == "proj":
                    rope1_products(b, 0)
                elif step == "ctx":
                    qk2_evacuate(b)
                elif step == "energy":
                    energy_max(b)
                elif step == "pack":
                    pack(b, n)
                elif step == "rope":
                    rope1_products(b, 1)
                elif step == "kt" and n == 0:
                    evac_k(b, n)
                elif step == "qt":
                    evac_q(b, S_QT, n)
                elif step == "max":
                    maxima1(b, n)
                elif step == "packmax":
                    pack_maxima(b)
                elif step == "att2":
                    att2_normalise(b)
                elif step == "qt2":
                    evac_q(b, S_QT2, n)
                elif step == "pv":
                    evac_o(b, n)
                elif step == "ot":
                    normalise1(b, n)
                elif step == "wo":
                    dve.wait_ge(ld_x, b * 16 + 16)
                    layer_norm(b, "wo1", xs, x1, 0)
                elif step == "xm":
                    dve.wait_ge(x2_read, b + 1)
                    layer_norm(b, "x_m", x1, x2, 1)

            def rms_norm(b, src, nth):
                for t in range(TT):
                    ins = v.tensor_tensor_reduce(xnb[:, t, :], src[:, t, :], src[:, t, :], 1.0, 0.0, ALU.mult, ALU.add,
                                                 sqb[:, t:t + 1])
                link(ins)
                v.tensor_scalar(varb[:], sqb[:], 1.0 / D, EPS, ALU.mult, ALU.add).then_inc(varb_ready, 1)

            def rms_scale(b, src, nth):
                dve.wait_ge(rstdb_ready, b * 2 + nth + 1)
                for t in range(TT):
                    last = v.tensor_scalar(xnb[:, t, :], src[:, t, :], rstdb[:, t:t + 1], None, ALU.mult)
                last.then_inc(xn_ready, 1)

            def turned_scaled(b, name, w, dst):
                u = k_use(b)[name]
                K.wait_filled(dve, b, u)
                for k in range(DT):
                    last = v.tensor_scalar(dst[:, k, :], psK[:, u % 2, k * T:(k + 1) * T], nws[:, w, k:k + 1], None, ALU.mult)
                last.then_inc(K.emptied[u % 2], 1)

            def rope3_products(b, c):
                u, i = k_use(b)["p3", c], c % 2
                K.wait_filled(dve, b, u)
                if c >= 2:
                    dve.wait_ge(summed3, b * 10 + c)
                dve.wait_ge(swapped3, b * 10 + c + 1)
                v.tensor_tensor(ra[:, i], psK[:, u % 2, :].rearrange("p (a t) -> p a t", a=2),
                                rope3s[:, 0, :].unsqueeze(1).broadcast_to([P, 2, T]), ALU.mult).then_inc(K.emptied[u % 2], 1)

            def maxima3(b, c):
                if is_last(b):
                    S.wait_filled(dve, B, c)
                    banks = psS[:, c % 2, :].rearrange("p (a k) -> p a k", a=2)
                else:
                    for a in range(2):
                        K.wait_filled(dve, b, k_use(b)["s3", 2 * c + a])
                    banks = psK
                v.tensor_reduce(mx3[:, c % 2, 0:2], banks[:, :, 0:P], AX.X, ALU.max, negate=True)
                v.tensor_reduce(mx3[:, c % 2, 2:4], banks[:, :, P:384], AX.X, ALU.max, negate=True).then_inc(max3, 1)

            def evac_o3(b, c):
                u = k_use(b)["pv3", c]
                K.wait_filled(dve, b, u)
                v.tensor_copy(O3[:, 2 * c:2 * c + 2, :], psK[:, u % 2, :].rearrange("p (a t) -> p a t", a=2)).then_inc(K.emptied[u % 2], 1)

            def low_n2(n):
                dve.wait_ge(n2_high, n + 1)
                cols = (slice(0, NTOK - T), slice(NTOK - T, NTOK))[n]
                v.tensor_tensor(n2l[:, :, cols], n2T[:, :, cols], n2h[:, :, cols].bitcast(F32), ALU.subtract).then_inc(n2_split, 1)

            def read_logits(n):
                dve.wait_ge(lg_filled, n + 1)
                t0, t1 = ((0, NT - TT), (NT - TT, NT))[n]
                v.tensor_copy(lg[:, t0:t1, :].rearrange("p t e -> p (t e)"), psA[:, n, t0 * E:t1 * E]).then_inc(lg_read, 1)

            def back(b, step, n, final=None):
                if step == "n1":
                    dve.wait_ge(x2_ready, b + 1)
                    rms_norm(b, x2, 0)
                elif step == "n1 scale":
                    rms_scale(b, x2, 0)
                elif step == "t1":
                    dve.wait_ge(spilled, b * 32 + 1)
                    v.tensor_copy(x2b[:], x2[:]).then_inc(x2_read, 1)
                    turned_scaled(b, "turn_n1", 0, nT)
                elif step == "p3":
                    rope3_products(b, n)
                elif step == "s3":
                    maxima3(b, n)
                elif step == "pv3":
                    evac_o3(b, n)
                elif step == "early":
                    read_logits(0)
                    low_n2(0)
                elif step == "wo3" and n % 2:
                    if n == 1:
                        dve.wait_ge(x2_read, b + 2)
                    u = k_use(b)["wo3", n // 2]
                    K.wait_filled(dve, b, u)
                    v.tensor_tensor(hb[:, n // 2, :], psK[:, u % 2, 0:D], x2b[:, n // 2, :], ALU.add).then_inc(K.emptied[u % 2], 1)
                elif step == "n2":
                    for t in range(TT):
                        K.wait_emptied(dve, b, k_use(b)["wo3", t])
                    rms_norm(b, hb, 1)
                    v.tensor_tensor(x2b[:] if final is None else acc[:, final * TT:(final + 1) * TT, :], hb[:], x2b[:], ALU.add)\
                        .then_inc(acc_ready, 1)
                    rms_scale(b, hb, 1)
                elif step == "t2":
                    turned_scaled(b, "turn_n2", 1, nT if final is None else n2T[:, :, final * T:(final + 1) * T])

            def one_pass(b, order):
                for which, step, n in order:
                    if which == BACK:
                        back(b, step, n)
                    else:
                        front(b + 1 + which, step, n)

            for start in (*S.emptied, *A.emptied, *K.emptied, *U_read, *hid_ready, *h_ready, *Y_added, summed3, x2_read, spilled):
                dve.sem_inc(start, 1)
            v.memset(qpack[:], 0.0)
            v.memset(kpack[:], 0.0)
            link(v.memset(Vx[:], 0.0))
            v.memset(kpack[:, :, :, 48:51], 1.0)
            link(v.memset(Vx[:, :, :, HD1:HD1 + 1], 1.0))

            def lambda_dots():
                dve.wait_ge(ld_small, 32)
                link(v.tensor_tensor(lamp[:], lams[:, 0:4:2, :], lams[:, 1:4:2, :], ALU.mult))
                v.tensor_reduce(lamd[:], lamp[:], AX.X, ALU.add).then_inc(lam_dots, 1)

            def lambda_factors():
                dve.wait_ge(lam_exp, 1)
                link(v.tensor_tensor(lamd[:, 0:1], lame[:, 0:1], lame[:, 1:2], ALU.subtract))
                v.memset(fac[:, 0, :], 1.0 - LAMBDA_INIT)
                for a in range(2):
                    ins = v.tensor_scalar(fac[:, 1, a:a + 1], lamd[:, 0:1], LAMBDA_INIT, 1.0 - LAMBDA_INIT, ALU.add, ALU.mult)
                link(ins)

            dve.wait_ge(ld_rope1, 16)
            for which, step, n in [(0, *x[1:]) for x in ORDER if x[0] == HEAD] + [x for x in ORDER if x[0] != BACK]:
                if step == "kt" and n == which == 0:
                    dve.wait_ge(zeros_made, 1)
                elif step == "ctx":
                    dve.wait_ge(ld_w2, 48)
                    lambda_dots()
                elif step == "att2":
                    lambda_factors()
                front(which, step, n)
            first = n_[0]
            dve.wait_ge(ld_w3v, 32)
            for whole in (True, False):
                n_[0] = 0
                if whole:
                    with dve.Fori(0, B - 2) as b:
                        base[0] = b * VEC_STEPS + first
                        one_pass(b, ORDER)
                else:
                    base[0] = (B - 2) * VEC_STEPS + first
                    one_pass(B - 2, headless_order())
                assert n_[0] == VEC_STEPS, n_[0]
            base[0] = (B - 1) * VEC_STEPS + first
            n_[0] = 0
            for _, step, n in LAST_ORDER:
                back(B - 1, step, n, final=B - 1)

            low_n2(1)
            read_logits(1)
            dve.wait_ge(lg_read, 2)
            for t in range(NT):
                ins = v.max(top[:, t, :], lg[:, t, :])
            link(ins)
            v.tensor_tensor(pr[:, 0, :], top[:, :, 1], top[:, :, 0], ALU.subtract).then_inc(top_diff, 1)
            for t in range(NT):
                ins = v.max_index(tix[:, t, :], top[:, t, :], lg[:, t, :])
            link(ins)
            link(v.tensor_copy(tixf[:], tix[:]))
            dve.wait_ge(top_exp, 1)
            link(v.tensor_scalar(pr[:, 2, :], pr[:, 1, :], 1.0, None, ALU.add))
            link(v.reciprocal(pr[:, 2, :], pr[:, 2, :]))
            link(v.tensor_tensor(pr[:, 3, :], pr[:, 1, :], pr[:, 2, :], ALU.mult))
            it = iota8[:].unsqueeze(1).broadcast_to([P, NT, E])
            for j, w in ((0, wgt), (1, wgt2)):
                link(v.tensor_tensor(w[:], it, tixf[:, :, j].unsqueeze(2).broadcast_to([P, NT, E]), ALU.is_equal))
                link(v.tensor_tensor(w[:], w[:], pr[:, 2 + j, :].unsqueeze(2).broadcast_to([P, NT, E]), ALU.mult))
            link(v.tensor_tensor(wgt[:], wgt[:], wgt2[:], ALU.add))
            dve.wait_ge(ld_acc, 16 * (B - 1))

            def low_part(ep, i, f, c):
                dve.wait_ge(hid_high[c], ep * 8 + 4 * i + f + 1)
                o = hTh[:, f, c * 512:(c + 1) * 512]
                v.tensor_tensor(hTl[:, f, c * 512:(c + 1) * 512], hid[:, c, :], o.bitcast(F32), ALU.subtract).then_inc(h_ready[c], 1)

            with dve.Fori(0, E // 2) as ep:
                for i in range(2):
                    for n in range(2 * FT):
                        f, c = n // 2, n % 2
                        dve.wait_ge(U_read[c], ep * 8 + 4 * i + f + 2)
                        dve.wait_ge(W_filled[c], ep * 8 + 4 * i + f + 1)
                        dve.wait_ge(h_ready[c], ep * 8 + 4 * i + f + 1)
                        v.tensor_tensor(hid[:, c, :], sil[:, c, :], psS[:, c, 512:1024], ALU.mult).then_inc(hid_ready[c], 1)
                        low_part(ep, i, f, c)
                    for t in range(NT):
                        dve.wait_ge(Y_filled[t % 2], ep * 8 + 4 * i + t // 2 + 1)
                        v.scalar_tensor_tensor(out=acc[:, t, :], in0=psA[:, t % 2, 0:D],
                                               scalar=wgt[:, t, bass.ds(ep * 2 + i, 1)],
                                               in1=acc[:, t, :], op0=ALU.mult, op1=ALU.add).then_inc(Y_added[t % 2], 1)
            dve.wait_ge(Y_added[0], E * 4 + 1)
            dve.wait_ge(Y_added[1], E * 4 + 1)
            halves = [range(NT // 2), range(NT // 2, NT)]
            for half in halves:
                for t in half:
                    ins = v.bn_stats(bstF[:, t, :], acc[:, t, :])
                link(ins)
                for t in half:
                    ins = v.bn_aggr(mvF[:, t, :], bstF[:, t, :])
                link(ins)
                v.tensor_scalar(varF[:, half.start:half.stop], mvF[:, half.start:half.stop, 1], EPS, None, ALU.add).then_inc(fin_var, 1)
            for n, half in enumerate(halves):
                dve.wait_ge(fin_rstd, n + 1)
                for t in half:
                    v.tensor_scalar(acc[:, t, :], acc[:, t, :], mvF[:, t, 0:1], rstdF[:, t:t + 1],
                                    ALU.subtract, ALU.mult).then_inc(fin_ready, 1)

        @block.scalar
        def _(act):
            a_ = nc.scalar

            def exp2(b):
                u = A_USE["energy"]
                act.wait_ge(att2_max, b + 1)
                for n in range(TT):
                    ins = a_.activation(att2[:, n, :], psA[:, u % 2, n * T:(n + 1) * T], ACT.Exp, bias=mx2[:, n:n + 1],
                                        accum_out=sm2[:, n:n + 1])
                ins.then_inc(A.emptied[u % 2], 1)

            def high_parts(b, t):
                act.wait_ge(summed1, b * TT + t + 1)
                a_.copy(hib[:, t, :], rt1[:, t, :]).then_inc(high1, 1)
                act.wait_ge(rest1, b * TT + t + 1)
                a_.copy(midb[:, t, :], rt1[:, t, :]).then_inc(mid1, 1)

            def exp1(b, g, uses):
                for c in uses:
                    u = S_EXP + 3 * g + c
                    before = (3 * g + c - PTN) // 3
                    if before >= 0:
                        A.wait_filled(act, b, A_USE["pv", before])
                    S.wait_filled(act, b, u)
                    a_.activation(PT[:, (3 * g + c) % PTN, :], psS[:, u % 2, :], ACT.Exp, scale=HD1 ** -0.5).then_inc(S.emptied[u % 2], 1)

            def evac4(b, name, dst):
                u = A_USE[name]
                A.wait_filled(act, b, u)
                a_.copy(dst[:].rearrange("p k t -> p (k t)"), psA[:, u % 2, :]).then_inc(A.emptied[u % 2], 1)

            def evac_k(b, t):
                u = S_KT + t
                S.wait_filled(act, b, u)
                src = psT[:, u % 2, :].rearrange("p (j q) -> p j q", q=P)
                a_.copy(KT[0:64, :, 0, t * P:(t + 1) * P], src[0:64])
                a_.copy(KT[64:128, :, 1, t * P:(t + 1) * P], src[64:128]).then_inc(S.emptied[u % 2], 1)

            def evac_q(b, u0, t):
                s = 0 if u0 == S_QT else 1
                u = u0 + 2 * t + s
                S.wait_filled(act, b, u)
                a_.copy(QT[:, 16 * s:16 * s + 16, t * P:(t + 1) * P],
                        psT[:, u % 2, :].rearrange("p (j q) -> p j q", q=P)).then_inc(S.emptied[u % 2], 1)

            def front(b, step, n):
                if step == "exp2":
                    exp2(b)
                elif step == "split":
                    high_parts(b, n)
                elif step == "sTa":
                    exp1(b, n, (0, 1))
                elif step == "sTb":
                    exp1(b, n, (2,))
                elif step == "kt" and n == 1:
                    evac_k(b, n)
                elif step == "qt":
                    evac_q(b, S_QT, n)
                elif step == "qt2":
                    evac_q(b, S_QT2, n)
                elif step == "at":
                    evac4(b, "turn_att1", tT)
                elif step == "a2t":
                    evac4(b, "turn_att2", q2T)
                elif step == "x1t":
                    evac4(b, "turn_x1", tT)

            def evac_v3(b, t):
                u = k_use(b)["v3", t]
                K.wait_filled(act, b, u)
                a_.copy(V3[:, t, :], psK[:, u % 2, :]).then_inc(K.emptied[u % 2], 1)

            def swap3(b, c):
                u, i = k_use(b)["p3", c], c % 2
                K.wait_filled(act, b, u)
                if c >= 2:
                    act.wait_ge(summed3, b * 10 + c)
                q = psK[:, u % 2, :].rearrange("p (a t) -> p a t", a=2)
                a_.copy(rb[0:64, i], q[64:128])
                a_.copy(rb[64:128, i], q[0:64]).then_inc(swapped3, 1)

            def exp3(b, c):
                i = c % 2
                act.wait_ge(max3, b * 8 + c + 1)
                if c >= 2:
                    K.wait_filled(act, b, k_use(b)["turn_p", 2 * c - 3])
                for a in range(2):
                    if is_last(b):
                        bank, scores = a, psS[:, c % 2, a * 512:a * 512 + 384]
                    else:
                        bank = k_use(b)["s3", 2 * c + a] % 2
                        scores = psK[:, bank, 0:384]
                    for t, (lo, hi) in enumerate(((0, P), (P, 384))):
                        ins = a_.activation(P3[:, i, a, lo:hi], scores[:, lo:hi], ACT.Exp,
                                            bias=mx3[:, i, 2 * t + bank:2 * t + bank + 1],
                                            accum_out=sm3[:, i, 2 * t + a:2 * t + a + 1])
                    if not is_last(b):
                        ins.then_inc(K.emptied[bank], 1)
                if is_last(b):
                    ins.then_inc(S.emptied[c % 2], 1)

            def evac_p(b, h):
                u = k_use(b)["turn_p", h]
                K.wait_filled(act, b, u)
                if h >= 2:
                    K.wait_filled(act, b, k_use(b)["pv3", h // 2 - 1])
                a_.copy(PT3[:, h % 2, :], psK[:, u % 2, 0:384]).then_inc(K.emptied[u % 2], 1)

            def back(b, step, n):
                if step == "v3":
                    evac_v3(b, n)
                elif step == "early":
                    act.wait_ge(ld_n2T, 16 * (B - 1))
                    a_.copy(n2h[:, :, 0:NTOK - T], n2T[:, :, 0:NTOK - T]).then_inc(n2_high, 1)
                elif step == "p3":
                    swap3(b, n)
                elif step == "e3":
                    exp3(b, n)
                elif step == "pt3":
                    evac_p(b, 2 * n)
                    evac_p(b, 2 * n + 1)

            def one_pass(b, order):
                for which, step, n in order:
                    if which == BACK:
                        back(b, step, n)
                    else:
                        front(b + 1 + which, step, n)

            act.dma_start(wqkv1[:, 1, :], w1qkv[P:D, :]).then_inc(ld_w1, 16)
            act.wait_ge(consts_made, 1)
            for which, step, n in [(0, *x[1:]) for x in ORDER if x[0] == HEAD] + [x for x in ORDER if x[0] != BACK]:
                if step == "energy":
                    act.wait_ge(lam_dots, 1)
                    a_.activation(lame[:], lamd[:], ACT.Exp).then_inc(lam_exp, 1)
                front(which, step, n)
            with act.Fori(0, B - 2) as b:
                one_pass(b, ORDER)
            one_pass(B - 2, headless_order())
            one_pass(B - 1, LAST_ORDER)

            def high_weights(ep, i):
                act.wait_ge(ld_e[i], ep * 48 + 48)
                a_.copy(eh[:, i, :], ew[:, i, :]).then_inc(w_high, 1)

            K.wait_filled(act, B - 1, k_use(B - 1)["wo3", TT - 1])
            high_weights(0, 0)
            K.wait_emptied(act, B - 1, k_use(B - 1)["turn_n2"])
            a_.copy(n2h[:, :, NTOK - T:NTOK], n2T[:, :, NTOK - T:NTOK]).then_inc(n2_high, 1)
            act.wait_ge(top_diff, 1)
            a_.activation(pr[:, 1, :], pr[:, 0, :], ACT.Exp).then_inc(top_exp, 1)

            def high_part(ep, i, f, c):
                act.wait_ge(hid_ready[c], ep * 8 + 4 * i + f + 2)
                a_.copy(hTh[:, f, c * 512:(c + 1) * 512], hid[:, c, :]).then_inc(hid_high[c], 1)

            def expert(ep, i, more):
                for n in range(2 * FT):
                    f, c = n // 2, n % 2
                    act.wait_ge(U_filled[c], ep * 8 + 4 * i + f + 1)
                    act.wait_ge(hid_ready[c], ep * 8 + 4 * i + f + 1)
                    a_.activation(sil[:, c, :], psS[:, c, 0:512], ACT.Silu).then_inc(U_read[c], 1)
                    high_part(ep, i, f, c)
                if more:
                    high_weights(ep + i, 1 - i)

            with act.Fori(0, E // 2 - 1) as ep:
                for i in range(2):
                    expert(ep, i, True)
            for i in range(2):
                expert(E // 2 - 1, i, i == 0)

        @block.gpsimd
        def _(pool):
            p_ = nc.gpsimd
            p_.memset(ident[:], 0.0)
            p_.memset(maskb[:], 0.0)
            p_.memset(maskTb[:], 0.0)
            p_.memset(neghalf[:], -0.5)
            p_.memset(neg1[:], -1.0)
            p_.memset(nhF[:], -0.5).then_inc(pool_step, 1)
            pool.wait_ge(pool_step, 1)
            p_.affine_select(out=ident[:], in_=ident[:], compare_op=ALU.not_equal, fill=1.0, base=0,
                             pattern=[[-1, P]], channel_multiplier=1).then_inc(pool_step, 1)
            p_.affine_select(out=maskb[:], in_=maskb[:], compare_op=ALU.is_ge, fill=NEG, base=0,
                             pattern=[[-1, P]], channel_multiplier=1)
            p_.affine_select(out=maskTb[:], in_=maskTb[:], compare_op=ALU.is_ge, fill=NEG, base=0,
                             pattern=[[1, P]], channel_multiplier=-1)
            p_.iota(iota8[:], [[1, E]], base=0, channel_multiplier=0, allow_small_or_imprecise_dtypes=True)
            pool.wait_ge(pool_step, 2)
            p_.tensor_copy(identb[:], ident[:]).then_inc(consts_made, 1)
            p_.memset(KT[:], 0.0).then_inc(zeros_made, 1)

            def split1(b, t):
                pool.wait_ge(roped1, b * TT + t + 1)
                p_.tensor_tensor(rt1[:, t, :], rt1[:, t, :], rt2[:, t, :], ALU.add).then_inc(summed1, 1)
                pool.wait_ge(high1, b * TT + t + 1)
                p_.tensor_tensor(rt1[:, t, :], rt1[:, t, :], hib[:, t, :], ALU.subtract).then_inc(rest1, 1)
                pool.wait_ge(mid1, b * TT + t + 1)
                p_.tensor_tensor(lob[:, t, :], rt1[:, t, :], midb[:, t, :], ALU.subtract).then_inc(low1, 1)

            def front(b, step, n):
                if step == "split":
                    split1(b, n)
                elif step in ("wo", "xm"):
                    pool.wait_ge(var_ready, b * 2 + (step == "xm") + 1)
                    p_.tensor_tensor(rstd[:], var[:], neghalf[:], ALU.pow).then_inc(rstd_ready, 1)

            def back(b, step, n):
                if step in ("n1", "n2"):
                    pool.wait_ge(varb_ready, b * 2 + (step == "n2") + 1)
                    p_.tensor_tensor(rstdb[:], varb[:], neghalf[:], ALU.pow).then_inc(rstdb_ready, 1)
                elif step == "p3":
                    i = n % 2
                    pool.wait_ge(swapped3, b * 10 + n + 1)
                    p_.tensor_tensor(rb[:, i], rb[:, i], rope3s[:, 1, :].unsqueeze(1).broadcast_to([P, 2, T]), ALU.mult)\
                        .then_inc(sined3, 1)
                    K.wait_emptied(pool, b, k_use(b)["p3", n])
                    pool.wait_ge(sined3, b * 10 + n + 1)
                    p_.tensor_tensor(QK3[:, 2 * n:2 * n + 2, :], ra[:, i], rb[:, i], ALU.add).then_inc(summed3, 1)
                elif step == "e3":
                    i = n % 2
                    if is_last(b):
                        S.wait_emptied(pool, B, n)
                    else:
                        for a in range(2):
                            K.wait_emptied(pool, b, k_use(b)["s3", 2 * n + a])
                    p_.tensor_tensor(rc3[:, i, :], sm3[:, i, :], neg1[:], ALU.pow).then_inc(rec3, 1)
                    pool.wait_ge(rec3, b * 8 + n + 1)
                    p_.tensor_tensor(P3[:, i, :, 0:P], P3[:, i, :, 0:P], rc3[:, i, 0:2].unsqueeze(2).broadcast_to([P, 2, P]), ALU.mult)
                    p_.tensor_tensor(P3[:, i, :, P:384], P3[:, i, :, P:384], rc3[:, i, 2:4].unsqueeze(2).broadcast_to([P, 2, T]),
                                     ALU.mult).then_inc(norm3, 1)

            def one_pass(b, order):
                for which, step, n in order:
                    if which == BACK:
                        back(b, step, n)
                    else:
                        front(b + 1 + which, step, n)

            for which, step, n in [(0, *x[1:]) for x in ORDER if x[0] == HEAD] + [x for x in ORDER if x[0] != BACK]:
                front(which, step, n)
            with pool.Fori(0, B - 2) as b:
                one_pass(b, ORDER)
            one_pass(B - 2, headless_order())
            one_pass(B - 1, LAST_ORDER)
            def low_weights(e, i):
                pool.wait_ge(w_high, e + 1)
                p_.tensor_tensor(el[:, i, :], ew[:, i, :], eh[:, i, :].bitcast(F32), ALU.subtract).then_inc(w_split, 1)

            with pool.Fori(0, E // 2) as ep:
                for i in range(2):
                    low_weights(ep * 2 + i, i)
            for n in range(2):
                half = slice(n * NT // 2, (n + 1) * NT // 2)
                pool.wait_ge(fin_var, n + 1)
                p_.tensor_tensor(rstdF[:, half], varF[:, half], nhF[:, half], ALU.pow).then_inc(fin_rstd, 1)


def kernel(**inputs):
    import numpy as _np
    import concourse.bacc as _bacc
    from concourse import mybir as _mybir
    from concourse.bass_utils import run_bass_kernel_spmd as _run

    i = {k: _np.asarray(v) for k, v in inputs.items()}
    f32 = _np.float32

    def angles(n, width, theta):
        inv = (1.0 / theta ** (_np.arange(0, width, 2, dtype=f32) / f32(width))).astype(f32)
        return _np.arange(n, dtype=f32)[:, None] * inv[None, :]

    a1 = angles(T, HD1, 10000.0)
    s1 = _np.sin(a1)
    rope1 = _np.stack([_np.tile(_np.cos(a1), (1, 2)), _np.concatenate([-s1, s1], 1)], 1).astype(f32)
    a3 = angles(T, HD3, 1000000.0).T
    s3 = _np.sin(a3)
    rope3 = (_np.stack([_np.tile(_np.cos(a3), (2, 1)), _np.concatenate([-s3, s3], 0)], 1) * HD3 ** -0.25).astype(f32)

    feed = {
        "x": i["x"],
        "xT": i["x"].transpose(0, 2, 1),
        "ctxT": i["ctx_1024"].transpose(0, 2, 1),
        "w1qkv": _np.concatenate([i["L0_attn_wq"].T, i["L0_attn_wk"].T, i["L0_attn_wv"].T], 1),
        "w1o": i["L0_attn_wo"].T,
        "lam": _np.stack([i["L0_attn_lambda_q1"], i["L0_attn_lambda_k1"], i["L0_attn_lambda_q2"], i["L0_attn_lambda_k2"]]),
        "w2q": i["L0_xattn_Wq"].T,
        "w2k": i["L0_xattn_Wk"].T,
        "b2": _np.stack([i["L0_xattn_bq"], i["L0_xattn_bk"]], 1),
        "nw": _np.stack([i["L0_ffn_norm1_w"].reshape(DT, P).T, i["L0_ffn_norm2_w"].reshape(DT, P).T], 1),
        "w3q": i["L0_ffn_wq"], "w3k": i["L0_ffn_wk"], "w3v": i["L0_ffn_wv"], "w3o": i["L0_ffn_wo"],
        "gate": i["L0_ffn_gate_w"],
        "e1": i["L0_ffn_w1"], "e3": i["L0_ffn_w3"], "e2": i["L0_ffn_w2"],
        "rope1": rope1, "rope3": rope3,
    }
    nc = _bacc.Bacc("TRN2", target_bir_lowering=False, num_devices=1)
    arrays, args = {}, []
    for name, a in feed.items():
        a = _np.ascontiguousarray(a)
        arrays[f"in_{name}"] = a
        args.append(nc.dram_tensor(f"in_{name}", a.shape, _mybir.dt.from_np(a.dtype), kind="ExternalInput").ap())
    args.append(nc.dram_tensor("out_0", (B, T, D), _mybir.dt.float32, kind="ExternalOutput").ap())
    decoder_kernel(nc, *args)
    r = _run(nc, [arrays], core_ids=[0])
    return r.results[0]["out_0"]
```
